# Optimizing a Trainium2 kernel written in Bass

```python
import numpy as np
import jax
import jax.numpy as jnp

def _softmax(x, axis=-1):
    return jax.nn.softmax(x, axis=axis)
def _gelu(x):
    return jax.nn.gelu(x, approximate=True)
def _silu(x):
    return jax.nn.silu(x)
def _sigmoid(x):
    return jax.nn.sigmoid(x)
def _layernorm(x, axis=-1, eps=1e-5):
    m = jnp.mean(x, axis=axis, keepdims=True)
    v = jnp.var(x, axis=axis, keepdims=True)
    return (x - m) / jnp.sqrt(v + eps)
def _scatter_add(tgt, idx, src, axis=0):
    return tgt.at[idx].add(src)
def _segment_sum(src, seg, n):
    return jax.ops.segment_sum(src, seg, n)

kernel_name = 'mk_conv_attn_hybrid_d4_conv_nhwc128_183bdb'

def setup_inputs(seed: int = 0):
    np.random.seed(seed)
    _w = jnp.asarray
    def _rec_inputs():
        import jax
        import jax.numpy as jnp
        _gk = jax.random.key(seed)
        x = -0.000929 + 1 * jax.random.normal(jax.random.fold_in(_gk, 1), (2, 64, 64, 128), jnp.float32)
        return x
    x = _rec_inputs()
    def _L0_conv_setup():
        import jax, jax.numpy as jnp
        import numpy as np
        NUM_HEADS = 4
        KEY_DIMS = 32

        def rel_to_abs(x):
            b, n, w, _ = x.shape
            x = jnp.pad(x, ((0, 0), (0, 0), (0, 0), (0, 1)))
            x = x.reshape(b, n, w * 2 * w)
            x = jnp.pad(x, ((0, 0), (0, 0), (0, w - 1)))
            x = x.reshape(b, n, w + 1, 2 * w - 1)
            return x[:, :, :w, w - 1:]

        def rel_logits_1d(q, rel_k):
            b, nh, xx, yy, d = q.shape
            rl = jnp.einsum('bhxyd,md->bhxym', q, rel_k)
            rl = rel_to_abs(rl.reshape(b, nh * xx, yy, 2 * yy - 1))
            rl = rl.reshape(b, nh, xx, 1, yy, yy)
            return jnp.broadcast_to(rl, (b, nh, xx, xx, yy, yy))

        def relative_position_bias(pos_q, pos_emb_h, pos_emb_w):
            rw = rel_logits_1d(pos_q, pos_emb_w)
            rw = rw.transpose(0, 1, 2, 4, 3, 5)
            rh = rel_logits_1d(pos_q.transpose(0, 1, 3, 2, 4), pos_emb_h)
            rh = rh.transpose(0, 1, 4, 2, 5, 3)
            return rw + rh
        key = jax.random.key(seed)
        k1, k2, k3, k4 = jax.random.split(key, 4)
        B, H, W, C = (2, 64, 64, 128)
        qk_dims = NUM_HEADS * KEY_DIMS
        out_channels = C
        x = jax.random.normal(k1, (B, H, W, C), dtype=jnp.float32)
        w_qkv = jax.random.normal(k2, (C, 2 * qk_dims + out_channels), dtype=jnp.float32) * 0.05
        pos_emb_h = jax.random.normal(k3, (2 * H - 1, KEY_DIMS), dtype=jnp.float32) * 0.05
        pos_emb_w = jax.random.normal(k4, (2 * W - 1, KEY_DIMS), dtype=jnp.float32) * 0.05
        return {'x': x, 'w_qkv': w_qkv, 'pos_emb_h': pos_emb_h, 'pos_emb_w': pos_emb_w}
    _L0_conv_all = _L0_conv_setup()
    _L0_conv_in = {k: v for k, v in _L0_conv_all.items() if k in ('w_qkv', 'pos_emb_h', 'pos_emb_w', )}
    del _L0_conv_all

    def _L1_conv_setup():
        import jax, jax.numpy as jnp
        import numpy as np
        B, H, W = (4, 64, 64)
        D_MODEL, D_STATE, D_CONV, EXPAND = (128, 16, 3, 2)
        D_INNER = EXPAND * D_MODEL
        DT_RANK = D_MODEL // 16
        LN_EPS = 1e-05

        def _selective_scan(u, delta, A, Bm, Cm, Dp, delta_bias):
            delta = jax.nn.softplus(delta + delta_bias[None, :, None])
            u_t = jnp.moveaxis(u, 2, 0)
            d_t = jnp.moveaxis(delta, 2, 0)
            B_t = jnp.moveaxis(Bm, 2, 0)
            C_t = jnp.moveaxis(Cm, 2, 0)

            def step(h, inp):
                u_i, d_i, b_i, c_i = inp
                dA = jnp.exp(d_i[..., None] * A)
                h = h * dA + (d_i * u_i)[..., None] * b_i[:, None, :]
                y = jnp.einsum('gdn,gn->gd', h, c_i)
                return (h, y)
            h0 = jnp.zeros((u.shape[0], u.shape[1], A.shape[1]), u.dtype)
            _, ys = jax.lax.scan(step, h0, (u_t, d_t, B_t, C_t))
            return jnp.moveaxis(ys, 0, 2) + u * Dp[None, :, None]

        def _forward(x, w_in, conv_w, conv_b, w_xproj, w_dt, b_dt, A_log, D_param, ln_w, ln_b, w_out):
            b, h, w, _ = x.shape
            L = h * w
            xz = x @ w_in
            xc, z = jnp.split(xz, 2, axis=-1)
            pad = (D_CONV - 1) // 2
            xc = jax.lax.conv_general_dilated(xc, conv_w, window_strides=(1, 1), padding=[(pad, pad), (pad, pad)], feature_group_count=D_INNER, dimension_numbers=('NHWC', 'HWIO', 'NHWC')) + conv_b
            xa = jax.nn.silu(xc)
            x_flat = xa.reshape(b, L, D_INNER)
            x_dbl = x_flat @ w_xproj
            dts, Bp, Cp = jnp.split(x_dbl, [DT_RANK, DT_RANK + D_STATE], axis=-1)
            dts = dts @ w_dt
            x_t = jnp.transpose(xa, (0, 2, 1, 3)).reshape(b, L, D_INNER)
            xs = jnp.stack([x_flat, x_t, jnp.flip(x_flat, 1), jnp.flip(x_t, 1)], axis=1)
            xs = xs.reshape(b * 4, L, D_INNER).transpose(0, 2, 1)

            def rep4(t):
                return jnp.broadcast_to(t[:, None], (b, 4) + t.shape[1:]).reshape((b * 4,) + t.shape[1:]).transpose(0, 2, 1)
            dts4, Bp4, Cp4 = (rep4(dts), rep4(Bp), rep4(Cp))
            A = -jnp.exp(A_log.astype(jnp.float32))
            ys = _selective_scan(xs, dts4, A, Bp4, Cp4, D_param.astype(jnp.float32), b_dt.astype(jnp.float32))
            ys = ys.transpose(0, 2, 1).reshape(b, 4, L, D_INNER)
            y = ys[:, 0].reshape(b, h, w, D_INNER) + jnp.transpose(ys[:, 1].reshape(b, w, h, D_INNER), (0, 2, 1, 3)) + jnp.flip(ys[:, 2], 1).reshape(b, h, w, D_INNER) + jnp.transpose(jnp.flip(ys[:, 3], 1).reshape(b, w, h, D_INNER), (0, 2, 1, 3))
            mu = jnp.mean(y, axis=-1, keepdims=True)
            var = jnp.mean(jnp.square(y - mu), axis=-1, keepdims=True)
            y = (y - mu) * jax.lax.rsqrt(var + LN_EPS) * ln_w + ln_b
            y = y * jax.nn.silu(z)
            return y @ w_out
        key = jax.random.key(seed)
        ks = jax.random.split(key, 9)
        s = 0.02
        x = jax.random.normal(ks[0], (B, H, W, D_MODEL), dtype=jnp.float32)
        w_in = jax.random.normal(ks[1], (D_MODEL, 2 * D_INNER), dtype=jnp.float32) * s
        conv_w = jax.random.normal(ks[2], (D_CONV, D_CONV, 1, D_INNER), dtype=jnp.float32) * s
        conv_b = jax.random.normal(ks[3], (D_INNER,), dtype=jnp.float32) * s
        w_xproj = jax.random.normal(ks[4], (D_INNER, DT_RANK + 2 * D_STATE), dtype=jnp.float32) * s
        w_dt = jax.random.normal(ks[5], (DT_RANK, D_INNER), dtype=jnp.float32) * s
        b_dt = jax.random.normal(ks[6], (D_INNER,), dtype=jnp.float32) * s
        A_log = jnp.log(jnp.broadcast_to(jnp.arange(1, D_STATE + 1, dtype=jnp.float32), (D_INNER, D_STATE)))
        D_param = jnp.ones((D_INNER,), dtype=jnp.float32)
        ln_w = jnp.ones((D_INNER,), dtype=jnp.float32)
        ln_b = jnp.zeros((D_INNER,), dtype=jnp.float32)
        w_out = jax.random.normal(ks[7], (D_INNER, D_MODEL), dtype=jnp.float32) * s
        return {'x': x, 'w_in': w_in, 'conv_w': conv_w, 'conv_b': conv_b, 'w_xproj': w_xproj, 'w_dt': w_dt, 'b_dt': b_dt, 'A_log': A_log, 'D_param': D_param, 'ln_w': ln_w, 'ln_b': ln_b, 'w_out': w_out}
    _L1_conv_all = _L1_conv_setup()
    _L1_conv_in = {k: v for k, v in _L1_conv_all.items() if k in ('w_in', 'conv_w', 'conv_b', 'w_xproj', 'w_dt', 'b_dt', 'A_log', 'D_param', 'ln_w', 'ln_b', 'w_out', )}
    del _L1_conv_all

    def _L2_attn_setup():
        import jax, jax.numpy as jnp
        import numpy as np
        EMB = 128
        B, N = (8, 4096)
        key = jax.random.key(seed)
        k_x, k_q, k_k, k_v = jax.random.split(key, 4)
        return {'x': jax.random.normal(k_x, (B, N, EMB), dtype=jnp.float32), 'w_query': jax.random.uniform(k_q, (EMB, EMB), dtype=jnp.float32), 'w_key': jax.random.uniform(k_k, (EMB, EMB), dtype=jnp.float32), 'w_value': jax.random.uniform(k_v, (EMB, EMB), dtype=jnp.float32)}
    _L2_attn_all = _L2_attn_setup()
    _L2_attn_in = {k: v for k, v in _L2_attn_all.items() if k in ('w_query', 'w_key', 'w_value', )}
    del _L2_attn_all

    def _L2_ffn_setup():
        import jax, jax.numpy as jnp
        import numpy as np
        PADDED_SL = 8192
        TEMPERATURE = 1.0
        SIGMA_POW = 0.25

        def _stu_conv(phi, u, n):
            b, sl, d = u.shape
            sgn = jnp.where(jnp.arange(sl) % 2 == 0, 1.0, -1.0).astype(u.dtype)
            sgn3 = sgn[None, :, None]
            Vf = jnp.fft.rfft(phi, n=n, axis=0)
            Uf_p = jnp.fft.rfft(u, n=n, axis=1)
            Uf_m = jnp.fft.rfft(u * sgn3, n=n, axis=1)
            U_plus = jnp.fft.irfft(Vf[None, :, :, None] * Uf_p[:, :, None, :], n=n, axis=1)[:, :sl]
            U_minus = jnp.fft.irfft(Vf[None, :, :, None] * Uf_m[:, :, None, :], n=n, axis=1)[:, :sl]
            U_minus = U_minus * sgn[None, :, None, None]
            return (U_plus, U_minus)

        def _compute_spectral(u, sigma, phi, Mpp, Mpm):
            U_plus, U_minus = _stu_conv(phi, u, PADDED_SL)
            s = sigma ** SIGMA_POW
            out = jnp.einsum('btkd,k,kde->bte', U_plus, s, Mpp)
            out = out + jnp.einsum('btkd,k,kde->bte', U_minus, s, Mpm)
            return out

        def _compute_ar_u(Mu, u):
            sl = u.shape[1]
            out = jnp.zeros(u.shape[:2] + (Mu.shape[-1],), dtype=u.dtype)
            for i in range(Mu.shape[0]):
                ui = jnp.pad(u, ((0, 0), (i, 0), (0, 0)))[:, :sl]
                out = out + jnp.einsum('btd,de->bte', ui, Mu[i])
            return out

        def _stu(u, sigma, phi, Mu, Mpp, Mpm):
            return _compute_spectral(u, sigma, phi, Mpp, Mpm) + _compute_ar_u(Mu, u)
        key = jax.random.key(seed)
        ks = jax.random.split(key, 8)
        b, sl, d, K, k_u = (2, 4096, 128, 16, 3)
        x = jax.random.normal(ks[0], (b, sl, d), dtype=jnp.float32)
        sigma = jax.random.uniform(ks[1], (K,), dtype=jnp.float32, minval=0.001, maxval=1.0)
        phi = jax.random.normal(ks[2], (sl, K), dtype=jnp.float32) / np.sqrt(sl)
        M_u = jax.random.normal(ks[3], (4, k_u, d, d), dtype=jnp.float32) * 0.02
        M_phi_plus = jax.random.normal(ks[4], (4, K, d, d), dtype=jnp.float32) * 0.02
        M_phi_minus = jax.random.normal(ks[5], (4, K, d, d), dtype=jnp.float32) * 0.02
        log_weights = jnp.ones((4,), dtype=jnp.float32)
        u01 = jax.random.uniform(ks[6], (4,), dtype=jnp.float32, minval=1e-06, maxval=1.0 - 1e-06)
        gumbel = -jnp.log(-jnp.log(u01))
        return {'x': x, 'sigma': sigma, 'phi': phi, 'M_u': M_u, 'M_phi_plus': M_phi_plus, 'M_phi_minus': M_phi_minus, 'log_weights': log_weights, 'gumbel': gumbel}
    _L2_ffn_all = _L2_ffn_setup()
    _L2_ffn_in = {k: v for k, v in _L2_ffn_all.items() if k in ('sigma', 'phi', 'M_u', 'M_phi_plus', 'M_phi_minus', 'log_weights', 'gumbel', )}
    del _L2_ffn_all

    def _L3_attn_setup():
        import jax, jax.numpy as jnp
        import numpy as np
        B, N, D = (8, 8192, 128)
        H, KQ = (8, 64)
        key = jax.random.key(seed)
        k1, k2, k3, k4 = jax.random.split(key, 4)
        std = 0.02
        x = jax.random.normal(k1, (B, N, D), dtype=jnp.float32)
        Wk = jax.random.normal(k2, (H, KQ, D), dtype=jnp.float32) * std
        Wq = jax.random.normal(k3, (H, KQ, D), dtype=jnp.float32) * std
        Wv = jax.random.normal(k4, (H, D, D), dtype=jnp.float32) * std
        return {'x': x, 'Wk': Wk, 'Wq': Wq, 'Wv': Wv}
    _L3_attn_all = _L3_attn_setup()
    _L3_attn_in = {k: v for k, v in _L3_attn_all.items() if k in ('Wk', 'Wq', 'Wv', )}
    del _L3_attn_all

    def _L3_ffn_setup():
        import jax, jax.numpy as jnp
        import numpy as np
        B, N, D, C, E, K = (8, 8192, 128, 128, 8, 2)
        key = jax.random.key(seed)
        k0, k1, k2 = jax.random.split(key, 3)
        x = jax.random.normal(k0, (B, N, D), dtype=jnp.float32)
        router_w = jax.random.normal(k1, (D, E), dtype=jnp.float32) * 0.05
        router_b = jnp.zeros((E,), dtype=jnp.float32)
        expert_w = jax.random.normal(k2, (E, D, C), dtype=jnp.float32) * (1.0 / np.sqrt(D))
        expert_b = jnp.zeros((E, C), dtype=jnp.float32)
        return {'x': x, 'router_w': router_w, 'router_b': router_b, 'expert_w': expert_w, 'expert_b': expert_b}
    _L3_ffn_all = _L3_ffn_setup()
    _L3_ffn_in = {k: v for k, v in _L3_ffn_all.items() if k in ('router_w', 'router_b', 'expert_w', 'expert_b', )}
    del _L3_ffn_all

    return {
        "x": x,
        "L0_conv_w_qkv": _L0_conv_in["w_qkv"],
        "L0_conv_pos_emb_h": _L0_conv_in["pos_emb_h"],
        "L0_conv_pos_emb_w": _L0_conv_in["pos_emb_w"],
        "L1_conv_w_in": _L1_conv_in["w_in"],
        "L1_conv_conv_w": _L1_conv_in["conv_w"],
        "L1_conv_conv_b": _L1_conv_in["conv_b"],
        "L1_conv_w_xproj": _L1_conv_in["w_xproj"],
        "L1_conv_w_dt": _L1_conv_in["w_dt"],
        "L1_conv_b_dt": _L1_conv_in["b_dt"],
        "L1_conv_A_log": _L1_conv_in["A_log"],
        "L1_conv_D_param": _L1_conv_in["D_param"],
        "L1_conv_ln_w": _L1_conv_in["ln_w"],
        "L1_conv_ln_b": _L1_conv_in["ln_b"],
        "L1_conv_w_out": _L1_conv_in["w_out"],
        "L2_attn_w_query": _L2_attn_in["w_query"],
        "L2_attn_w_key": _L2_attn_in["w_key"],
        "L2_attn_w_value": _L2_attn_in["w_value"],
        "L2_ffn_sigma": _L2_ffn_in["sigma"],
        "L2_ffn_phi": _L2_ffn_in["phi"],
        "L2_ffn_M_u": _L2_ffn_in["M_u"],
        "L2_ffn_M_phi_plus": _L2_ffn_in["M_phi_plus"],
        "L2_ffn_M_phi_minus": _L2_ffn_in["M_phi_minus"],
        "L2_ffn_log_weights": _L2_ffn_in["log_weights"],
        "L2_ffn_gumbel": _L2_ffn_in["gumbel"],
        "L3_attn_Wk": _L3_attn_in["Wk"],
        "L3_attn_Wq": _L3_attn_in["Wq"],
        "L3_attn_Wv": _L3_attn_in["Wv"],
        "L3_ffn_router_w": _L3_ffn_in["router_w"],
        "L3_ffn_router_b": _L3_ffn_in["router_b"],
        "L3_ffn_expert_w": _L3_ffn_in["expert_w"],
        "L3_ffn_expert_b": _L3_ffn_in["expert_b"],
    }

def reference(x, L0_conv_w_qkv, L0_conv_pos_emb_h, L0_conv_pos_emb_w, L1_conv_w_in, L1_conv_conv_w, L1_conv_conv_b, L1_conv_w_xproj, L1_conv_w_dt, L1_conv_b_dt, L1_conv_A_log, L1_conv_D_param, L1_conv_ln_w, L1_conv_ln_b, L1_conv_w_out, L2_attn_w_query, L2_attn_w_key, L2_attn_w_value, L2_ffn_sigma, L2_ffn_phi, L2_ffn_M_u, L2_ffn_M_phi_plus, L2_ffn_M_phi_minus, L2_ffn_log_weights, L2_ffn_gumbel, L3_attn_Wk, L3_attn_Wq, L3_attn_Wv, L3_ffn_router_w, L3_ffn_router_b, L3_ffn_expert_w, L3_ffn_expert_b):
    import jax
    import jax.numpy as jnp
    def _L0_conv_ref(x, w_qkv, pos_emb_h, pos_emb_w):
        import jax, jax.numpy as jnp
        import numpy as np
        NUM_HEADS = 4
        KEY_DIMS = 32

        def rel_to_abs(x):
            b, n, w, _ = x.shape
            x = jnp.pad(x, ((0, 0), (0, 0), (0, 0), (0, 1)))
            x = x.reshape(b, n, w * 2 * w)
            x = jnp.pad(x, ((0, 0), (0, 0), (0, w - 1)))
            x = x.reshape(b, n, w + 1, 2 * w - 1)
            return x[:, :, :w, w - 1:]

        def rel_logits_1d(q, rel_k):
            b, nh, xx, yy, d = q.shape
            rl = jnp.einsum('bhxyd,md->bhxym', q, rel_k)
            rl = rel_to_abs(rl.reshape(b, nh * xx, yy, 2 * yy - 1))
            rl = rl.reshape(b, nh, xx, 1, yy, yy)
            return jnp.broadcast_to(rl, (b, nh, xx, xx, yy, yy))

        def relative_position_bias(pos_q, pos_emb_h, pos_emb_w):
            rw = rel_logits_1d(pos_q, pos_emb_w)
            rw = rw.transpose(0, 1, 2, 4, 3, 5)
            rh = rel_logits_1d(pos_q.transpose(0, 1, 3, 2, 4), pos_emb_h)
            rh = rh.transpose(0, 1, 4, 2, 5, 3)
            return rw + rh
        B, H, W, C = x.shape
        nh, kd = (NUM_HEADS, KEY_DIMS)
        qk_dims = nh * kd
        oc = C
        scale = 1.0 / float(kd) ** 0.5
        qkv = jnp.einsum('bhwc,cd->bhwd', x, w_qkv)
        q, k, v = jnp.split(qkv, [qk_dims, 2 * qk_dims], axis=-1)
        L = H * W
        q = q.reshape(B, L, nh, kd).transpose(0, 2, 1, 3)
        k = k.reshape(B, L, nh, kd).transpose(0, 2, 1, 3)
        v = v.reshape(B, L, nh, oc // nh).transpose(0, 2, 1, 3)
        pos_q = q.reshape(B, nh, H, W, kd)
        pos = relative_position_bias(pos_q, pos_emb_h, pos_emb_w).reshape(B, nh, L, L)
        scores = jnp.einsum('bnqd,bnkd->bnqk', q, k) * scale + pos
        attn = jax.nn.softmax(scores, axis=-1)
        out = jnp.einsum('bnqk,bnkd->bnqd', attn, v)
        out = out.transpose(0, 2, 1, 3).reshape(B, H, W, oc)
        return out

    def _L1_conv_ref(x, w_in, conv_w, conv_b, w_xproj, w_dt, b_dt, A_log, D_param, ln_w, ln_b, w_out):
        import jax, jax.numpy as jnp
        import numpy as np
        B, H, W = (4, 64, 64)
        D_MODEL, D_STATE, D_CONV, EXPAND = (128, 16, 3, 2)
        D_INNER = EXPAND * D_MODEL
        DT_RANK = D_MODEL // 16
        LN_EPS = 1e-05

        def _selective_scan(u, delta, A, Bm, Cm, Dp, delta_bias):
            delta = jax.nn.softplus(delta + delta_bias[None, :, None])
            u_t = jnp.moveaxis(u, 2, 0)
            d_t = jnp.moveaxis(delta, 2, 0)
            B_t = jnp.moveaxis(Bm, 2, 0)
            C_t = jnp.moveaxis(Cm, 2, 0)

            def step(h, inp):
                u_i, d_i, b_i, c_i = inp
                dA = jnp.exp(d_i[..., None] * A)
                h = h * dA + (d_i * u_i)[..., None] * b_i[:, None, :]
                y = jnp.einsum('gdn,gn->gd', h, c_i)
                return (h, y)
            h0 = jnp.zeros((u.shape[0], u.shape[1], A.shape[1]), u.dtype)
            _, ys = jax.lax.scan(step, h0, (u_t, d_t, B_t, C_t))
            return jnp.moveaxis(ys, 0, 2) + u * Dp[None, :, None]

        def _forward(x, w_in, conv_w, conv_b, w_xproj, w_dt, b_dt, A_log, D_param, ln_w, ln_b, w_out):
            b, h, w, _ = x.shape
            L = h * w
            xz = x @ w_in
            xc, z = jnp.split(xz, 2, axis=-1)
            pad = (D_CONV - 1) // 2
            xc = jax.lax.conv_general_dilated(xc, conv_w, window_strides=(1, 1), padding=[(pad, pad), (pad, pad)], feature_group_count=D_INNER, dimension_numbers=('NHWC', 'HWIO', 'NHWC')) + conv_b
            xa = jax.nn.silu(xc)
            x_flat = xa.reshape(b, L, D_INNER)
            x_dbl = x_flat @ w_xproj
            dts, Bp, Cp = jnp.split(x_dbl, [DT_RANK, DT_RANK + D_STATE], axis=-1)
            dts = dts @ w_dt
            x_t = jnp.transpose(xa, (0, 2, 1, 3)).reshape(b, L, D_INNER)
            xs = jnp.stack([x_flat, x_t, jnp.flip(x_flat, 1), jnp.flip(x_t, 1)], axis=1)
            xs = xs.reshape(b * 4, L, D_INNER).transpose(0, 2, 1)

            def rep4(t):
                return jnp.broadcast_to(t[:, None], (b, 4) + t.shape[1:]).reshape((b * 4,) + t.shape[1:]).transpose(0, 2, 1)
            dts4, Bp4, Cp4 = (rep4(dts), rep4(Bp), rep4(Cp))
            A = -jnp.exp(A_log.astype(jnp.float32))
            ys = _selective_scan(xs, dts4, A, Bp4, Cp4, D_param.astype(jnp.float32), b_dt.astype(jnp.float32))
            ys = ys.transpose(0, 2, 1).reshape(b, 4, L, D_INNER)
            y = ys[:, 0].reshape(b, h, w, D_INNER) + jnp.transpose(ys[:, 1].reshape(b, w, h, D_INNER), (0, 2, 1, 3)) + jnp.flip(ys[:, 2], 1).reshape(b, h, w, D_INNER) + jnp.transpose(jnp.flip(ys[:, 3], 1).reshape(b, w, h, D_INNER), (0, 2, 1, 3))
            mu = jnp.mean(y, axis=-1, keepdims=True)
            var = jnp.mean(jnp.square(y - mu), axis=-1, keepdims=True)
            y = (y - mu) * jax.lax.rsqrt(var + LN_EPS) * ln_w + ln_b
            y = y * jax.nn.silu(z)
            return y @ w_out
        return _forward(x, w_in, conv_w, conv_b, w_xproj, w_dt, b_dt, A_log, D_param, ln_w, ln_b, w_out)

    def _L2_attn_ref(x, w_query, w_key, w_value):
        import jax, jax.numpy as jnp
        import numpy as np
        EMB = 128
        B, N = (8, 4096)
        q = jnp.einsum('bnd,de->bne', x, w_query)
        k = jnp.einsum('bnd,de->bne', x, w_key)
        v = jnp.einsum('bnd,de->bne', x, w_value)
        dk = k.shape[-1]
        scale = jnp.einsum('bqd,bkd->bqk', q, k) / jnp.sqrt(jnp.float32(dk))
        probs = jax.nn.softmax(scale, axis=2)
        return jnp.einsum('bqk,bkd->bqd', probs, v)

    def _L2_ffn_ref(x, sigma, phi, M_u, M_phi_plus, M_phi_minus, log_weights, gumbel):
        import jax, jax.numpy as jnp
        import numpy as np
        PADDED_SL = 8192
        TEMPERATURE = 1.0
        SIGMA_POW = 0.25

        def _stu_conv(phi, u, n):
            b, sl, d = u.shape
            sgn = jnp.where(jnp.arange(sl) % 2 == 0, 1.0, -1.0).astype(u.dtype)
            sgn3 = sgn[None, :, None]
            Vf = jnp.fft.rfft(phi, n=n, axis=0)
            Uf_p = jnp.fft.rfft(u, n=n, axis=1)
            Uf_m = jnp.fft.rfft(u * sgn3, n=n, axis=1)
            U_plus = jnp.fft.irfft(Vf[None, :, :, None] * Uf_p[:, :, None, :], n=n, axis=1)[:, :sl]
            U_minus = jnp.fft.irfft(Vf[None, :, :, None] * Uf_m[:, :, None, :], n=n, axis=1)[:, :sl]
            U_minus = U_minus * sgn[None, :, None, None]
            return (U_plus, U_minus)

        def _compute_spectral(u, sigma, phi, Mpp, Mpm):
            U_plus, U_minus = _stu_conv(phi, u, PADDED_SL)
            s = sigma ** SIGMA_POW
            out = jnp.einsum('btkd,k,kde->bte', U_plus, s, Mpp)
            out = out + jnp.einsum('btkd,k,kde->bte', U_minus, s, Mpm)
            return out

        def _compute_ar_u(Mu, u):
            sl = u.shape[1]
            out = jnp.zeros(u.shape[:2] + (Mu.shape[-1],), dtype=u.dtype)
            for i in range(Mu.shape[0]):
                ui = jnp.pad(u, ((0, 0), (i, 0), (0, 0)))[:, :sl]
                out = out + jnp.einsum('btd,de->bte', ui, Mu[i])
            return out

        def _stu(u, sigma, phi, Mu, Mpp, Mpm):
            return _compute_spectral(u, sigma, phi, Mpp, Mpm) + _compute_ar_u(Mu, u)
        T = x.shape[1]
        outs = []
        for i, frac in enumerate((1, 2, 4, 8)):
            xi = x[:, :T // frac]
            si = _stu(xi, sigma, phi, M_u[i], M_phi_plus[i], M_phi_minus[i])
            si = jnp.pad(si, ((0, 0), (0, T - si.shape[1]), (0, 0)))
            outs.append(si)
        y_soft = jax.nn.softmax((log_weights + gumbel) / TEMPERATURE)
        y_hard = jax.nn.one_hot(jnp.argmax(y_soft), 4, dtype=y_soft.dtype)
        weights = y_hard - jax.lax.stop_gradient(y_soft) + y_soft
        stacked = jnp.stack(outs, axis=-1)
        return jnp.sum(stacked * weights, axis=-1)

    def _L3_attn_ref(x, Wk, Wq, Wv):
        import jax, jax.numpy as jnp
        import numpy as np
        B, N, D = (8, 8192, 128)
        H, KQ = (8, 64)
        K = jnp.einsum('bnd,hkd->bhnk', x, Wk)
        Q = jnp.einsum('bnd,hkd->bhnk', x, Wq)
        V = jnp.einsum('bnd,hed->bhne', x, Wv)
        KtV = jnp.einsum('bhnk,bhne->bhke', K, V)
        out = jnp.einsum('bhnk,bhke->bne', Q, KtV)
        return out

    def _L3_ffn_ref(x, router_w, router_b, expert_w, expert_b):
        import jax, jax.numpy as jnp
        import numpy as np
        B, N, D, C, E, K = (8, 8192, 128, 128, 8, 2)
        router_probs = jax.nn.softmax(x @ router_w + router_b, axis=-1)
        top_p, top_i = jax.lax.top_k(router_probs, K)
        top_p = top_p / jnp.sum(top_p, axis=-1, keepdims=True)
        expert_out = jnp.einsum('bnd,edc->bnec', x, expert_w) + expert_b
        gathered = jnp.take_along_axis(expert_out, top_i[..., None], axis=2)
        return jnp.einsum('bnk,bnkc->bnc', top_p, gathered)

    def _gn(v, G=32, eps=1e-5):
        B_, H_, W_, C_ = v.shape
        g = v.reshape(B_, H_, W_, G, C_ // G)
        m = jnp.mean(g, axis=(1, 2, 4), keepdims=True)
        s = jnp.var(g, axis=(1, 2, 4), keepdims=True)
        return ((g - m) / jnp.sqrt(s + eps)).reshape(v.shape)

    def _ln_c(v, eps=1e-6):
        m = jnp.mean(v, axis=-1, keepdims=True)
        s = jnp.var(v, axis=-1, keepdims=True)
        return (v - m) / jnp.sqrt(s + eps)

    def _ln_t(v, eps=1e-5):
        m = jnp.mean(v, axis=-1, keepdims=True)
        s = jnp.var(v, axis=-1, keepdims=True)
        return (v - m) / jnp.sqrt(s + eps)

    def _to_tokens(v):
        B_, H_, W_, C_ = v.shape
        return v.reshape(B_, H_ * W_, C_)
    def _from_tokens(t, like):
        return t.reshape(like.shape)

    x = x + _L0_conv_ref(_gn(x), L0_conv_w_qkv, L0_conv_pos_emb_h, L0_conv_pos_emb_w)
    x = x + _L1_conv_ref(_gn(x), L1_conv_w_in, L1_conv_conv_w, L1_conv_conv_b, L1_conv_w_xproj, L1_conv_w_dt, L1_conv_b_dt, L1_conv_A_log, L1_conv_D_param, L1_conv_ln_w, L1_conv_ln_b, L1_conv_w_out)
    t = _to_tokens(x)
    t = t + _L2_attn_ref(_ln_t(t), L2_attn_w_query, L2_attn_w_key, L2_attn_w_value)
    t = t + _L2_ffn_ref(_ln_t(t), L2_ffn_sigma, L2_ffn_phi, L2_ffn_M_u, L2_ffn_M_phi_plus, L2_ffn_M_phi_minus, L2_ffn_log_weights, L2_ffn_gumbel)
    t = t + _L3_attn_ref(_ln_t(t), L3_attn_Wk, L3_attn_Wq, L3_attn_Wv)
    t = t + _L3_ffn_ref(_ln_t(t), L3_ffn_router_w, L3_ffn_router_b, L3_ffn_expert_w, L3_ffn_expert_b)
    x = _from_tokens(t, x)
    return x


_drawn_inputs = setup_inputs


def setup_inputs(seed=0):
    import zlib

    import numpy as np

    out = dict(_drawn_inputs(seed))
    spreads = {'L1_conv_D_param': (1.0, 0.2),
     'L1_conv_ln_w': (1.0, 0.2),
     'L1_conv_ln_b': (0.0, 0.387),
     'L2_ffn_log_weights': (1.0, 0.2),
     'L3_ffn_router_b': (0.0, 2.0),
     'L3_ffn_expert_b': (0.0, 2.0)}
    factors = {'L0_conv_pos_emb_h': 7.209,
     'L0_conv_pos_emb_w': 7.22,
     'L1_conv_w_xproj': 64.0,
     'L1_conv_w_dt': 200.0,
     'L1_conv_b_dt': 200.0,
     'L1_conv_A_log': 200.0,
     'L3_ffn_router_w': 8.0,
     'L3_ffn_expert_w': 8.0}
    for name, (base, spread) in spreads.items():
        noise = np.random.default_rng([zlib.crc32(name.encode()), seed]).standard_normal(out[name].shape)
        drawn = base * np.exp(spread * noise) if base else spread * noise
        out[name] = jnp.asarray(drawn.astype(out[name].dtype))
    for name, factor in factors.items():
        out[name] = (out[name] * factor).astype(out[name].dtype)
    return out
```

```python
from contextlib import ExitStack

import concourse.bass as bass
from concourse import mybir

F32 = mybir.dt.float32
F32R = mybir.dt.float32r
ALU = mybir.AluOpType
ACT = mybir.ActivationFunctionType
AX = mybir.AxisListType

P = 128
BATCH = 2
SIDE = 64
L = SIDE * SIDE
TOK = BATCH * L
TW = 512
NT = TOK // TW
NTB = L // TW
KT = L // P


class Mem:

    def __init__(self, nc, stage, sems=None):
        self.nc, self.stage, self.stack, self.blocks, self.held = nc, stage, ExitStack(), ExitStack(), []

    def __enter__(self):
        self.stack.__enter__()
        return self

    def __exit__(self, *how):
        self.blocks.close()
        if how[0] is None:
            with self.nc.Block() as block:
                @block.sync
                def _(sp):
                    for s in self.held:
                        sp.sem_clear(s)
        return self.stack.__exit__(*how)

    def sb(self, name, shape, dtype=F32):
        return self.stack.enter_context(self.nc.sbuf_tensor(f"{self.stage}_{name}", shape, dtype))

    def ps(self, name, shape, dtype=F32):
        return self.stack.enter_context(self.nc.psum_tensor(f"{self.stage}_ps_{name}", shape, dtype))

    def sem(self, name):
        self.held.append(self.stack.enter_context(self.nc.semaphore(f"{self.stage}_sem_{name}")))
        return self.held[-1]

    def block(self):
        return self.blocks.enter_context(self.nc.Block())


class Chain:

    def __init__(self, eng, sem):
        self.eng, self.sem, self.n = eng, sem, 0

    def step(self, ins):
        self.n += 1
        ins.then_inc(self.sem, 1)

    def done(self):
        self.eng.wait_ge(self.sem, self.n)

    def link(self, ins):
        self.step(ins)
        self.done()
def group_norm(nc, sems, stage, x, xn, group_mean, eps, addend=None, x_sum=None):
    with Mem(nc, stage, sems) as m:
        xs = m.sb("x", [P, TOK])
        more = m.sb("addend", [P, TOK]) if addend is not None else None
        xo = m.sb("xn", [P, TOK])
        added, sum_stored = m.sem("added"), m.sem("sum_stored")
        gm = m.sb("group_mean", [P, P])
        stats = m.sb("stats", [P, BATCH, NTB, 6])
        aggr = m.sb("aggr", [P, BATCH, 2])
        mom = m.sb("moments", [P, BATCH, 2])
        grp = m.sb("group_moments", [P, BATCH, 2])
        msq = m.sb("mean_squared", [P, BATCH, 1])
        var = m.sb("variance", [P, BATCH, 1])
        std = m.sb("deviation", [P, BATCH, 1])
        rstd = m.sb("reciprocal", [P, BATCH, 1])
        gps = m.ps("sums", [P, BATCH, 2])
        loaded, weights = m.sem("loaded"), m.sem("weights")
        own, moments, sums, variance, deviation = (m.sem(n) for n in ("own", "moments", "sums", "variance", "deviation"))
        normed, stored = m.sem("normed"), m.sem("stored")
        block = m.block()

        @block.sync
        def _(sp):
            sp.dma_start(gm[:, :], group_mean).then_inc(weights, 16)
            for b in range(BATCH):
                sp.dma_start(xs[:, b * L:(b + 1) * L], x[:, b * L:(b + 1) * L]).then_inc(loaded, 16)
                if more is not None:
                    sp.dma_start(more[:, b * L:(b + 1) * L], addend[:, b * L:(b + 1) * L]).then_inc(loaded, 16)
            if more is not None:
                sp.wait_ge(added, BATCH)
                sp.dma_start(x_sum, xs[:, :]).then_inc(sum_stored, 16)
                sp.wait_ge(sum_stored, 16)
            for b in range(BATCH):
                sp.wait_ge(normed, b + 1)
                sp.dma_start(xn[:, b * L:(b + 1) * L], xo[:, b * L:(b + 1) * L]).then_inc(stored, 16)
            sp.wait_ge(stored, 16 * BATCH)

        @block.vector
        def _(dve):
            own_chain = Chain(dve, own)
            dve.wait_ge(loaded, 16 * BATCH * (1 if more is None else 2))
            if more is not None:
                for b in range(BATCH):
                    part = slice(b * L, (b + 1) * L)
                    dve.tensor_tensor(xs[:, part], xs[:, part], more[:, part], ALU.add).then_inc(added, 1)
                dve.wait_ge(added, BATCH)
            for b in range(BATCH):
                for t in range(NTB):
                    own_chain.step(dve.bn_stats(stats[:, b, t, :], xs[:, b * L + t * TW:b * L + (t + 1) * TW]))
            own_chain.done()
            for b in range(BATCH):
                own_chain.step(dve.bn_aggr(aggr[:, b, :], stats[:, b, :, :]))
            own_chain.done()
            own_chain.link(dve.tensor_tensor(msq[:, :, :], aggr[:, :, 0:1], aggr[:, :, 0:1], ALU.mult))
            dve.tensor_copy(mom[:, :, 0:1], aggr[:, :, 0:1]).then_inc(moments, 1)
            dve.tensor_tensor(mom[:, :, 1:2], msq[:, :, :], aggr[:, :, 1:2], ALU.add).then_inc(moments, 1)
            dve.wait_ge(sums, 1)
            own_chain.link(dve.tensor_copy(grp[:, :, :], gps[:, :, :]))
            own_chain.link(dve.tensor_tensor(msq[:, :, :], grp[:, :, 0:1], grp[:, :, 0:1], ALU.mult))
            own_chain.link(dve.tensor_tensor(var[:, :, :], grp[:, :, 1:2], msq[:, :, :], ALU.subtract))
            dve.tensor_scalar(std[:, :, :], var[:, :, :], 0.0, eps, ALU.max, ALU.add).then_inc(variance, 1)
            dve.wait_ge(deviation, 1)
            own_chain.link(dve.reciprocal(rstd[:, :, :], var[:, :, :]))
            for b in range(BATCH):
                part = slice(b * L, (b + 1) * L)
                dve.tensor_scalar(xo[:, part], xs[:, part], grp[:, b, 0:1], rstd[:, b, 0:1], ALU.subtract, ALU.mult).then_inc(normed, 1)

        @block.tensor
        def _(pe):
            pe.wait_ge(weights, 16)
            pe.wait_ge(moments, 2)
            pe.matmul(gps[:, :, :], gm[:, :], mom[:, :, :], start=True, stop=True).then_inc(sums, 1)

        @block.scalar
        def _(act):
            act.wait_ge(variance, 1)
            act.activation(var[:, :, :], std[:, :, :], ACT.Sqrt).then_inc(deviation, 1)


def layer_norm(nc, sems, stage, x, xn, channel_mean, eps):
    with Mem(nc, stage, sems) as m:
        xs, xc, sq = m.sb("x", [P, TOK]), m.sb("centred", [P, TOK]), m.sb("square", [P, TOK])
        cm = m.sb("channel_mean", [P, P])
        epst = m.sb("eps", [P, 1])
        std, rstd = m.sb("deviation", [P, 2, TW]), m.sb("reciprocal", [P, 2, TW])
        mean_ps, var_ps = m.ps("mean", [P, 2, TW]), m.ps("variance", [P, 2, TW])
        loaded, weights, own = m.sem("loaded"), m.sem("weights"), m.sem("own")
        mean, centred, squared, variance, deviation, recip, normed, stored = (
            m.sem(n) for n in ("mean", "centred", "squared", "variance", "deviation", "recip", "normed", "stored"))
        block = m.block()
        lot = 4

        def at(t):
            return slice(t * TW, (t + 1) * TW)

        @block.sync
        def _(sp):
            sp.dma_start(cm[:, :], channel_mean).then_inc(weights, 16)
            for t in range(0, NT, lot):
                part = slice(t * TW, (t + lot) * TW)
                sp.dma_start(xs[:, part], x[:, part]).then_inc(loaded, 16)
            for t in range(0, NT, lot):
                part = slice(t * TW, (t + lot) * TW)
                sp.wait_ge(normed, t + lot)
                sp.dma_start(xn[:, part], xc[:, part]).then_inc(stored, 16)
            sp.wait_ge(stored, 16 * NT // lot)

        @block.tensor
        def _(pe):
            pe.wait_ge(weights, 16)
            pe.wait_ge(loaded, 16 * NT // lot)
            for t in range(NT + 1):
                if t < NT:
                    if t >= 2:
                        pe.wait_ge(centred, t - 1)
                    pe.matmul(mean_ps[:, t % 2, :], cm[:, :], xs[:, at(t)], start=True, stop=True).then_inc(mean, 1)
                if t >= 1:
                    u = t - 1
                    pe.wait_ge(squared, u + 1)
                    if u >= 2:
                        pe.wait_ge(deviation, u - 1)
                    pe.matmul(var_ps[:, u % 2, :], cm[:, :], sq[:, at(u)], start=True, stop=True).then_inc(variance, 1)

        @block.scalar
        def _(act):
            act.wait_ge(own, 1)
            for t in range(NT):
                act.wait_ge(centred, t + 1)
                act.activation(sq[:, at(t)], xc[:, at(t)], ACT.Square).then_inc(squared, 1)
                act.wait_ge(variance, t + 1)
                if t >= 2:
                    act.wait_ge(recip, t - 1)
                act.activation(std[:, t % 2, :], var_ps[:, t % 2, :], ACT.Sqrt, bias=epst[:, :]).then_inc(deviation, 1)

        @block.vector
        def _(dve):
            dve.memset(epst[:, :], eps).then_inc(own, 1)
            dve.wait_ge(loaded, 16 * NT // lot)
            for t in range(NT + 1):
                if t < NT:
                    dve.wait_ge(mean, t + 1)
                    dve.tensor_tensor(xc[:, at(t)], xs[:, at(t)], mean_ps[:, t % 2, :], ALU.subtract).then_inc(centred, 1)
                if t >= 1:
                    u = t - 1
                    dve.wait_ge(deviation, u + 1)
                    if u >= 2:
                        dve.wait_ge(normed, u - 1)
                    dve.reciprocal(rstd[:, u % 2, :], std[:, u % 2, :]).then_inc(recip, 1)
                    dve.wait_ge(recip, u + 1)
                    dve.wait_ge(squared, u + 1)
                    dve.tensor_tensor(xc[:, at(u)], xc[:, at(u)], rstd[:, u % 2, :], ALU.mult).then_inc(normed, 1)
def bias_attention(nc, sems, stage, xn, att, w_heads, emb_h, emb_w, cells_in, ident_in, pick_in):
    HEADS, D = 4, 32
    SCALE = 1.0 / float(D) ** 0.5
    LINKS = 4 * NTB + 1
    IT_JOBS = 2 * NTB + 2 + 2 * NTB + NTB
    with Mem(nc, stage, sems) as m:
        xs = m.sb("xn", [P, L])
        w = m.sb("w", [P, 2 * P + D])
        eh, ew = m.sb("emb_h", [D, 2 * SIDE - 1]), m.sb("emb_w", [D, 2 * SIDE - 1])
        ident, pick = m.sb("ident", [P, P]), m.sb("pick", [P, 2 * D])
        cells = m.sb("cells", [P, L], F32R)
        qs, ks = m.sb("q_parts", [P, L], F32R), m.sb("k_parts", [P, L], F32R)
        q32 = m.sb("q", [D, L])
        r32 = m.sb("bias", [P, L])
        rh, rl = m.sb("bias_high", [P, L], F32R), m.sb("bias_low", [P, L], F32R)
        vv = m.sb("v_and_ones", [P, KT, 2 * D])
        mx2, mx = m.sb("max_halves", [P, KT, 2]), m.sb("max", [P, KT])
        mxw = m.sb("max_wide", [P, KT, SIDE])
        pt = m.sb("probs", [P, 4, TW])
        osb = m.sb("out_parts", [P, TW])
        inv, o32 = m.sb("inverse", [D, TW]), m.sb("out", [D, 2, TW])
        ps = m.ps("all", [P, 8, TW])
        entered = m.sem("entered")
        const, cells_ok, ones_ok = m.sem("const"), m.sem("cells_ok"), m.sem("ones_ok")
        image_in, w_in = m.sem("image_in"), m.sem("w_in")
        filled, taken, own = m.sem("filled"), m.sem("taken"), m.sem("own")
        max_filled, max_taken, wide_ok = m.sem("max_filled"), m.sem("max_taken"), m.sem("wide_ok")
        scored, expd, weighed = m.sem("scored"), m.sem("expd"), m.sem("weighed")
        parts_ok, summed, parted = m.sem("parts_ok"), m.sem("summed"), m.sem("inverted")
        divided, stored = m.sem("divided"), [m.sem("stored0"), m.sem("stored1")]
        block = m.block()
        raw_cells = r32

        def f(ap):
            return ap.bitcast(F32)

        @block.sync
        def _(sp):
            for s in stored:
                sp.sem_inc(s, 16)
            for dst, src in ((eh, emb_h), (ew, emb_w), (ident, ident_in), (pick, pick_in), (raw_cells, cells_in)):
                sp.dma_start(dst[:], src).then_inc(const, 16)
            with sp.Fori(0, BATCH) as b:
                with sp.Fori(0, HEADS) as h:
                    it = b * HEADS + h
                    sp.wait_ge(filled, it * IT_JOBS + 1)
                    sp.dma_start(xs[:, :], xn[:, bass.ts(b, L)]).then_inc(image_in, 16)
                    sp.dma_start(w[:, :], w_heads[bass.ts(h, P), :]).then_inc(w_in, 16)
                    for j in range(NTB):
                        sp.wait_ge(divided, it * NTB + j + 2)
                        sp.dma_start(att[bass.ts(h, D), bass.ds(b * L + j * TW, TW)], o32[:, j % 2, :]).then_inc(stored[j % 2], 16)
            for s in stored:
                sp.wait_ge(s, 8 * NTB * BATCH * HEADS + 16)

        @block.tensor
        def _(pe):
            pe.sem_inc(filled, 1)
            pe.sem_inc(summed, 1)
            pe.wait_ge(const, 80)
            pe.wait_ge(cells_ok, 1)
            with pe.Fori(0, BATCH * HEADS) as it:
                job0 = it * IT_JOBS + 1
                pe.wait_ge(image_in, it * 16 + 16)
                pe.wait_ge(w_in, it * 16 + 16)
                n = 0

                def bank_free(k):
                    if k >= 4:
                        pe.wait_ge(taken, job0 + (k - 3))

                for part in range(2):
                    for t in range(NTB):
                        bank_free(n)
                        pe.matmul(ps[:, n % 4, :], w[:, part * P:(part + 1) * P], xs[:, t * TW:(t + 1) * TW],
                                  start=True, stop=True).then_inc(filled, 1)
                        n += 1
                for half in range(2):
                    bank_free(n)
                    for t in range(KT // 2):
                        tok = (half * KT // 2 + t) * P
                        ins = pe.matmul(ps[:, n % 4, t * D:(t + 1) * D], xs[:, tok:tok + P], w[:, 2 * P:2 * P + D],
                                        start=True, stop=True)
                    ins.then_inc(filled, 1)
                    n += 1
                for g in range(NTB):
                    bank_free(n)
                    if g == 0:
                        pe.wait_ge(taken, job0 + NTB)
                    for k in range(8):
                        x = 8 * g + k
                        ins = pe.matmul(ps[0:SIDE, n % 4, k * SIDE:(k + 1) * SIDE], eh[:, SIDE - 1 - x:2 * SIDE - 1 - x],
                                        q32[:, x * SIDE:(x + 1) * SIDE], start=True, stop=True)
                    ins.then_inc(filled, 1)
                    n += 1
                qcol = q32[:, :].rearrange("d (x y) -> d y x", y=SIDE)
                for g in range(NTB):
                    bank_free(n)
                    for k in range(8):
                        y = 8 * g + k
                        ins = pe.matmul(ps[SIDE:P, n % 4, k * SIDE:(k + 1) * SIDE], ew[:, SIDE - 1 - y:2 * SIDE - 1 - y],
                                        qcol[:, y, :], start=True, stop=True)
                    ins.then_inc(filled, 1)
                    n += 1
                pe.wait_ge(taken, job0 + n)
                for t in range(KT):
                    for half in range(2):
                        k = 2 * t + half
                        if k >= 2:
                            pe.wait_ge(max_taken, it * 2 * KT + (k - 1))
                        for c in range(4):
                            o, keys = ps[:, 4 * half + c, :], slice((4 * half + c) * TW, (4 * half + c + 1) * TW)
                            pe.matmul(o, qs[:, t * P:(t + 1) * P], ks[:, keys], start=True, stop=False)
                            ins = pe.matmul(o, rh[:, t * P:(t + 1) * P], cells[:, keys], start=False, stop=True)
                        ins.then_inc(max_filled, 1)
                pe.wait_ge(wide_ok, it + 1)
                for t in range(NTB):
                    for k in range(4):
                        ins = pe.matmul(ps[0:SIDE, t, k * P:(k + 1) * P], mxw[:, 4 * t + k, :], ident[:, :], start=True, stop=True)
                    ins.then_inc(filled, 1)
                    n += 1
                pe.wait_ge(taken, job0 + n)
                pe.sem_inc(entered, 1)
                with pe.Fori(0, NTB) as j:
                    row = it * NTB + j
                    tile0 = row * KT
                    obank = ps[:, 4, :]
                    queries = bass.ts(j, TW)

                    def score(i):
                        if i >= 4:
                            pe.wait_ge(expd, tile0 + (i - 3))
                        o, keys = ps[:, i % 4, :], slice(i * P, (i + 1) * P)
                        pe.matmul(o, ks[:, keys], qs[:, queries], start=True, stop=False)
                        pe.matmul(o, cells[:, keys], rh[:, queries], start=False, stop=False)
                        pe.matmul(o, cells[:, keys], rl[:, queries], start=False, stop=True).then_inc(scored, 1)

                    for i in range(3):
                        score(i)
                    pe.wait_ge(parts_ok, row + 1)
                    for i in range(KT):
                        if i + 3 < KT:
                            score(i + 3)
                        pe.wait_ge(expd, tile0 + (i + 1))
                        s = SIDE * (i % 2)
                        pe.matmul(ps[s:s + SIDE, 4, :], vv[:, i, :], pt[:, i % 4, :], start=(i < 2), stop=(i >= KT - 2)).then_inc(weighed, 1)
                    pe.wait_ge(parts_ok, row + 2)
                    pe.wait_ge(divided, row + 1)
                    pe.matmul(ps[0:D, 5, :], pick[:, 0:D], osb[:, :], start=True, stop=True)
                    pe.matmul(ps[0:D, 6, :], pick[:, D:2 * D], osb[:, :], start=True, stop=True).then_inc(summed, 1)

        @block.scalar
        def _(act):
            with act.Fori(0, BATCH * HEADS * NTB) as row:
                for i in range(KT):
                    act.wait_ge(scored, row * KT + (i + 1))
                    if i >= 4:
                        act.wait_ge(weighed, row * KT + (i - 3))
                    act.activation(pt[:, i % 4, :], ps[:, i % 4, :], ACT.Exp).then_inc(expd, 1)

        @block.vector
        def _(dve):
            for s in (taken, parts_ok, divided):
                dve.sem_inc(s, 1)
            dve.memset(vv[:, :, D:2 * D], 1.0).then_inc(ones_ok, 1)
            dve.wait_ge(const, 80)
            dve.tensor_copy(cells[:, :], raw_cells[:, :]).then_inc(cells_ok, 1)
            dve.wait_ge(cells_ok, 1)
            with dve.Fori(0, BATCH * HEADS) as it:
                job0 = it * IT_JOBS + 1
                link0 = it * LINKS
                links = 0

                def link(ins):
                    nonlocal links
                    links += 1
                    ins.then_inc(own, 1)
                    dve.wait_ge(own, link0 + links)

                n = 0
                for t in range(NTB):
                    dve.wait_ge(filled, job0 + (n + 1))
                    cols, bank = slice(t * TW, (t + 1) * TW), n % 4
                    dve.tensor_copy(q32[:, cols], ps[0:D, bank, :])
                    link(dve.tensor_copy(qs[:, cols], ps[:, bank, :]))
                    for s in (D, 3 * D):
                        ins = dve.tensor_tensor(qs[s:s + D, cols], ps[s:s + D, bank, :], f(qs[s:s + D, cols]), ALU.subtract)
                    ins.then_inc(taken, 1)
                    n += 1
                for t in range(NTB):
                    dve.wait_ge(filled, job0 + (n + 1))
                    cols, bank = slice(t * TW, (t + 1) * TW), n % 4
                    link(dve.tensor_scalar(ks[:, cols], ps[:, bank, :], SCALE, None, ALU.mult))
                    dve.scalar_tensor_tensor(ks[SIDE:P, cols], ps[SIDE:P, bank, :], SCALE, f(ks[SIDE:P, cols]),
                                             ALU.mult, ALU.subtract).then_inc(taken, 1)
                    n += 1
                for half in range(2):
                    dve.wait_ge(filled, job0 + (n + 1))
                    dve.tensor_copy(vv[:, half * KT // 2:(half + 1) * KT // 2, 0:D],
                                    ps[:, n % 4, :].rearrange("p (t d) -> p t d", d=D)).then_inc(taken, 1)
                    n += 1
                for g in range(NTB):
                    dve.wait_ge(filled, job0 + (n + 1))
                    cols = slice(g * TW, (g + 1) * TW)
                    dve.tensor_copy(r32[0:SIDE, cols], ps[0:SIDE, n % 4, :])
                    dve.tensor_copy(rh[0:SIDE, cols], ps[0:SIDE, n % 4, :]).then_inc(taken, 1)
                    n += 1
                for g in range(NTB):
                    dve.wait_ge(filled, job0 + (n + 1))
                    src = ps[SIDE:P, n % 4, :].rearrange("p (y x) -> p y x", x=SIDE)
                    for dst in (r32, rh):
                        ins = dve.tensor_copy(dst[SIDE:P, :].rearrange("p (x y) -> p y x", y=SIDE)[:, 8 * g:8 * g + 8, :], src)
                    ins.then_inc(taken, 1)
                    n += 1
                for k in range(2 * KT):
                    dve.wait_ge(max_filled, it * 2 * KT + (k + 1))
                    half = k % 2
                    dve.tensor_reduce(mx2[:, k // 2, half:half + 1], ps[:, 4 * half:4 * half + 4, :], AX.XY, ALU.max).then_inc(max_taken, 1)
                dve.wait_ge(max_taken, it * 2 * KT + 2 * KT)
                link(dve.tensor_reduce(mx[:, :], mx2[:, :, :], AX.X, ALU.max))
                dve.tensor_copy(mxw[:, :, :], mx[:, :].rearrange("p (t a) -> p t a", a=1).to_broadcast((P, KT, SIDE))).then_inc(wide_ok, 1)
                for t in range(NTB):
                    dve.wait_ge(filled, job0 + (n + 1))
                    cols = slice(t * TW, (t + 1) * TW)
                    link(dve.tensor_tensor(r32[0:SIDE, cols], r32[0:SIDE, cols], ps[0:SIDE, t, :], ALU.subtract))
                    link(dve.tensor_copy(rh[:, cols], r32[:, cols]))
                    dve.tensor_tensor(rl[:, cols], r32[:, cols], f(rh[:, cols]), ALU.subtract).then_inc(taken, 1)
                    n += 1
                assert links == LINKS and n == IT_JOBS
                for j in range(NTB):
                    row = it * NTB + j
                    dve.wait_ge(weighed, row * KT + KT)
                    dve.wait_ge(summed, row + 1)
                    dve.tensor_copy(osb[:, :], ps[:, 4, :]).then_inc(parts_ok, 1)
                    dve.wait_ge(summed, row + 2)
                    dve.reciprocal(inv[:, :], ps[0:D, 6, :]).then_inc(parted, 1)
                    dve.wait_ge(parted, row + 1)
                    dve.wait_ge(stored[j % 2], 8 * NTB * it + 16 * (j // 2 + 1))
                    dve.tensor_tensor(o32[:, j % 2, :], ps[0:D, 5, :], inv[:, :], ALU.mult).then_inc(divided, 1)
INNER_TILES, STATES, RANK, DIRS = 2, 16, 8, 4


W = 1024
CHUNKS = L // W


def in_chunks(steps):
    return steps.rearrange("p (q t) -> p q t", t=W)


def scan_order(image, direction):
    part, (step, _), base = list(image.ap[0]), image.ap[1], image.offset
    if direction == 0:
        return image.rearrange("p (a c) -> p a c", c=SIDE)
    if direction == 1:
        return image.rearrange("p (a c) -> p c a", c=SIDE)
    last = base + (L - 1) * step
    strides = (SIDE, 1) if direction == 2 else (1, SIDE)
    return bass.AP(image.tensor, last, [part] + [[-s * step, SIDE] for s in strides])


def log1p_coefficients():
    import numpy as np
    n = 10
    x = (np.cos(np.pi * (np.arange(400) + 0.5) / 400) + 1) / 2
    fit = np.polynomial.chebyshev.Chebyshev.fit(x, np.log1p(x) / x, n, domain=[0, 1])
    return [float(c) for c in fit.convert(kind=np.polynomial.Polynomial).coef]


def mamba_prepare(nc, sems, stage, xn, gates, u_img, delta, du, bc, w_in, conv_w, conv_b, w_x, w_dt, b_dt, ident_in):
    PADW = SIDE + 2
    CO = log1p_coefficients()
    ROWS = TW // SIDE
    plan = []
    for b in range(BATCH):
        for ct in range(INNER_TILES):
            plan += [(kind, b, ct, t) for kind in ("inner", "gate", "conv") for t in range(NTB)]
        plan += [("bc", b, 0, t) for t in range(NTB)] + [("rank", b, 0, t) for t in range(NTB)]
        for ct in range(INNER_TILES):
            plan += [("step", b, ct, t) for t in range(NTB)]
    on_dve = ("bc", "step")
    number = {job: n for n, job in enumerate(plan)}
    dve_jobs = [job for job in plan if job[0] in on_dve]
    act_jobs = [job for job in plan if job[0] not in on_dve]
    dve_number = {job: n for n, job in enumerate(dve_jobs)}
    act_number = {job: n for n, job in enumerate(act_jobs)}
    last = NTB - 1
    with Mem(nc, stage, sems) as m:
        xs, wi = m.sb("xn", [P, L]), m.sb("w_in", [P, 4 * P])
        cw, cb, bd = m.sb("conv_w", [P, INNER_TILES, 9]), m.sb("conv_b", [P, INNER_TILES]), m.sb("b_dt", [P, INNER_TILES])
        wx, wd, ident = m.sb("w_x", [P, INNER_TILES, 64 + RANK]), m.sb("w_dt", [RANK, INNER_TILES * P]), m.sb("ident", [P, P])
        diag = m.sb("conv_diagonals", [P, INNER_TILES, 9, P])
        padded = m.sb("padded", [P, PADW, PADW])
        xa = m.sb("u", [P, INNER_TILES, L])
        bcs, rank = m.sb("bc_parts", [64, L], F32R), m.sb("rank", [RANK, L])
        s, e, poly = m.sb("step", [P, L]), m.sb("exp", [P, L]), m.sb("poly", [P, L])
        dus = m.sb("delta_u", [P, 2, L])
        gs = m.sb("gate", [P, 4, TW])
        ps = m.ps("all", [P, 8, TW])
        names = ("const", "image_in", "border", "filled", "act_taken", "dve_taken", "own", "diagonals", "magnitude",
                 "expd", "delta_ok", "du_ok", "bc_stored", "u_stored", "conv_done", "bc_ok")
        (const, image_in, border, filled, act_taken, dve_taken, own, diagonals, magnitude, expd, delta_ok, du_ok,
         bc_stored, u_stored, conv_done, bc_ok) = (m.sem(n) for n in names)
        gate_stored = [m.sem(f"gate_stored{i}") for i in range(4)]
        du_stored = [m.sem(f"du_stored{i}") for i in range(2)]
        delta_stored = m.sem("delta_stored")
        block = m.block()

        @block.sync
        def _(sp):
            for dst, src in ((wi, w_in), (cw, conv_w), (cb, conv_b), (bd, b_dt), (wx, w_x), (wd, w_dt), (ident, ident_in)):
                sp.dma_start(dst[:], src).then_inc(const, 16)
            for b in range(BATCH):
                if b:
                    sp.wait_ge(filled, number["gate", b - 1, 1, last] + 1)
                sp.dma_start(xs[:, :], xn[:, b * L:(b + 1) * L]).then_inc(image_in, 16)
                for ct in range(INNER_TILES):
                    for t in range(NTB):
                        n = act_number["gate", b, ct, t]
                        sp.wait_ge(act_taken, n + 1)
                        sp.dma_start(gates[b, ct, :, t * TW:(t + 1) * TW], gs[:, t % 4, :]).then_inc(gate_stored[t % 4], 16)
                for ct in range(INNER_TILES):
                    sp.wait_ge(act_taken, act_number["conv", b, ct, last] + 1)
                    sp.dma_start(u_img[b, ct], xa[:, ct, :]).then_inc(u_stored, 16)
                sp.wait_ge(dve_taken, dve_number["bc", b, 0, last] + 1)
                sp.dma_start(bc[b], in_chunks(bcs[:, :].bitcast(F32))).then_inc(bc_stored, 16)
                for ct in range(INNER_TILES):
                    g = b * INNER_TILES + ct
                    sp.wait_ge(delta_ok, g + 1)
                    sp.dma_start(delta[g], in_chunks(s[:, :])).then_inc(delta_stored, 16)
                    for d in range(DIRS):
                        sp.wait_ge(du_ok, g * DIRS + d + 1)
                        sp.dma_start(du[g, :, :, d], in_chunks(dus[:, d % 2, :])).then_inc(du_stored[d % 2], 16)
            for q in gate_stored:
                sp.wait_ge(q, 16 * NTB * BATCH * INNER_TILES // 4)
            for q in du_stored:
                sp.wait_ge(q, 16 * DIRS * BATCH * INNER_TILES // 2)
            sp.wait_ge(u_stored, 16 * BATCH * INNER_TILES)
            sp.wait_ge(delta_stored, 16 * BATCH * INNER_TILES)
            sp.wait_ge(bc_stored, 16 * BATCH)

        @block.tensor
        def _(pe):
            pe.wait_ge(const, 112)
            pe.wait_ge(diagonals, 18)
            for n, (kind, b, ct, t) in enumerate(plan):
                if n >= 8:
                    before = plan[n - 8]
                    if before[0] in on_dve:
                        pe.wait_ge(dve_taken, dve_number[before] + 1)
                    else:
                        pe.wait_ge(act_taken, act_number[before] + 1)
                cols, bank = slice(t * TW, (t + 1) * TW), ps[:, n % 8, :]
                if kind in ("inner", "gate"):
                    pe.wait_ge(image_in, 16 * (b + 1))
                    w0 = (0 if kind == "inner" else INNER_TILES * P) + ct * P
                    ins = pe.matmul(bank, wi[:, w0:w0 + P], xs[:, cols], start=True, stop=True)
                elif kind == "conv":
                    pe.wait_ge(act_taken, act_number["inner", b, ct, last] + 1)
                    for tap in range(9):
                        src = padded[:, ROWS * t + tap // 3:ROWS * t + tap // 3 + ROWS, tap % 3:tap % 3 + SIDE]
                        ins = pe.matmul(bank.rearrange("p (r c) -> p r c", c=SIDE), diag[:, ct, tap, :], src, start=(tap == 0), stop=(tap == 8))
                elif kind == "bc":
                    pe.wait_ge(act_taken, act_number["conv", b, 1, last] + 1)
                    for k in range(INNER_TILES):
                        ins = pe.matmul(bank[0:64, :], wx[:, k, 0:64], xa[:, k, cols], start=(k == 0), stop=(k == INNER_TILES - 1))
                elif kind == "rank":
                    for k in range(INNER_TILES):
                        ins = pe.matmul(bank[0:RANK, :], wx[:, k, 64:64 + RANK], xa[:, k, cols], start=(k == 0), stop=(k == INNER_TILES - 1))
                else:
                    pe.wait_ge(act_taken, act_number["rank", b, 0, last] + 1)
                    ins = pe.matmul(bank, wd[:, ct * P:(ct + 1) * P], rank[:, cols], start=True, stop=True)
                ins.then_inc(filled, 1)

        @block.scalar
        def _(act):
            act.wait_ge(const, 112)
            act.wait_ge(border, 1)
            for kind, b, ct, t in act_jobs:
                n = number[kind, b, ct, t]
                g = b * INNER_TILES + ct
                cols, bank = slice(t * TW, (t + 1) * TW), ps[:, n % 8, :]
                act.wait_ge(filled, n + 1)
                if kind == "inner":
                    if t == 0 and g:
                        act.wait_ge(filled, number["conv", (g - 1) // 2, (g - 1) % 2, last] + 1)
                    ins = act.activation(padded[:, 1 + ROWS * t:1 + ROWS * (t + 1), 1:1 + SIDE],
                                         bank.rearrange("p (r c) -> p r c", c=SIDE), ACT.Copy)
                elif kind == "gate":
                    uses = g * NTB // 4 + t // 4
                    if uses:
                        act.wait_ge(gate_stored[t % 4], 16 * uses)
                    ins = act.activation(gs[:, t % 4, :], bank, ACT.Silu)
                elif kind == "conv":
                    if t == 0 and b:
                        act.wait_ge(u_stored, 16 * b * INNER_TILES)
                        act.wait_ge(du_ok, DIRS * b * INNER_TILES)
                        act.wait_ge(filled, number["rank", b - 1, 0, last] + 1)
                    ins = act.activation(xa[:, ct, cols], bank, ACT.Silu, bias=cb[:, ct:ct + 1])
                else:
                    if t == 0 and b:
                        act.wait_ge(filled, number["step", b - 1, 1, last] + 1)
                    ins = act.activation(rank[:, cols], bank[0:RANK, :], ACT.Copy)
                ins.then_inc(act_taken, 1)
                if kind == "rank" and t == last:
                    for k in range(INNER_TILES):
                        h = b * INNER_TILES + k
                        act.wait_ge(dve_taken, dve_number["step", b, k, last] + 1)
                        if h:
                            act.wait_ge(delta_ok, h)
                        act.activation(e[:, :], s[:, :], ACT.Abs).then_inc(magnitude, 1)
                        act.wait_ge(magnitude, h + 1)
                        act.activation(e[:, :], e[:, :], ACT.Exp, scale=-1.0).then_inc(expd, 1)

        @block.vector
        def _(dve):
            chain = Chain(dve, own)
            dve.memset(padded[:, :, :], 0.0).then_inc(border, 1)
            dve.wait_ge(const, 112)
            for ct in range(INNER_TILES):
                for tap in range(9):
                    dve.tensor_scalar(diag[:, ct, tap, :], ident[:, :], cw[:, ct, tap:tap + 1], None, ALU.mult).then_inc(diagonals, 1)

            for kind, b, ct, t in dve_jobs:
                n = number[kind, b, ct, t]
                g = b * INNER_TILES + ct
                cols, bank = slice(t * TW, (t + 1) * TW), ps[:, n % 8, :]
                dve.wait_ge(filled, n + 1)
                if kind == "bc":
                    if t == 0 and b:
                        dve.wait_ge(bc_stored, 16 * b)
                    chain.link(dve.tensor_copy(bcs[:, cols], bank[0:64, :]))
                    dve.tensor_tensor(bcs[32:64, cols], bank[32:64, :], bcs[32:64, cols].bitcast(F32), ALU.subtract).then_inc(dve_taken, 1)
                else:
                    if t == 0 and g:
                        dve.wait_ge(delta_stored, 16 * g)
                        dve.wait_ge(du_ok, DIRS * g)
                    dve.tensor_scalar(s[:, cols], bank, bd[:, ct:ct + 1], None, ALU.add).then_inc(dve_taken, 1)
                    if t == last:
                        dve.wait_ge(expd, g + 1)
                        chain.link(dve.tensor_scalar(poly[:, :], e[:, :], CO[-1], None, ALU.mult))
                        for c in CO[-2::-1]:
                            chain.link(dve.scalar_tensor_tensor(poly[:, :], poly[:, :], c, e[:, :], ALU.add, ALU.mult))
                        dve.scalar_tensor_tensor(s[:, :], s[:, :], 0.0, poly[:, :], ALU.max, ALU.add).then_inc(delta_ok, 1)
                        dve.wait_ge(delta_ok, g + 1)
                        for d in range(DIRS):
                            uses = g * DIRS // 2 + d // 2
                            if uses:
                                dve.wait_ge(du_stored[d % 2], 16 * uses)
                            dve.tensor_tensor(dus[:, d % 2, :].rearrange("p (a c) -> p a c", c=SIDE),
                                              s[:, :].rearrange("p (a c) -> p a c", c=SIDE), scan_order(xa[:, ct, :], d), ALU.mult).then_inc(du_ok, 1)


def mamba_scan(nc, sems, stage, delta, du, bc, ys, a_log, pick_in, ident_in):
    UNITS = DIRS * STATES
    GROUPS = BATCH * INNER_TILES
    BACK = UNITS - 3 * STATES
    with Mem(nc, stage, sems) as m:
        dl = m.sb("delta", [P, W])
        dus = m.sb("delta_u", [P, DIRS, W])
        bcs = m.sb("bc", [64, 2, W], F32R)
        raw_pick, pick, ident = m.sb("raw_pick", [64, 32]), m.sb("pick", [64, 32], F32R), m.sb("ident", [P, P])
        al, exp_al = m.sb("a_log", [P, INNER_TILES, STATES]), m.sb("exp_a_log", [P, INNER_TILES, STATES])
        a = m.sb("a", [P, STATES])
        decay, c = m.sb("decay", [P, STATES, W]), m.sb("c", [P, STATES, W])
        h, ch = m.sb("h", [P, 4, W]), m.sb("c_h", [P, 4, W])
        state = m.sb("state", [P, UNITS])
        yo = m.sb("y", [P, W])
        b_ps, c_ps, y_ps = m.ps("b", [P, 2, W]), m.ps("c", [P, W]), m.ps("y", [P, W])
        const, pick_ok, exp_a, a_ok = m.sem("const"), m.sem("pick_ok"), m.sem("exp_a"), m.sem("a_ok")
        delta_in, du_in = m.sem("delta_in"), [m.sem(f"du_in{d}") for d in range(DIRS)]
        bc_in = [m.sem("bc_in0"), m.sem("bc_in1")]
        b_filled, driven, scanned = m.sem("b_filled"), m.sem("driven"), m.sem("scanned")
        c_filled, c_ok, decay_ok, kept = m.sem("c_filled"), m.sem("c_ok"), m.sem("decay_ok"), m.sem("kept")
        weighed, summed, y_taken, stored = m.sem("weighed"), m.sem("summed"), m.sem("y_taken"), m.sem("stored")
        held = m.sem("held")
        block = m.block()

        def scanned_at(u0, u): return u0 + (u + 1 + BACK)
        def weighed_at(u0, u): return u0 + (u + 1 + BACK)
        def driven_at(u0, u): return u0 + (u + 1 + UNITS)
        def kept_at(u0, u): return u0 + (u + 1 + UNITS)
        def summed_at(u0, u): return u0 + (u + 1 + 4)

        @block.sync
        def _(sp):
            for dst, src in ((raw_pick, pick_in), (ident, ident_in), (al, a_log)):
                sp.dma_start(dst[:], src).then_inc(const, 16)
            with sp.Fori(0, BATCH) as b:
                for ct in range(INNER_TILES):
                    for q in range(CHUNKS):
                        g = b * INNER_TILES + ct
                        it = g * CHUNKS + q
                        u0 = it * UNITS
                        sp.wait_ge(decay_ok, it * STATES + 1)
                        sp.dma_start(dl[:, :], delta[bass.ds(g, 1), q].rearrange("a p t -> (a p) t")).then_inc(delta_in, 16)
                        sp.dma_start(bcs[:, q % 2, :].bitcast(F32), bc[bass.ds(b, 1), q].rearrange("a p t -> (a p) t")).then_inc(bc_in[q % 2], 16)
                        for d in range(DIRS):
                            sp.wait_ge(driven, driven_at(u0, d * STATES + STATES - 1 - UNITS))
                            sp.dma_start(dus[:, d, :], du[bass.ds(g, 1), q, d].rearrange("a p t -> (a p) t")).then_inc(du_in[d], 16)

        @block.tensor
        def _(pe):
            pe.sem_inc(summed, 4)
            pe.wait_ge(const, 48)
            pe.wait_ge(pick_ok, 1)
            with pe.Fori(0, GROUPS * CHUNKS // 2) as pair:
                for q in range(2):
                    it = pair * 2 + q
                    u0 = it * UNITS

                    def spread(dst, row):
                        ones = pick[:, row:row + 1].to_broadcast((64, P))
                        for k in range(2):
                            ins = pe.matmul(dst[:, k * TW:(k + 1) * TW], ones, bcs[:, q, k * TW:(k + 1) * TW], start=True, stop=True)
                        return ins

                    def spread_b(u):
                        pe.wait_ge(scanned, scanned_at(u0, u - 2))
                        spread(b_ps[:, u % 2, :], u % STATES).then_inc(b_filled, 1)

                    def spread_c(n):
                        pe.wait_ge(c_ok, it * STATES + (n + 1))
                        spread(c_ps, STATES + n).then_inc(c_filled, 1)

                    def add_up(u):
                        pe.wait_ge(weighed, weighed_at(u0, u))
                        if u % STATES == 0:
                            pe.wait_ge(y_taken, it * DIRS + (u // STATES + 1))
                        for k in range(2):
                            ins = pe.matmul(y_ps[:, k * TW:(k + 1) * TW], ident[:, :], ch[:, u % 4, k * TW:(k + 1) * TW],
                                            start=(u % STATES == 0), stop=(u % STATES == STATES - 1))
                        ins.then_inc(summed, 1)

                    pe.wait_ge(bc_in[q], pair * 16 + 16)
                    spread_b(0)
                    spread_c(0)
                    spread_b(1)
                    spread_c(1)
                    for u in range(0, UNITS, 2):
                        for v in (u + 2, u + 3):
                            if v < UNITS:
                                spread_b(v)
                            if v < STATES:
                                spread_c(v)
                        for v in (u - 2, u - 1):
                            if v >= 0:
                                add_up(v)
                    add_up(UNITS - 2)
                    add_up(UNITS - 1)

        @block.scalar
        def _(act):
            for s, credits in ((c_ok, 1), (y_taken, 1), (kept, UNITS), (decay_ok, 1), (stored, 16)):
                act.sem_inc(s, credits)
            act.wait_ge(held, 1)
            act.activation(exp_al[:, :, :], al[:, :, :], ACT.Exp).then_inc(exp_a, 1)
            act.wait_ge(exp_a, 1)
            with act.Fori(0, BATCH) as b:
                for ct in range(INNER_TILES):
                    g = b * INNER_TILES + ct
                    act.wait_ge(decay_ok, g * (CHUNKS * STATES) + 1)
                    act.activation(a[:, :], exp_al[:, ct, :], ACT.Copy, scale=-1.0).then_inc(a_ok, 1)
                    with act.Fori(0, CHUNKS) as q:
                        it = g * CHUNKS + q
                        u0 = it * UNITS

                        def make_decay(n):
                            if n == 0:
                                act.wait_ge(delta_in, it * 16 + 16)
                                act.wait_ge(a_ok, g + 1)
                            act.wait_ge(scanned, scanned_at(u0, 3 * STATES + n - UNITS))
                            act.activation(decay[:, n, :], dl[:, :], ACT.Exp, scale=a[:, n:n + 1]).then_inc(decay_ok, 1)

                        def copy_c(n):
                            act.wait_ge(c_filled, it * STATES + (n + 1))
                            act.wait_ge(weighed, weighed_at(u0, 3 * STATES + n - UNITS))
                            act.activation(c[:, n, :], c_ps[:, :], ACT.Copy).then_inc(c_ok, 1)

                        for n in range(2):
                            make_decay(n)
                            copy_c(n)
                        for u in range(UNITS):
                            d, n = u // STATES, u % STATES
                            if u + 2 < STATES:
                                make_decay(u + 2)
                                copy_c(u + 2)
                            act.wait_ge(scanned, scanned_at(u0, u))
                            act.activation(state[:, u:u + 1], h[:, u % 4, W - 1:W], ACT.Copy).then_inc(kept, 1)
                            if n == STATES - 1:
                                act.wait_ge(summed, summed_at(u0, u))
                                act.wait_ge(stored, it * 64 + (16 * d + 16))
                                act.activation(yo[:, :], y_ps[:, :], ACT.Copy).then_inc(y_taken, 1)
                                act.wait_ge(y_taken, it * DIRS + (d + 2))
                                act.dma_start(ys[bass.ds(it, 1), d].rearrange("a p t -> (a p) t"), yo[:, :]).then_inc(stored, 16)
            act.wait_ge(stored, 16 * DIRS * CHUNKS * GROUPS + 16)

        @block.vector
        def _(dve):
            dve.sem_inc(scanned, BACK)
            dve.sem_inc(driven, UNITS)
            dve.wait_ge(const, 48)
            dve.tensor_copy(pick[:, :], raw_pick[:, :]).then_inc(pick_ok, 1)
            dve.tensor_scalar(al[:, :, :], al[:, :, :], 80.0, None, ALU.min).then_inc(held, 1)
            with dve.Fori(0, GROUPS) as g:
                for q in range(CHUNKS):
                    it = g * CHUNKS + q
                    u0 = it * UNITS

                    def drive(u):
                        dve.wait_ge(b_filled, u0 + (u + 1))
                        if u % STATES == 0:
                            dve.wait_ge(du_in[u // STATES], it * 16 + 16)
                        both = b_ps[:, u % 2, :]
                        dve.tensor_tensor(both, both, dus[:, u // STATES, :], ALU.mult).then_inc(driven, 1)

                    def scan(u):
                        dve.wait_ge(driven, driven_at(u0, u))
                        if u < STATES:
                            dve.wait_ge(decay_ok, it * STATES + (u + 2))
                        dve.wait_ge(weighed, weighed_at(u0, u - 4))
                        dve.wait_ge(kept, kept_at(u0, u - 4))
                        dve.tensor_tensor_scan(h[:, u % 4, :], decay[:, u % STATES, :], b_ps[:, u % 2, :],
                                               state[:, u:u + 1] if q else 0.0, ALU.mult, ALU.add).then_inc(scanned, 1)

                    for u in range(0, UNITS, 2):
                        drive(u)
                        drive(u + 1)
                        scan(u)
                        scan(u + 1)

        @block.gpsimd
        def _(pool):
            pool.sem_inc(weighed, BACK)
            with pool.Fori(0, GROUPS * CHUNKS) as it:
                u0 = it * UNITS
                for u in range(UNITS):
                    pool.wait_ge(scanned, scanned_at(u0, u))
                    if u < STATES:
                        pool.wait_ge(c_ok, it * STATES + (u + 2))
                    pool.wait_ge(summed, summed_at(u0, u - 4))
                    pool.tensor_tensor(ch[:, u % 4, :], h[:, u % 4, :], c[:, u % STATES, :], ALU.mult).then_inc(weighed, 1)


def mamba_finish(nc, sems, stage, x, x_out, ys, u_img, gates, d_param, ln_w, ln_b, w_out, inner_mean, eps):
    with Mem(nc, stage, sems) as m:
        yd, acc = m.sb("direction", [P, 2, L]), m.sb("acc", [P, INNER_TILES, L])
        xs = m.sb("x", [P, L])
        gs = m.sb("gate", [P, 2, INNER_TILES, TW])
        sq = m.sb("square", [P, 2, INNER_TILES, TW])
        dp, d4 = m.sb("d", [P, INNER_TILES]), m.sb("four_d", [P, INNER_TILES])
        lw, lb, wo = m.sb("ln_w", [P, INNER_TILES]), m.sb("ln_b", [P, INNER_TILES]), m.sb("w_out", [P, INNER_TILES, P])
        mean, epst = m.sb("inner_mean", [P, P]), m.sb("eps", [P, 1])
        std, rstd = m.sb("deviation", [P, 2, TW]), m.sb("reciprocal", [P, 2, TW])
        mean_ps, var_ps, out_ps = m.ps("mean", [P, 2, TW]), m.ps("variance", [P, 2, TW]), m.ps("out", [P, 2, TW])
        const, x_in, own, eps_ok = m.sem("const"), m.sem("x_in"), m.sem("own"), m.sem("eps_ok")
        part_in, part_used = [m.sem("part_in0"), m.sem("part_in1")], m.sem("part_used")
        gate_in = [m.sem("gate_in0"), m.sem("gate_in1")]
        combined, meaned, centred, squared, varied, rooted, gated, outed, added, stored = (m.sem(n) for n in (
            "combined", "meaned", "centred", "squared", "varied", "rooted", "gated", "outed", "added", "stored"))
        block = m.block()
        PARTS = DIRS + 1

        @block.sync
        def _(sp):
            for dst, src in ((dp, d_param), (lw, ln_w), (lb, ln_b), (wo, w_out), (mean, inner_mean)):
                sp.dma_start(dst[:], src).then_inc(const, 16)
            for b in range(BATCH):
                for ct in range(INNER_TILES):
                    g = b * INNER_TILES + ct
                    for d in range(PARTS):
                        k = g * PARTS + d
                        if k >= 2:
                            sp.wait_ge(part_used, k - 1)
                        src = in_chunks(u_img[b, ct]) if d == DIRS else ys[g * CHUNKS:(g + 1) * CHUNKS, d].rearrange("q p t -> p q t")
                        sp.dma_start(in_chunks(yd[:, k % 2, :]), src).then_inc(part_in[k % 2], 16)
                if b:
                    sp.wait_ge(stored, 16 * b)
                sp.dma_start(xs[:, :], x[:, b * L:(b + 1) * L]).then_inc(x_in, 16)
                for t in range(NTB):
                    n = b * NTB + t
                    if n >= 2:
                        sp.wait_ge(gated, (n - 1) * INNER_TILES)
                    sp.dma_start(gs[:, n % 2, :, :], gates[b, :, :, t * TW:(t + 1) * TW].rearrange("c p t -> p c t")).then_inc(gate_in[n % 2], 16)
                sp.wait_ge(added, NTB * (b + 1))
                sp.dma_start(x_out[:, b * L:(b + 1) * L], xs[:, :]).then_inc(stored, 16)
            sp.wait_ge(stored, 16 * BATCH)

        @block.tensor
        def _(pe):
            pe.wait_ge(const, 80)
            for b in range(BATCH):
                pe.wait_ge(combined, INNER_TILES * (b + 1))
                for t in range(NTB):
                    n = b * NTB + t
                    cols = slice(t * TW, (t + 1) * TW)
                    if n >= 2:
                        pe.wait_ge(centred, (n - 1) * INNER_TILES)
                    for ct in range(INNER_TILES):
                        ins = pe.matmul(mean_ps[:, n % 2, :], mean[:, :], acc[:, ct, cols], start=(ct == 0), stop=(ct == INNER_TILES - 1))
                    ins.then_inc(meaned, 1)
                    pe.wait_ge(squared, (n + 1) * INNER_TILES)
                    if n >= 2:
                        pe.wait_ge(rooted, n - 1)
                    for ct in range(INNER_TILES):
                        ins = pe.matmul(var_ps[:, n % 2, :], mean[:, :], sq[:, n % 2, ct, :], start=(ct == 0), stop=(ct == INNER_TILES - 1))
                    ins.then_inc(varied, 1)
                    pe.wait_ge(gated, (n + 1) * INNER_TILES)
                    if n >= 2:
                        pe.wait_ge(added, n - 1)
                    for ct in range(INNER_TILES):
                        ins = pe.matmul(out_ps[:, n % 2, :], wo[:, ct, :], acc[:, ct, cols], start=(ct == 0), stop=(ct == INNER_TILES - 1))
                    ins.then_inc(outed, 1)

        @block.scalar
        def _(act):
            act.wait_ge(eps_ok, 1)
            for n in range(NT):
                t = n % NTB
                if n >= 2:
                    act.wait_ge(varied, n - 1)
                for ct in range(INNER_TILES):
                    act.wait_ge(centred, n * INNER_TILES + ct + 1)
                    act.activation(sq[:, n % 2, ct, :], acc[:, ct, t * TW:(t + 1) * TW], ACT.Square).then_inc(squared, 1)
                act.wait_ge(varied, n + 1)
                act.activation(std[:, n % 2, :], var_ps[:, n % 2, :], ACT.Sqrt, bias=epst[:, :]).then_inc(rooted, 1)

        @block.vector
        def _(dve):
            chain = Chain(dve, own)
            dve.memset(epst[:, :], eps).then_inc(eps_ok, 1)
            dve.wait_ge(const, 80)
            chain.link(dve.tensor_scalar(d4[:, :], dp[:, :], float(DIRS), None, ALU.mult))
            for b in range(BATCH):
                for ct in range(INNER_TILES):
                    g = b * INNER_TILES + ct
                    image = acc[:, ct, :].rearrange("p (a c) -> p a c", c=SIDE)
                    for d in range(PARTS):
                        k = g * PARTS + d
                        if d == 0 and b:
                            dve.wait_ge(outed, NTB * b)
                        dve.wait_ge(part_in[k % 2], 16 * (k // 2 + 1))
                        part = yd[:, k % 2, :]
                        if d == 0:
                            ins = dve.tensor_copy(acc[:, ct, :], part)
                        elif d < DIRS:
                            ins = dve.tensor_tensor(image, image, scan_order(part, d), ALU.add)
                        else:
                            ins = dve.scalar_tensor_tensor(acc[:, ct, :], part, d4[:, ct:ct + 1], acc[:, ct, :], ALU.mult, ALU.add)
                        ins.then_inc(part_used, 1)
                        dve.wait_ge(part_used, k + 1)
                    dve.sem_inc(combined, 1)
                for t in range(NTB):
                    n = b * NTB + t
                    cols = slice(t * TW, (t + 1) * TW)
                    dve.wait_ge(meaned, n + 1)
                    for ct in range(INNER_TILES):
                        dve.tensor_tensor(acc[:, ct, cols], acc[:, ct, cols], mean_ps[:, n % 2, :], ALU.subtract).then_inc(centred, 1)
                    dve.wait_ge(rooted, n + 1)
                    chain.link(dve.reciprocal(rstd[:, n % 2, :], std[:, n % 2, :]))
                    dve.wait_ge(squared, (n + 1) * INNER_TILES)
                    for ct in range(INNER_TILES):
                        v = acc[:, ct, cols]
                        chain.link(dve.scalar_tensor_tensor(v, v, lw[:, ct:ct + 1], rstd[:, n % 2, :], ALU.mult, ALU.mult))
                        if ct == 0:
                            dve.wait_ge(gate_in[n % 2], 16 * (n // 2 + 1))
                        dve.scalar_tensor_tensor(v, v, lb[:, ct:ct + 1], gs[:, n % 2, ct, :], ALU.add, ALU.mult).then_inc(gated, 1)
                    dve.wait_ge(outed, n + 1)
                    if t == 0:
                        dve.wait_ge(x_in, 16 * (b + 1))
                    dve.tensor_tensor(xs[:, cols], out_ps[:, n % 2, :], xs[:, cols], ALU.add).then_inc(added, 1)
def full_attention(nc, sems, stage, xn, x, x_out, wq, wk, wv, ident_in, first_in):
    SCALE = float(P) ** -0.5
    LINKS = 2 * NTB + 1
    IT_JOBS = 3 * NTB + NTB
    with Mem(nc, stage, sems) as m:
        xs = m.sb("xn", [P, L])
        w = m.sb("w", [P, 3, P])
        ident, ones = m.sb("ident", [P, P]), m.sb("ones", [P, P])
        raw_first, first = m.sb("raw_first", [P, P]), m.sb("first", [P, P], F32R)
        qh, ql = m.sb("q_high", [P, L], F32R), m.sb("q_low", [P, L], F32R)
        kh, kl = m.sb("k_high", [P, L], F32R), m.sb("k_low", [P, L], F32R)
        v = m.sb("v", [P, KT, P])
        mx2, mx = m.sb("max_halves", [P, KT, 2]), m.sb("max", [P, KT])
        mxw = m.sb("max_wide", [P, KT, P])
        shift = m.sb("shift", [P, L], F32R)
        pt = m.sb("probs", [P, 4, TW])
        acc = m.sb("probs_sum", [P, TW])
        inv, res, o = m.sb("inverse", [P, TW]), m.sb("x", [P, 2, TW]), m.sb("out", [P, 2, TW])
        ps = m.ps("all", [P, 8, TW])
        const, first_ok, ones_ok, entered = m.sem("const"), m.sem("first_ok"), m.sem("ones_ok"), m.sem("entered")
        image_in, filled, taken, own = m.sem("image_in"), m.sem("filled"), m.sem("taken"), m.sem("own")
        max_filled, max_taken, wide_ok = m.sem("max_filled"), m.sem("max_taken"), m.sem("wide_ok")
        scored, expd, weighed, added = m.sem("scored"), m.sem("expd"), m.sem("weighed"), m.sem("added")
        summed, inverted, scaled, done = m.sem("summed"), m.sem("inverted"), m.sem("scaled"), m.sem("done")
        stored = [m.sem("stored0"), m.sem("stored1")]
        res_in = [m.sem("res_in0"), m.sem("res_in1")]
        block = m.block()

        def f(ap):
            return ap.bitcast(F32)

        @block.sync
        def _(sp):
            for s in stored:
                sp.sem_inc(s, 16)
            for n, src in enumerate((wq, wk, wv)):
                sp.dma_start(w[:, n, :], src).then_inc(const, 16)
            sp.dma_start(ident[:, :], ident_in).then_inc(const, 16)
            sp.dma_start(raw_first[:, :], first_in).then_inc(const, 16)
            with sp.Fori(0, BATCH) as b:
                sp.wait_ge(filled, b * IT_JOBS + 1)
                sp.dma_start(xs[:, :], xn[:, bass.ts(b, L)]).then_inc(image_in, 16)
                for j in range(NTB):
                    tokens = bass.ds(b * L + j * TW, TW)
                    sp.wait_ge(done, b * NTB + j + 1 if j < 2 else b * NTB + j)
                    sp.dma_start(res[:, j % 2, :], x[:, tokens]).then_inc(res_in[j % 2], 16)
                    sp.wait_ge(done, b * NTB + j + 2)
                    sp.dma_start(x_out[:, tokens], o[:, j % 2, :]).then_inc(stored[j % 2], 16)
            for s in stored:
                sp.wait_ge(s, 8 * NTB * BATCH + 16)

        @block.tensor
        def _(pe):
            pe.sem_inc(filled, 1)
            pe.sem_inc(summed, 1)
            pe.wait_ge(const, 80)
            pe.wait_ge(first_ok, 1)
            pe.wait_ge(ones_ok, 1)
            with pe.Fori(0, BATCH) as it:
                job0 = it * IT_JOBS + 1
                pe.wait_ge(image_in, it * 16 + 16)
                n = 0
                for part in range(3):
                    for t in range(NTB):
                        if n >= 4:
                            pe.wait_ge(taken, job0 + (n - 3))
                        if part < 2:
                            ins = pe.matmul(ps[:, n % 4, :], w[:, part, :], xs[:, t * TW:(t + 1) * TW], start=True, stop=True)
                        else:
                            for k in range(4):
                                tok = (4 * t + k) * P
                                ins = pe.matmul(ps[:, n % 4, k * P:(k + 1) * P], xs[:, tok:tok + P], w[:, 2, :], start=True, stop=True)
                        ins.then_inc(filled, 1)
                        n += 1
                pe.wait_ge(taken, job0 + n)
                for t in range(KT):
                    for half in range(2):
                        k = 2 * t + half
                        if k >= 2:
                            pe.wait_ge(max_taken, it * 2 * KT + (k - 1))
                        for c in range(4):
                            keys = slice((4 * half + c) * TW, (4 * half + c + 1) * TW)
                            ins = pe.matmul(ps[:, 4 * half + c, :], qh[:, t * P:(t + 1) * P], kh[:, keys], start=True, stop=True)
                        ins.then_inc(max_filled, 1)
                pe.wait_ge(wide_ok, it + 1)
                for t in range(NTB):
                    for k in range(4):
                        ins = pe.matmul(ps[:, t, k * P:(k + 1) * P], mxw[:, 4 * t + k, :], ident[:, :], start=True, stop=True)
                    ins.then_inc(filled, 1)
                    n += 1
                pe.wait_ge(taken, job0 + n)
                pe.sem_inc(entered, 1)
                with pe.Fori(0, NTB // 2) as jj:
                    for par in range(2):
                        row = it * NTB + jj * 2 + par
                        tile0 = row * KT
                        queries = bass.ds(jj * 2 * TW + par * TW, TW)

                        def score(i):
                            if i >= 4:
                                pe.wait_ge(expd, tile0 + (i - 3))
                            o_, keys = ps[:, i % 4, :], slice(i * P, (i + 1) * P)
                            pe.matmul(o_, first[:, :], shift[:, queries], start=True, stop=False)
                            pe.matmul(o_, kh[:, keys], qh[:, queries], start=False, stop=False)
                            pe.matmul(o_, kh[:, keys], ql[:, queries], start=False, stop=False)
                            pe.matmul(o_, kl[:, keys], qh[:, queries], start=False, stop=True).then_inc(scored, 1)

                        for i in range(3):
                            score(i)
                        pe.wait_ge(scaled, row + 1)
                        for i in range(KT):
                            if i + 3 < KT:
                                score(i + 3)
                            pe.wait_ge(expd, tile0 + (i + 1))
                            pe.matmul(ps[:, 4 + par, :], v[:, i, :], pt[:, i % 4, :], start=(i == 0), stop=(i == KT - 1)).then_inc(weighed, 1)
                        pe.wait_ge(added, tile0 + KT)
                        pe.matmul(ps[:, 6 + par, :], ones[:, :], acc[:, :], start=True, stop=True).then_inc(summed, 1)

        @block.scalar
        def _(act):
            with act.Fori(0, BATCH * NTB) as row:
                for i in range(KT):
                    act.wait_ge(scored, row * KT + (i + 1))
                    if i >= 4:
                        act.wait_ge(weighed, row * KT + (i - 3))
                        act.wait_ge(added, row * KT + (i - 3))
                    act.activation(pt[:, i % 4, :], ps[:, i % 4, :], ACT.Exp).then_inc(expd, 1)

        @block.vector
        def _(dve):
            for s in (taken, scaled, done):
                dve.sem_inc(s, 1)
            dve.memset(ones[:, :], 1.0).then_inc(ones_ok, 1)
            dve.wait_ge(const, 80)
            dve.tensor_copy(first[:, :], raw_first[:, :]).then_inc(first_ok, 1)
            with dve.Fori(0, BATCH) as it:
                job0 = it * IT_JOBS + 1
                link0 = it * LINKS
                links = 0

                def link(ins):
                    nonlocal links
                    links += 1
                    ins.then_inc(own, 1)
                    dve.wait_ge(own, link0 + links)

                n = 0
                for high, low, scale in ((qh, ql, 1.0), (kh, kl, SCALE)):
                    for t in range(NTB):
                        dve.wait_ge(filled, job0 + (n + 1))
                        cols, bank = slice(t * TW, (t + 1) * TW), n % 4
                        link(dve.tensor_scalar(high[:, cols], ps[:, bank, :], scale, None, ALU.mult))
                        dve.scalar_tensor_tensor(low[:, cols], ps[:, bank, :], scale, f(high[:, cols]), ALU.mult, ALU.subtract).then_inc(taken, 1)
                        n += 1
                for t in range(NTB):
                    dve.wait_ge(filled, job0 + (n + 1))
                    dve.tensor_copy(v[:, 4 * t:4 * t + 4, :], ps[:, n % 4, :].rearrange("p (t d) -> p t d", d=P)).then_inc(taken, 1)
                    n += 1
                for k in range(2 * KT):
                    dve.wait_ge(max_filled, it * 2 * KT + (k + 1))
                    half = k % 2
                    dve.tensor_reduce(mx2[:, k // 2, half:half + 1], ps[:, 4 * half:4 * half + 4, :], AX.XY, ALU.max).then_inc(max_taken, 1)
                dve.wait_ge(max_taken, it * 2 * KT + 2 * KT)
                link(dve.tensor_reduce(mx[:, :], mx2[:, :, :], AX.X, ALU.max))
                dve.tensor_copy(mxw[:, :, :], mx[:, :].rearrange("p (t a) -> p t a", a=1).to_broadcast((P, KT, P))).then_inc(wide_ok, 1)
                for t in range(NTB):
                    dve.wait_ge(filled, job0 + (n + 1))
                    dve.tensor_scalar(shift[:, t * TW:(t + 1) * TW], ps[:, t, :], -1.0, None, ALU.mult).then_inc(taken, 1)
                    n += 1
                assert links == LINKS and n == IT_JOBS
                for j in range(NTB):
                    row, par = it * NTB + j, j % 2
                    for i in range(KT):
                        dve.wait_ge(expd, row * KT + (i + 1))
                        if i == 0:
                            dve.wait_ge(summed, row + 1)
                            ins = dve.tensor_copy(acc[:, :], pt[:, 0, :])
                        else:
                            dve.wait_ge(added, row * KT + i)
                            ins = dve.tensor_tensor(acc[:, :], acc[:, :], pt[:, i % 4, :], ALU.add)
                        ins.then_inc(added, 1)
                    dve.wait_ge(summed, row + 2)
                    dve.reciprocal(inv[:, :], ps[:, 6 + par, :]).then_inc(inverted, 1)
                    dve.wait_ge(inverted, row + 1)
                    dve.wait_ge(stored[par], 8 * NTB * it + 16 * (j // 2 + 1))
                    dve.tensor_tensor(o[:, par, :], ps[:, 4 + par, :], inv[:, :], ALU.mult).then_inc(scaled, 1)
                    dve.wait_ge(scaled, row + 2)
                    dve.wait_ge(res_in[par], 8 * NTB * it + 16 * (j // 2 + 1))
                    dve.tensor_tensor(o[:, par, :], o[:, par, :], res[:, par, :], ALU.add).then_inc(done, 1)
RANGES = 4


def spectral_prepare(nc, sems, stage, xn, x, y0, u_tok, scales, logits_in, gumbel_in, sigma_in, m_u, ident_in, exchange_in, rank_in):
    TAPS, K = 3, 16
    with Mem(nc, stage, sems) as m:
        pad = TAPS - 1
        xs = m.sb("xn", [P, BATCH, L + pad])
        y = m.sb("y", [P, TOK])
        ident, mu, mr = m.sb("ident", [P, P]), m.sb("m_u", [P, 4, TAPS * P]), m.sb("m_range", [P, RANGES, TAPS * P])
        ut, exchange = m.sb("u_tok", [P, TOK]), m.sb("exchange", [P, P])
        flipped, reversed_ok = m.sem("flipped"), m.sem("reversed_ok")
        z, e4, soft, hard, key, rank = (m.sb(n, [P, 4]) for n in ("logits", "exp", "soft", "hard", "key", "rank"))
        g4, sg, sc = m.sb("gumbel", [P, 4]), m.sb("sigma", [P, K]), m.sb("scales", [P, K + 1, 4])
        root, root2 = m.sb("root", [P, K]), m.sb("root_of_root", [P, K])
        tr_ps, ar_ps = m.ps("turned", [P, 4, TW]), m.ps("auto", [P, 2, TW])
        loaded, padded, own, own_act = m.sem("loaded"), m.sem("padded"), m.sem("own"), m.sem("own_act")
        shifted, expd, rooted = m.sem("shifted"), m.sem("expd"), m.sem("rooted")
        turned, copied, ranged, auto, added, stored, scales_ok = (
            m.sem(n) for n in ("turned", "copied", "ranged", "auto", "added", "stored", "scales_ok"))
        block = m.block()
        LOADS = 16 * 10

        @block.sync
        def _(sp):
            for dst, src in ((ident, ident_in), (exchange, exchange_in), (mu, m_u), (z, logits_in), (g4, gumbel_in), (sg, sigma_in), (rank, rank_in), (y, x)):
                sp.dma_start(dst[:], src).then_inc(loaded, 16)
            for b in range(BATCH):
                sp.dma_start(xs[:, b, pad:], xn[:, b * L:(b + 1) * L]).then_inc(loaded, 16)
            sp.wait_ge(reversed_ok, NT)
            sp.dma_start(u_tok, ut[:, :]).then_inc(stored, 16)
            sp.wait_ge(scales_ok, 1)
            sp.dma_start(scales, sc[:, :, :]).then_inc(stored, 16)
            sp.wait_ge(added, NT)
            sp.dma_start(y0, y[:, :]).then_inc(stored, 16)
            sp.wait_ge(stored, 48)

        @block.tensor
        def _(pe):
            pe.wait_ge(loaded, LOADS)
            for t in range(NT):
                if t >= 4:
                    pe.wait_ge(copied, t - 3)
                for k in range(4):
                    n = 4 * t + k
                    b, par, j = n // 32, n // 16 % 2, n % 16
                    first = pad + 2 * P * j + par
                    ins = pe.matmul(tr_ps[:, t % 4, k * P:(k + 1) * P], xs[:, b, first:first + 2 * P - 1:2], ident[:, :], start=True, stop=True)
                ins.then_inc(turned, 1)
            for t in range(NT):
                pe.wait_ge(copied, t + 1)
                if t >= 2:
                    pe.wait_ge(reversed_ok, t - 1)
                pe.matmul(ar_ps[:, t % 2, :], exchange[:, :], ut[:, t * TW:(t + 1) * TW], start=True, stop=True).then_inc(flipped, 1)
            pe.wait_ge(reversed_ok, NT)
            pe.wait_ge(ranged, 1)
            pe.wait_ge(padded, 1)
            for t in range(NT):
                b, tile = t // NTB, t % NTB
                r = (0, 1, 2, 2, 3, 3, 3, 3)[tile]
                if t >= 2:
                    pe.wait_ge(added, t - 1)
                for tap in range(TAPS):
                    first = pad + tile * TW - tap
                    ins = pe.matmul(ar_ps[:, t % 2, :], mr[:, r, tap * P:(tap + 1) * P], xs[:, b, first:first + TW],
                                    start=(tap == 0), stop=(tap == TAPS - 1))
                ins.then_inc(auto, 1)

        @block.scalar
        def _(act):
            act.wait_ge(loaded, LOADS)
            act.activation(root[:, :], sg[:, :], ACT.Sqrt).then_inc(own_act, 1)
            act.wait_ge(own_act, 1)
            act.activation(root2[:, :], root[:, :], ACT.Sqrt).then_inc(rooted, 1)
            act.wait_ge(shifted, 1)
            act.activation(e4[:, :], z[:, :], ACT.Exp).then_inc(expd, 1)

        @block.vector
        def _(dve):
            chain = Chain(dve, own)
            dve.memset(xs[:, :, 0:pad], 0.0).then_inc(padded, 1)
            dve.wait_ge(loaded, LOADS)
            chain.link(dve.tensor_tensor(z[:, :], z[:, :], g4[:, :], ALU.add))
            chain.link(dve.tensor_reduce(key[:, 0:1], z[:, :], AX.X, ALU.max))
            dve.tensor_scalar(z[:, :], z[:, :], key[:, 0:1], None, ALU.subtract).then_inc(shifted, 1)
            dve.wait_ge(expd, 1)
            chain.link(dve.tensor_reduce(key[:, 0:1], e4[:, :], AX.X, ALU.add))
            chain.link(dve.reciprocal(key[:, 1:2], key[:, 0:1]))
            chain.link(dve.tensor_scalar(soft[:, :], e4[:, :], key[:, 1:2], None, ALU.mult))
            chain.link(dve.tensor_reduce(g4[:, 0:1], soft[:, :], AX.X, ALU.max))
            chain.link(dve.tensor_scalar(hard[:, :], soft[:, :], g4[:, 0:1], None, ALU.is_equal))
            chain.link(dve.tensor_tensor(key[:, :], hard[:, :], rank[:, :], ALU.mult))
            chain.link(dve.tensor_reduce(g4[:, 1:2], key[:, :], AX.X, ALU.max))
            chain.link(dve.tensor_scalar(hard[:, :], key[:, :], g4[:, 1:2], None, ALU.is_equal))
            chain.link(dve.tensor_tensor(hard[:, :], hard[:, :], soft[:, :], ALU.subtract))
            chain.link(dve.tensor_tensor(sc[:, K, :], hard[:, :], soft[:, :], ALU.add))
            dve.wait_ge(rooted, 1)
            for i in range(4):
                chain.step(dve.tensor_scalar(sc[:, 0:K, i], root2[:, :], sc[:, K, i:i + 1], None, ALU.mult))
            chain.done()
            dve.sem_inc(scales_ok, 1)
            chain.link(dve.tensor_scalar(mr[:, 3, :], mu[:, 0, :], sc[:, K, 0:1], None, ALU.mult))
            for i in range(1, 4):
                ins = dve.scalar_tensor_tensor(mr[:, 3 - i, :], mu[:, i, :], sc[:, K, i:i + 1], mr[:, 4 - i, :], ALU.mult, ALU.add)
                if i < 3:
                    chain.link(ins)
            ins.then_inc(ranged, 1)
            for t in range(NT):
                dve.wait_ge(turned, t + 1)
                dve.tensor_copy(ut[:, t * TW:(t + 1) * TW], tr_ps[:, t % 4, :]).then_inc(copied, 1)
            for t in range(NT):
                dve.wait_ge(flipped, t + 1)
                dve.tensor_copy(ut[:, t * TW:(t + 1) * TW], ar_ps[:, t % 2, :]).then_inc(reversed_ok, 1)
            for t in range(NT):
                dve.wait_ge(auto, t + 1)
                part = y[:, t * TW:(t + 1) * TW]
                dve.tensor_tensor(part, ar_ps[:, t % 2, :], part, ALU.add).then_inc(added, 1)


def spectral(nc, sems, stage, u_tok, y0, y_out, scales_in, phi, m_phi):
    K, HALF = 16, L // 2
    CHUNKS, BLOCKS = HALF // TW, HALF // P
    ODD = HALF
    WIDTH = 2 * HALF + 1
    YJOBS = BATCH * CHUNKS * 2
    LINKS = 5 + 8
    with Mem(nc, stage, sems) as m:
        uh, ul = m.sb("u_high", [P, TOK], F32R), m.sb("u_low", [P, TOK], F32R)
        raw = m.sb("toeplitz", [P, WIDTH])
        th, tl = m.sb("toeplitz_high", [P, 2, WIDTH], F32R), m.sb("toeplitz_low", [P, 2, WIDTH], F32R)
        y = m.sb("y", [P, TOK])
        mraw, meff = m.sb("m_phi", [P, 2, 4 * P]), m.sb("m_range", [P, 2, RANGES, 2, P])
        pq = m.sb("sum_and_difference", [P, 4, 2, P])
        sc, sk = m.sb("scales", [P, (K + 1) * 4]), m.sb("scales_k", [P, 4])
        a = m.sb("filtered", [P, 4, TW])
        ps = m.ps("all", [P, 6, TW])
        loaded, u_in, u_split, own = m.sem("loaded"), m.sem("u_in"), m.sem("u_split"), m.sem("own")
        t_in, m_in, piece_done, matrices = m.sem("t_in"), m.sem("m_in"), m.sem("piece_done"), m.sem("matrices")
        convolved, taken, mixed, added, stored = (m.sem(n) for n in ("convolved", "taken", "mixed", "added", "stored"))
        entered = m.sem("entered")
        block = m.block()

        def f(ap):
            return ap.bitcast(F32)

        def pieces():
            return [slice(i * TW, (i + 1) * TW if i < 7 else WIDTH) for i in range(8)]

        @block.sync
        def _(sp):
            sp.dma_start(sc[:, :], scales_in).then_inc(loaded, 16)
            sp.dma_start(y[:, :], y0).then_inc(loaded, 16)
            for half in range(2):
                if half:
                    sp.wait_ge(u_split, 1)
                sp.dma_start(raw[:, 0:2 * HALF], u_tok[:, half * 2 * HALF:(half + 1) * 2 * HALF]).then_inc(u_in, 16)
            sp.wait_ge(u_split, 2)
            with sp.Fori(0, K) as k:
                sp.wait_ge(piece_done, k * 8 + 1)
                row = phi[bass.ds(k, 1), :]
                for first, count, dst in ((0, HALF, raw[:, 0:HALF]), (HALF + P, HALF + 1, raw[:, HALF:WIDTH])):
                    sp.dma_start(dst, bass.AP(row.tensor, row.offset + first, [[1, P], [1, count]])).then_inc(t_in, 16)
                sp.wait_ge(matrices, k + 1)
                sp.dma_start(mraw[:, :, :], m_phi[bass.ts(k, P), :]).then_inc(m_in, 16)
            sp.wait_ge(added, K * YJOBS + 1)
            sp.dma_start(y_out, y[:, :]).then_inc(stored, 16)
            sp.wait_ge(stored, 16)

        @block.tensor
        def _(pe):
            pe.wait_ge(u_split, 2)
            with pe.Fori(0, K // 2) as kk:
                for s in range(2):
                    k8, k1 = kk * 16 + s * 8, kk * 2 + s
                    job0, y0job = (kk * 2 + s) * 2 * YJOBS + 1, (kk * 2 + s) * YJOBS + 1
                    pe.wait_ge(piece_done, k8 + 9)

                    def conv(n):
                        b, c, par, kind = n // 16, n // 4 % 4, n // 2 % 2, n % 2
                        src = par if kind == 0 else 1 - par
                        t0 = 0 if kind == 0 else ODD + par
                        pe.wait_ge(taken, job0 + (n - 3) if n >= 4 else job0)
                        for j in range(4 * c + 4):
                            lag = TW * c - P * j
                            skip = max(0, -lag)
                            at_u = slice(((b * 2 + src) * BLOCKS + j) * P, ((b * 2 + src) * BLOCKS + j + 1) * P)
                            cols = slice(t0 + lag + skip, t0 + lag + TW)
                            o = ps[:, n % 4, skip:TW]
                            for q, (uu, tt) in enumerate(((uh, th), (uh, tl), (ul, th))):
                                ins = pe.matmul(o, uu[:, at_u], tt[:, s, cols], start=(j == 0 and q == 0), stop=(j == 4 * c + 3 and q == 2))
                        ins.then_inc(convolved, 1)

                    def mix(i):
                        b, c, par = i // 8, i // 2 % 4, i % 2
                        pe.wait_ge(taken, job0 + (2 * i + 2))
                        if i == 0:
                            pe.wait_ge(matrices, k1 + 2)
                        pe.wait_ge(added, y0job + (i - 1) if i >= 2 else y0job)
                        spans = [(0, 0, 256), (1, 256, 512)] if c == 0 else [(2 if c == 1 else 3, 0, TW)]
                        for r, lo, hi in spans:
                            for kind in range(2):
                                ins = pe.matmul(ps[:, 4 + i % 2, lo:hi], meff[:, s, r, kind, :], a[:, (2 * i + kind) % 4, lo:hi],
                                                start=(kind == 0), stop=(kind == 1))
                        ins.then_inc(mixed, 1)

                    for i in range(YJOBS + 1):
                        if i < YJOBS:
                            conv(2 * i)
                            conv(2 * i + 1)
                        if i >= 1:
                            mix(i - 1)

        @block.scalar
        def _(act):
            act.sem_inc(taken, 1)
            with act.Fori(0, K) as k:
                for n in range(2 * YJOBS):
                    act.wait_ge(convolved, k * 2 * YJOBS + (n + 1))
                    if n >= 4:
                        act.wait_ge(mixed, k * YJOBS + (n // 2 - 1))
                    act.activation(a[:, n % 4, :], ps[:, n % 4, :], ACT.Copy).then_inc(taken, 1)

        @block.vector
        def _(dve):
            for s in (piece_done, matrices, added):
                dve.sem_inc(s, 1)
            for half in range(2):
                dve.wait_ge(u_in, 16 * (half + 1))
                cols = slice(half * 2 * HALF, (half + 1) * 2 * HALF)
                dve.tensor_copy(uh[:, cols], raw[:, 0:2 * HALF]).then_inc(own, 1)
                dve.wait_ge(own, half + 1)
                dve.tensor_tensor(ul[:, cols], raw[:, 0:2 * HALF], f(uh[:, cols]), ALU.subtract).then_inc(u_split, 1)
            dve.wait_ge(loaded, 32)

            def split(k, s, i):
                cols = pieces()[i]
                if i == 0:
                    dve.wait_ge(t_in, k * 32 + 32)
                dve.tensor_copy(th[:, s, cols], raw[:, cols]).then_inc(own, 1)
                dve.wait_ge(own, k * LINKS + (3 + i))
                dve.tensor_tensor(tl[:, s, cols], raw[:, cols], f(th[:, s, cols]), ALU.subtract).then_inc(piece_done, 1)

            def combine(k, s):
                base = k * LINKS + 2 + 8
                dve.wait_ge(m_in, k * 16 + 16)
                plus = mraw[:, 0, :].rearrange("p (i e) -> p i e", e=P)
                minus = mraw[:, 1, :].rearrange("p (i e) -> p i e", e=P)
                dve.tensor_copy(sk[:, :], sc[:, bass.ts(k, 4)]).then_inc(own, 1)
                dve.tensor_tensor(pq[:, :, 0, :], plus, minus, ALU.add)
                dve.tensor_tensor(pq[:, :, 1, :], plus, minus, ALU.subtract).then_inc(own, 1)
                dve.wait_ge(own, base + 2)
                dve.tensor_scalar(meff[:, s, 3, :, :], pq[:, 0, :, :], sk[:, 0:1], None, ALU.mult).then_inc(own, 1)
                for i in range(1, 4):
                    dve.wait_ge(own, base + 2 + i)
                    ins = dve.scalar_tensor_tensor(meff[:, s, 3 - i, :, :], pq[:, i, :, :], sk[:, i:i + 1], meff[:, s, 4 - i, :, :], ALU.mult, ALU.add)
                    ins.then_inc(own if i < 3 else matrices, 1)

            def add(k, i):
                b, c, par = i // 8, i // 2 % 4, i % 2
                dve.wait_ge(mixed, k * YJOBS + (i + 1))
                part = y[:, :].rearrange("p (b a two) -> p b two a", b=BATCH, two=2)[:, b, par, c * TW:(c + 1) * TW]
                dve.tensor_tensor(part, ps[:, 4 + i % 2, :], part, ALU.add).then_inc(added, 1)

            for i in range(8):
                split(0, 0, i)
            combine(0, 0)

            def filter_sums(k, s, last):
                for i in range(YJOBS):
                    add(k, i)
                    if not last and i % 2 == 0:
                        split(k + 1, 1 - s, i // 2)
                if not last:
                    combine(k + 1, 1 - s)

            with dve.Fori(0, K // 2 - 1) as kk:
                for s in range(2):
                    filter_sums(kk * 2 + s, s, False)
            filter_sums(K - 2, 0, False)
            filter_sums(K - 1, 1, True)
def linear_attention(nc, sems, stage, xn, x, x_out, wk_t, wq, wv_t, ident_in):
    H, KQ = 8, 64
    with Mem(nc, stage, sems) as m:
        xs, res = m.sb("xn", [P, TOK]), m.sb("x", [P, TOK])
        ident, wks, wvs = m.sb("ident", [P, P]), m.sb("wk", [P, H * KQ]), m.sb("wv", [P, H * P])
        wqs = m.sb("wq", [KQ, H, P])
        xt = m.sb("xn_by_token", [P, 4, P])
        gram = m.sb("gram", [P, P])
        kg = m.sb("keys_gram", [P, H * KQ])
        ktv = m.sb("ktv", [KQ, H, P])
        mix = m.sb("mix", [P, BATCH, P])
        tr_ps, gram_ps = m.ps("transposed", [P, 4, TW]), m.ps("gram", [P, TW])
        kg_ps, ktv_ps = m.ps("keys_gram", [P, TW]), m.ps("ktv", [KQ, TW])
        mix_ps = m.ps("mix", [P, TW])
        loaded, own_pe, turned, copied, grammed = (m.sem(n) for n in ("loaded", "own_pe", "turned", "copied", "grammed"))
        gram_ok, kg_done, kg_ok, ktv_done, ktv_ok, mixed, mix_ok = (
            m.sem(n) for n in ("gram_ok", "kg_done", "kg_ok", "ktv_done", "ktv_ok", "mixed", "mix_ok"))
        outed, added, stored = m.sem("outed"), m.sem("added"), m.sem("stored")
        block = m.block()

        @block.sync
        def _(sp):
            for dst, src in ((ident, ident_in), (wks, wk_t), (wvs, wv_t), (wqs, wq), (xs, xn), (res, x)):
                sp.dma_start(dst[:], src).then_inc(loaded, 16)
            for b in range(BATCH):
                sp.wait_ge(added, NTB * (b + 1))
                sp.dma_start(x_out[:, b * L:(b + 1) * L], res[:, b * L:(b + 1) * L]).then_inc(stored, 16)
            sp.wait_ge(stored, 16 * BATCH)

        @block.tensor
        def _(pe):
            pe.wait_ge(loaded, 96)
            for b in range(BATCH):
                for t in range(KT + 1):
                    n = b * KT + t
                    if t < KT:
                        if n >= 4:
                            pe.wait_ge(copied, n - 3)
                        pe.transpose(tr_ps[:, n % 4, 0:P], xs[:, b * L + t * P:b * L + (t + 1) * P], ident[:, :]).then_inc(turned, 1)
                    if t >= 1:
                        u = n - 1
                        pe.wait_ge(copied, u + 1)
                        if t == 1 and b:
                            pe.wait_ge(gram_ok, b)
                        pe.matmul(gram_ps[:, 0:P], xt[:, u % 4, :], xt[:, u % 4, :],
                                  start=(t == 1), stop=(t == KT)).then_inc(grammed, 1)
                pe.wait_ge(gram_ok, b + 1)
                pe.matmul(kg_ps[:, :], gram[:, :], wks[:, :], start=True, stop=True).then_inc(kg_done, 1)
                pe.wait_ge(kg_ok, b + 1)
                for h in range(H):
                    if h % 4 == 0 and (h or b):
                        pe.wait_ge(ktv_ok, 2 * b + h // 4)
                    pe.matmul(ktv_ps[:, (h % 4) * P:(h % 4 + 1) * P], kg[:, h * KQ:(h + 1) * KQ], wvs[:, h * P:(h + 1) * P],
                              start=True, stop=True).then_inc(ktv_done, 1)
                pe.wait_ge(ktv_ok, 2 * b + 2)
                for h in range(H):
                    pe.matmul(mix_ps[:, 0:P], wqs[:, h, :], ktv[:, h, :], start=(h == 0), stop=(h == H - 1)).then_inc(mixed, 1)
                pe.wait_ge(mix_ok, b + 1)
                for t in range(NTB):
                    n = b * NTB + t
                    pe.wait_ge(copied, KT * (b + 1))
                    if n >= 4:
                        pe.wait_ge(added, n - 3)
                    pe.matmul(tr_ps[:, n % 4, :], mix[:, b, :], xs[:, n * TW:(n + 1) * TW], start=True, stop=True).then_inc(outed, 1)
                if b + 1 < BATCH:
                    pe.wait_ge(added, NTB * (b + 1))

        @block.vector
        def _(dve):
            dve.wait_ge(loaded, 96)
            for b in range(BATCH):
                for t in range(KT):
                    n = b * KT + t
                    dve.wait_ge(turned, n + 1)
                    if n >= 4:
                        dve.wait_ge(grammed, n - 3)
                    dve.tensor_copy(xt[:, n % 4, :], tr_ps[:, n % 4, 0:P]).then_inc(copied, 1)
                dve.wait_ge(grammed, KT * (b + 1))
                dve.tensor_copy(gram[:, :], gram_ps[:, 0:P]).then_inc(gram_ok, 1)
                dve.wait_ge(kg_done, b + 1)
                dve.tensor_copy(kg[:, :], kg_ps[:, :]).then_inc(kg_ok, 1)
                for g in range(2):
                    dve.wait_ge(ktv_done, H * b + 4 * g + 4)
                    dve.tensor_copy(ktv[:, 4 * g:4 * g + 4, :], ktv_ps[:, :].rearrange("p (h e) -> p h e", e=P)).then_inc(ktv_ok, 1)
                dve.wait_ge(mixed, H * (b + 1))
                dve.tensor_copy(mix[:, b, :], mix_ps[:, 0:P]).then_inc(mix_ok, 1)
                for t in range(NTB):
                    n = b * NTB + t
                    dve.wait_ge(outed, n + 1)
                    part = res[:, n * TW:(n + 1) * TW]
                    dve.tensor_tensor(part, tr_ps[:, n % 4, :], part, ALU.add).then_inc(added, 1)


def experts(nc, sems, stage, xn, x, out, router_w, router_b, expert_w, expert_b, ident_in, rank_in):
    E, BLK = 8, TOK // P
    with Mem(nc, stage, sems) as m:
        xs, res = m.sb("xn", [P, TOK]), m.sb("x", [P, TOK])
        ident, rw, ew = m.sb("ident", [P, P]), m.sb("router_w", [P, E]), m.sb("expert_w", [P, E * P])
        eb, rb, rank = m.sb("expert_b", [1, E * P]), m.sb("router_b", [P, E]), m.sb("rank", [P, E])
        ones = m.sb("ones", [1, P])
        pr = m.sb("probs", [P, BLK, E])
        rest, hit, key, gate = (m.sb(n, [P, BLK, E]) for n in ("rest", "hit", "key", "gate"))
        top1, top2, best, tot, inv = (m.sb(n, [P, BLK, 1]) for n in ("top1", "top2", "best", "total", "inverse"))
        acc = m.sb("acc", [P, 4, P])
        lg_ps = m.ps("logits", [P, TW])
        ex_ps = m.ps("expert_out", [P, 2, 2 * TW])
        xt_ps = m.ps("x_by_token", [P, 2, TW])
        loaded, own, own_act = m.sem("loaded"), m.sem("own"), m.sem("own_act")
        logits, gated, shifted, expd, mixed, turned, accd, stored = (
            m.sem(n) for n in ("logits", "gated", "shifted", "expd", "mixed", "turned", "accd", "stored"))
        chain_acc, one_set = m.sem("chain_acc"), m.sem("one_set")
        slot_stored = [m.sem(f"slot_stored{i}") for i in range(4)]
        block = m.block()

        @block.sync
        def _(sp):
            loads = ((ident, ident_in), (rw, router_w), (ew, expert_w), (eb, expert_b), (rb, router_b),
                     (rank, rank_in), (xs, xn), (res, x))
            for dst, src in loads:
                sp.dma_start(dst[:], src).then_inc(loaded, 16)
            for t in range(BLK):
                sp.wait_ge(accd, t + 1)
                sp.dma_start(out[t * P:(t + 1) * P, :], acc[:, t % 4, :]).then_inc(slot_stored[t % 4], 16)
            for i in range(4):
                sp.wait_ge(slot_stored[i], 16 * BLK // 4)

        @block.tensor
        def _(pe):
            pe.wait_ge(loaded, 128)
            pe.wait_ge(one_set, 1)
            for t in range(BLK):
                ins = pe.matmul(lg_ps[:, t * E:(t + 1) * E], xs[:, t * P:(t + 1) * P], rw[:, :], start=True, stop=True)
            ins.then_inc(logits, 1)
            for t in range(BLK):
                if t >= 2:
                    pe.wait_ge(accd, t - 1)
                for half in range(2):
                    o = ex_ps[:, t % 2, half * TW:(half + 1) * TW]
                    pe.matmul(o, xs[:, t * P:(t + 1) * P], ew[:, half * TW:(half + 1) * TW], start=True, stop=False)
                    pe.matmul(o, ones[:, :], eb[:, half * TW:(half + 1) * TW], start=False, stop=True)
                pe.transpose(xt_ps[:, t % 2, 0:P], res[:, t * P:(t + 1) * P], ident[:, :]).then_inc(mixed, 1)

        @block.scalar
        def _(act):
            act.wait_ge(shifted, 1)
            act.activation(pr[:, :, :], rest[:, :, :], ACT.Exp).then_inc(expd, 1)

        @block.vector
        def _(dve):
            own_chain = Chain(dve, own)
            dve.memset(ones[:, :], 1.0).then_inc(one_set, 1)
            dve.wait_ge(loaded, 128)
            dve.wait_ge(logits, 1)

            def wide(a):
                return a[:, :, :].to_broadcast((P, BLK, E))

            lg = lg_ps[:, :].rearrange("p (t e) -> p t e", e=E)
            rbw = rb[:, :].rearrange("p (a e) -> p a e", a=1).to_broadcast((P, BLK, E))
            rkw = rank[:, :].rearrange("p (a e) -> p a e", a=1).to_broadcast((P, BLK, E))
            own_chain.link(dve.tensor_tensor(pr[:, :, :], lg, rbw, ALU.add))
            own_chain.link(dve.tensor_reduce(best[:, :, :], pr[:, :, :], AX.X, ALU.max))
            dve.tensor_tensor(rest[:, :, :], pr[:, :, :], wide(best), ALU.subtract).then_inc(shifted, 1)
            dve.wait_ge(expd, 1)
            own_chain.link(dve.tensor_copy(rest[:, :, :], pr[:, :, :]))
            for n, top in enumerate((top1, top2)):
                own_chain.link(dve.tensor_reduce(top[:, :, :], rest[:, :, :], AX.X, ALU.max))
                own_chain.link(dve.tensor_tensor(hit[:, :, :], rest[:, :, :], wide(top), ALU.is_equal))
                own_chain.link(dve.tensor_tensor(key[:, :, :], hit[:, :, :], rkw, ALU.mult))
                own_chain.link(dve.tensor_reduce(best[:, :, :], key[:, :, :], AX.X, ALU.max))
                own_chain.link(dve.tensor_tensor(hit[:, :, :], key[:, :, :], wide(best), ALU.is_equal))
                own_chain.link(dve.tensor_tensor(key[:, :, :], hit[:, :, :], wide(top), ALU.mult))
                if n == 0:
                    own_chain.link(dve.tensor_copy(gate[:, :, :], key[:, :, :]))
                    own_chain.link(dve.scalar_tensor_tensor(rest[:, :, :], hit[:, :, :], -2.0, rest[:, :, :], ALU.mult, ALU.add))
            own_chain.link(dve.tensor_tensor(gate[:, :, :], gate[:, :, :], key[:, :, :], ALU.add))
            own_chain.link(dve.tensor_tensor(tot[:, :, :], top1[:, :, :], top2[:, :, :], ALU.add))
            own_chain.link(dve.reciprocal(inv[:, :, :], tot[:, :, :]))
            own_chain.link(dve.tensor_tensor(gate[:, :, :], gate[:, :, :], wide(inv), ALU.mult))
            acc_chain = Chain(dve, chain_acc)
            for t in range(BLK):
                dve.wait_ge(mixed, t + 1)
                if t >= 4:
                    dve.wait_ge(slot_stored[t % 4], 16 * (t // 4))
                a = acc[:, t % 4, :]
                acc_chain.link(dve.tensor_copy(a, xt_ps[:, t % 2, 0:P]))
                for e in range(E):
                    ins = dve.scalar_tensor_tensor(a, ex_ps[:, t % 2, e * P:(e + 1) * P], gate[:, t, e:e + 1], a, ALU.mult, ALU.add)
                    if e < E - 1:
                        acc_chain.link(ins)
                ins.then_inc(accd, 1)
def block_layers(nc, a, out):
    def dram(name, *shape):
        return nc.dram_tensor(name, shape, F32, kind="Internal").ap()

    def act_map(name):
        return dram(name, P, TOK)

    with ExitStack() as sems:
        xn0, att = act_map("xn0"), act_map("att")
        group_norm(nc, sems, "gn0", a["x"], xn0, a["group_mean"], 1e-5)
        bias_attention(nc, sems, "l0", xn0, att, a["w_heads"], a["emb_h"], a["emb_w"], a["cells"], a["ident"], a["pick_halves"])
        x1, xn1, x2 = act_map("x1"), act_map("xn1"), act_map("x2")
        group_norm(nc, sems, "gn1", a["x"], xn1, a["group_mean"], 1e-5, addend=att, x_sum=x1)
        gates, u_img = dram("gates", BATCH, INNER_TILES, P, L), dram("u_img", BATCH, INNER_TILES, P, L)
        delta = dram("delta", BATCH * INNER_TILES, CHUNKS, P, W)
        du = dram("du", BATCH * INNER_TILES, CHUNKS, DIRS, P, W)
        bc = dram("bc", BATCH, CHUNKS, 64, W)
        ys = dram("ys", BATCH * INNER_TILES * CHUNKS, DIRS, P, W)
        mamba_prepare(nc, sems, "m1", xn1, gates, u_img, delta.rearrange("g q p t -> g p q t"),
                      du.rearrange("g q d p t -> g p q d t"), bc.rearrange("b q p t -> b p q t"), a["w_in"], a["conv_w"],
                      a["conv_b"], a["w_x"], a["w_dt"], a["b_dt"], a["ident"])
        mamba_scan(nc, sems, "m2", delta, du, bc, ys, a["a_log"], a["pick_parts"], a["ident"])
        mamba_finish(nc, sems, "m3", x1, x2, ys, u_img, gates, a["d_param"], a["ln_w"], a["ln_b"], a["w_out"],
                     a["inner_mean"], 1e-5)
        xn2, x3, xn3 = act_map("xn2"), act_map("x3"), act_map("xn3")
        layer_norm(nc, sems, "ln2", x2, xn2, a["channel_mean"], 1e-5)
        full_attention(nc, sems, "l2", xn2, x2, x3, a["w_query"], a["w_key"], a["w_value"], a["ident"], a["first"])
        layer_norm(nc, sems, "ln3", x3, xn3, a["channel_mean"], 1e-5)
        y0, u_tok, x4, scales = act_map("y0"), act_map("u_tok"), act_map("x4"), dram("scales", P, 68)
        spectral_prepare(nc, sems, "s1", xn3, x3, y0, u_tok, scales, a["log_weights"], a["gumbel"], a["sigma"], a["m_u"],
                         a["ident"], a["exchange"], a["rank4"])
        spectral(nc, sems, "s2", u_tok, y0, x4, scales, a["phi"], a["m_phi"])
        xn4, x5, xn5 = act_map("xn4"), act_map("x5"), act_map("xn5")
        layer_norm(nc, sems, "ln4", x4, xn4, a["channel_mean"], 1e-5)
        linear_attention(nc, sems, "l3", xn4, x4, x5, a["wk_t"], a["wq_heads"], a["wv_t"], a["ident"])
        layer_norm(nc, sems, "ln5", x5, xn5, a["channel_mean"], 1e-5)
        experts(nc, sems, "moe", xn5, x5, out, a["router_w"], a["router_b"], a["expert_w"], a["expert_b"], a["ident"], a["rank8"])


def layout(i):
    import numpy as np

    i = {name: np.asarray(v) for name, v in i.items()}
    eye = np.eye(P, dtype=np.float32)
    side, e32, z32 = np.eye(SIDE, dtype=np.float32), np.eye(32, dtype=np.float32), np.zeros((32, 32), np.float32)

    def rows(v):
        return np.broadcast_to(v.reshape(1, -1), (P, v.size))

    def tiles(v):
        return v.reshape(INNER_TILES, P, -1).transpose(1, 0, 2)

    w = i["L0_conv_w_qkv"]
    heads = [np.concatenate([np.tile(w[:, h * 32:h * 32 + 32], (1, 4)), np.tile(w[:, P + h * 32:P + h * 32 + 32], (1, 4)),
                             w[:, 2 * P + h * 32:2 * P + h * 32 + 32]], 1) for h in range(4)]
    w_x, filters = i["L1_conv_w_xproj"], i["L2_ffn_phi"].T
    first = np.zeros((P, P), np.float32)
    first[0] = 1
    return {
        "x": i["x"].reshape(TOK, P).T,
        "group_mean": np.kron(np.eye(P // 4, dtype=np.float32), np.full((4, 4), 0.25, np.float32)),
        "channel_mean": np.full((P, P), 1 / P, np.float32),
        "inner_mean": np.full((P, P), 1 / (INNER_TILES * P), np.float32),
        "ident": eye, "exchange": eye[::-1], "first": first,
        "cells": np.concatenate([np.repeat(side, SIDE, 1), np.tile(side, (1, SIDE))], 0),
        "pick_halves": np.block([[e32, z32], [z32, e32], [e32, z32], [z32, e32]]),
        "pick_parts": np.concatenate([e32, e32], 0),
        "rank4": rows(np.arange(4, 0, -1).astype(np.float32)), "rank8": rows(np.arange(8, 0, -1).astype(np.float32)),
        "w_heads": np.concatenate(heads, 0), "emb_h": i["L0_conv_pos_emb_h"].T, "emb_w": i["L0_conv_pos_emb_w"].T,
        "w_in": i["L1_conv_w_in"], "conv_w": tiles(i["L1_conv_conv_w"].reshape(9, 2 * P).T), "conv_b": i["L1_conv_conv_b"].reshape(2, P).T,
        "w_x": tiles(np.concatenate([w_x[:, 8:40], w_x[:, 8:40], w_x[:, :8]], 1)), "w_dt": i["L1_conv_w_dt"],
        "b_dt": i["L1_conv_b_dt"].reshape(2, P).T, "a_log": tiles(i["L1_conv_A_log"]), "d_param": i["L1_conv_D_param"].reshape(2, P).T,
        "ln_w": i["L1_conv_ln_w"].reshape(2, P).T, "ln_b": i["L1_conv_ln_b"].reshape(2, P).T, "w_out": tiles(i["L1_conv_w_out"]),
        "w_query": i["L2_attn_w_query"], "w_key": i["L2_attn_w_key"], "w_value": i["L2_attn_w_value"],
        "log_weights": rows(i["L2_ffn_log_weights"]), "gumbel": rows(i["L2_ffn_gumbel"]), "sigma": rows(i["L2_ffn_sigma"]),
        "m_u": i["L2_ffn_M_u"].transpose(2, 0, 1, 3).reshape(P, 4, 3 * P),
        "phi": np.concatenate([np.zeros((16, 127), np.float32), filters[:, 0::2], np.zeros((16, 129), np.float32), filters[:, 1::2]], 1),
        "m_phi": np.stack([i["L2_ffn_M_phi_plus"], i["L2_ffn_M_phi_minus"]]).transpose(2, 3, 0, 1, 4).reshape(16 * P, 8 * P),
        "wk_t": i["L3_attn_Wk"].reshape(8 * 64, P).T, "wq_heads": i["L3_attn_Wq"].transpose(1, 0, 2), "wv_t": i["L3_attn_Wv"].reshape(8 * P, P).T,
        "router_w": i["L3_ffn_router_w"], "router_b": rows(i["L3_ffn_router_b"]),
        "expert_w": i["L3_ffn_expert_w"].transpose(1, 0, 2).reshape(P, 8 * P), "expert_b": i["L3_ffn_expert_b"].reshape(1, 8 * P),
    }


def kernel(**inputs):
    import numpy as _np
    import concourse.bacc as _bacc
    from concourse import mybir as _mybir
    from concourse.bass_utils import run_bass_kernel_spmd as _run

    nc = _bacc.Bacc("TRN2", target_bir_lowering=False, num_devices=1)
    arrays = {f"in_{name}": _np.ascontiguousarray(v) for name, v in layout(inputs).items()}
    args = {name[3:]: nc.dram_tensor(name, v.shape, _mybir.dt.from_np(v.dtype), kind="ExternalInput").ap() for name, v in arrays.items()}
    out = nc.dram_tensor("out", (TOK, P), _mybir.dt.float32, kind="ExternalOutput").ap()
    block_layers(nc, args, out)
    r = _run(nc, [arrays], core_ids=[0])
    return r.results[0]["out"].reshape(BATCH, SIDE, SIDE, P)
```

```python
from contextlib import ExitStack

import concourse.bass as bass
from concourse import mybir

F32 = mybir.dt.float32
F32R = mybir.dt.float32r
ALU = mybir.AluOpType
ACT = mybir.ActivationFunctionType
AX = mybir.AxisListType

P = 128
BATCH = 2
SIDE = 64
L = SIDE * SIDE
TOK = BATCH * L
TW = 512
NT = TOK // TW
NTB = L // TW
KT = L // P


class Mem:

    def __init__(self, nc, stage, sems=None):
        self.nc, self.stage, self.stack, self.blocks, self.held = nc, stage, ExitStack(), ExitStack(), []

    def __enter__(self):
        self.stack.__enter__()
        return self

    def __exit__(self, *how):
        self.blocks.close()
        if how[0] is None:
            with self.nc.Block() as block:
                @block.sync
                def _(sp):
                    for s in self.held:
                        sp.sem_clear(s)
        return self.stack.__exit__(*how)

    def sb(self, name, shape, dtype=F32):
        return self.stack.enter_context(self.nc.sbuf_tensor(f"{self.stage}_{name}", shape, dtype))

    def ps(self, name, shape, dtype=F32):
        return self.stack.enter_context(self.nc.psum_tensor(f"{self.stage}_ps_{name}", shape, dtype))

    def sem(self, name):
        self.held.append(self.stack.enter_context(self.nc.semaphore(f"{self.stage}_sem_{name}")))
        return self.held[-1]

    def block(self):
        return self.blocks.enter_context(self.nc.Block())


class Chain:

    def __init__(self, eng, sem):
        self.eng, self.sem, self.n = eng, sem, 0

    def step(self, ins):
        self.n += 1
        ins.then_inc(self.sem, 1)

    def done(self):
        self.eng.wait_ge(self.sem, self.n)

    def link(self, ins):
        self.step(ins)
        self.done()
def group_norm(nc, sems, stage, x, xn, group_mean, eps, addend=None, x_sum=None):
    with Mem(nc, stage, sems) as m:
        xs = m.sb("x", [P, TOK])
        more = m.sb("addend", [P, TOK]) if addend is not None else None
        xo = m.sb("xn", [P, TOK])
        added, sum_stored = m.sem("added"), m.sem("sum_stored")
        gm = m.sb("group_mean", [P, P])
        stats = m.sb("stats", [P, BATCH, NTB, 6])
        aggr = m.sb("aggr", [P, BATCH, 2])
        mom = m.sb("moments", [P, BATCH, 2])
        grp = m.sb("group_moments", [P, BATCH, 2])
        msq = m.sb("mean_squared", [P, BATCH, 1])
        var = m.sb("variance", [P, BATCH, 1])
        std = m.sb("deviation", [P, BATCH, 1])
        rstd = m.sb("reciprocal", [P, BATCH, 1])
        gps = m.ps("sums", [P, BATCH, 2])
        loaded, weights = m.sem("loaded"), m.sem("weights")
        own, moments, sums, variance, deviation = (m.sem(n) for n in ("own", "moments", "sums", "variance", "deviation"))
        normed, stored = m.sem("normed"), m.sem("stored")
        block = m.block()

        @block.sync
        def _(sp):
            sp.dma_start(gm[:, :], group_mean).then_inc(weights, 16)
            for b in range(BATCH):
                sp.dma_start(xs[:, b * L:(b + 1) * L], x[:, b * L:(b + 1) * L]).then_inc(loaded, 16)
                if more is not None:
                    sp.dma_start(more[:, b * L:(b + 1) * L], addend[:, b * L:(b + 1) * L]).then_inc(loaded, 16)
            if more is not None:
                sp.wait_ge(added, BATCH)
                sp.dma_start(x_sum, xs[:, :]).then_inc(sum_stored, 16)
                sp.wait_ge(sum_stored, 16)
            for b in range(BATCH):
                sp.wait_ge(normed, b + 1)
                sp.dma_start(xn[:, b * L:(b + 1) * L], xo[:, b * L:(b + 1) * L]).then_inc(stored, 16)
            sp.wait_ge(stored, 16 * BATCH)

        @block.vector
        def _(dve):
            own_chain = Chain(dve, own)
            dve.wait_ge(loaded, 16 * BATCH * (1 if more is None else 2))
            if more is not None:
                for b in range(BATCH):
                    part = slice(b * L, (b + 1) * L)
                    dve.tensor_tensor(xs[:, part], xs[:, part], more[:, part], ALU.add).then_inc(added, 1)
                dve.wait_ge(added, BATCH)
            for b in range(BATCH):
                for t in range(NTB):
                    own_chain.step(dve.bn_stats(stats[:, b, t, :], xs[:, b * L + t * TW:b * L + (t + 1) * TW]))
            own_chain.done()
            for b in range(BATCH):
                own_chain.step(dve.bn_aggr(aggr[:, b, :], stats[:, b, :, :]))
            own_chain.done()
            own_chain.link(dve.tensor_tensor(msq[:, :, :], aggr[:, :, 0:1], aggr[:, :, 0:1], ALU.mult))
            dve.tensor_copy(mom[:, :, 0:1], aggr[:, :, 0:1]).then_inc(moments, 1)
            dve.tensor_tensor(mom[:, :, 1:2], msq[:, :, :], aggr[:, :, 1:2], ALU.add).then_inc(moments, 1)
            dve.wait_ge(sums, 1)
            own_chain.link(dve.tensor_copy(grp[:, :, :], gps[:, :, :]))
            own_chain.link(dve.tensor_tensor(msq[:, :, :], grp[:, :, 0:1], grp[:, :, 0:1], ALU.mult))
            own_chain.link(dve.tensor_tensor(var[:, :, :], grp[:, :, 1:2], msq[:, :, :], ALU.subtract))
            dve.tensor_scalar(std[:, :, :], var[:, :, :], 0.0, eps, ALU.max, ALU.add).then_inc(variance, 1)
            dve.wait_ge(deviation, 1)
            own_chain.link(dve.reciprocal(rstd[:, :, :], var[:, :, :]))
            for b in range(BATCH):
                part = slice(b * L, (b + 1) * L)
                dve.tensor_scalar(xo[:, part], xs[:, part], grp[:, b, 0:1], rstd[:, b, 0:1], ALU.subtract, ALU.mult).then_inc(normed, 1)

        @block.tensor
        def _(pe):
            pe.wait_ge(weights, 16)
            pe.wait_ge(moments, 2)
            pe.matmul(gps[:, :, :], gm[:, :], mom[:, :, :], start=True, stop=True).then_inc(sums, 1)

        @block.scalar
        def _(act):
            act.wait_ge(variance, 1)
            act.activation(var[:, :, :], std[:, :, :], ACT.Sqrt).then_inc(deviation, 1)


def layer_norm(nc, sems, stage, x, xn, channel_mean, ident_in, eps):
    LOT = 4
    LOTS, COLS = NT // LOT, LOT * TW // P
    with Mem(nc, stage, sems) as m:
        xs, xc, sq = m.sb("x", [P, TOK]), m.sb("centred", [P, TOK]), m.sb("square", [P, TOK])
        cm, ident = m.sb("channel_mean", [P, P]), m.sb("ident", [P, P])
        epst = m.sb("eps", [P, 1])
        std, rstd = m.sb("deviation", [P, LOTS, COLS]), m.sb("reciprocal", [P, LOTS, COLS])
        mean_ps, var_ps, wide_ps = m.ps("mean", [P, 2, TW]), m.ps("variance", [P, 2, TW]), m.ps("reciprocal", [P, 2, TW])
        weights, own, loaded = m.sem("weights"), m.sem("own"), [m.sem(f"loaded{q}") for q in range(LOTS)]
        mean, centred, squared, variance, deviation, recip, spread, normed, stored = (
            m.sem(n) for n in ("mean", "centred", "squared", "variance", "deviation", "recip", "spread", "normed", "stored"))
        block = m.block()

        def at(t):
            return slice(t * TW, (t + 1) * TW)

        @block.sync
        def _(sp):
            sp.dma_start(cm[:, :], channel_mean).then_inc(weights, 16)
            sp.dma_start(ident[:, :], ident_in).then_inc(weights, 16)
            for q in range(LOTS):
                part = slice(q * LOT * TW, (q + 1) * LOT * TW)
                sp.dma_start(xs[:, part], x[:, part]).then_inc(loaded[q], 16)
            for q in range(LOTS):
                part = slice(q * LOT * TW, (q + 1) * LOT * TW)
                sp.wait_ge(normed, (q + 1) * LOT)
                sp.dma_start(xn[:, part], xc[:, part]).then_inc(stored, 16)
            sp.wait_ge(stored, 16 * LOTS)

        @block.tensor
        def _(pe):
            pe.wait_ge(weights, 32)

            def take_variance(t):
                q, k = t // LOT, t % LOT
                pe.wait_ge(squared, t + 1)
                if k == 0 and q >= 2:
                    pe.wait_ge(deviation, q - 1)
                for n in range(TW // P):
                    col = k * (TW // P) + n
                    ins = pe.matmul(var_ps[:, q % 2, col:col + 1], sq[:, t * TW + n * P:t * TW + (n + 1) * P], cm[:, 0:1], start=True, stop=True)
                ins.then_inc(variance, 1)

            def spread_out(t):
                q, k = t // LOT, t % LOT
                pe.wait_ge(recip, q + 1)
                if t >= 2:
                    pe.wait_ge(normed, t - 1)
                for n in range(TW // P):
                    col = k * (TW // P) + n
                    ins = pe.matmul(wide_ps[:, t % 2, n * P:(n + 1) * P], rstd[:, q, col:col + 1].to_broadcast((P, P)), ident[:, :], start=True, stop=True)
                ins.then_inc(spread, 1)

            for t in range(NT):
                if t % LOT == 0:
                    pe.wait_ge(loaded[t // LOT], 16)
                if t >= 2:
                    pe.wait_ge(centred, t - 1)
                pe.matmul(mean_ps[:, t % 2, :], cm[:, :], xs[:, at(t)], start=True, stop=True).then_inc(mean, 1)
                if t >= 1:
                    take_variance(t - 1)
                if t >= LOT + 2:
                    spread_out(t - LOT - 2)
            take_variance(NT - 1)
            for t in range(NT - LOT - 2, NT):
                spread_out(t)

        @block.scalar
        def _(act):
            act.wait_ge(own, 1)
            for t in range(NT):
                q = t // LOT
                act.wait_ge(centred, t + 1)
                act.activation(sq[:, at(t)], xc[:, at(t)], ACT.Square).then_inc(squared, 1)
                if t % LOT == LOT - 1:
                    act.wait_ge(variance, t + 1)
                    act.activation(std[:, q, :], var_ps[:, q % 2, 0:COLS], ACT.Sqrt, bias=epst[:, :]).then_inc(deviation, 1)

        @block.vector
        def _(dve):
            dve.memset(epst[:, :], eps).then_inc(own, 1)

            def normalise(t):
                dve.wait_ge(spread, t + 1)
                dve.tensor_tensor(xc[:, at(t)], xc[:, at(t)], wide_ps[:, t % 2, :], ALU.mult).then_inc(normed, 1)

            def invert(q):
                dve.wait_ge(deviation, q + 1)
                dve.reciprocal(rstd[:, q, :], std[:, q, :]).then_inc(recip, 1)

            for t in range(NT):
                dve.wait_ge(mean, t + 1)
                if t % LOT == 0:
                    dve.wait_ge(loaded[t // LOT], 16)
                dve.tensor_tensor(xc[:, at(t)], xs[:, at(t)], mean_ps[:, t % 2, :], ALU.subtract).then_inc(centred, 1)
                if t % LOT == 1 and t > LOT:
                    invert(t // LOT - 1)
                if t >= LOT + 2:
                    dve.wait_ge(squared, t - LOT - 1)
                    normalise(t - LOT - 2)
            invert(LOTS - 1)
            for t in range(NT - LOT - 2, NT):
                dve.wait_ge(squared, t + 1)
                normalise(t)
def bias_attention(nc, sems, stage, xn, att, w_heads, emb_h, emb_w, cells_in, ident_in, pick_in):
    HEADS, D = 4, 32
    SCALE = 1.0 / float(D) ** 0.5
    QT, KC = TW // P, L // TW
    UNITS = QT * KC
    BLOCKS = HEADS * BATCH * NTB
    JOBS = 2 * NTB + 2 + 2 * NTB
    SLOTS = 8
    TAKEN = 4 * NTB
    with Mem(nc, stage, sems) as m:
        xs = m.sb("xn", [P, L])
        w = m.sb("w", [P, 2 * P + D])
        eh, ew = m.sb("emb_h", [D, 2 * SIDE - 1]), m.sb("emb_w", [D, 2 * SIDE - 1])
        ident, pick, ones = m.sb("ident", [P, P]), m.sb("pick", [P, D]), m.sb("ones", [P, D])
        cells = m.sb("cells", [P, L], F32R)
        qs, ks = m.sb("q_parts", [P, L], F32R), m.sb("k_parts", [P, L], F32R)
        q32 = m.sb("q", [D, L])
        r32 = m.sb("bias", [P, L])
        rh, rl = m.sb("bias_high", [P, L], F32R), m.sb("bias_low", [P, L], F32R)
        qn, rn = m.sb("q_of_maxima", [P, TW], F32R), m.sb("bias_of_maxima", [P, TW], F32R)
        vv = m.sb("v", [P, KT, D])
        mx8, mx = m.sb("max_chunks", [P, QT, KC]), m.sb("max", [P, QT])
        mxw = m.sb("max_wide", [P, QT, SIDE])
        pt = m.sb("probs", [P, SLOTS, TW])
        acc = m.sb("probs_sum", [P, 2, TW])
        osb = m.sb("out_parts", [P, TW])
        inv, o32 = m.sb("inverse", [D, TW]), m.sb("out", [D, 2, TW])
        ps = m.ps("all", [P, 8, TW])
        MAX0, OUT, NUM, DEN = 3, 5, 6, 7
        entered = m.sem("entered")
        const, cells_ok, ones_ok = m.sem("const"), m.sem("cells_ok"), m.sem("ones_ok")
        image_in, w_in = m.sem("image_in"), m.sem("w_in")
        filled, copied, taken, own = m.sem("filled"), m.sem("copied"), m.sem("taken"), m.sem("own")
        max_filled, max_taken, wide_ok = m.sem("max_filled"), m.sem("max_taken"), m.sem("wide_ok")
        turned, shifted = m.sem("turned"), m.sem("shifted")
        fetched = m.sem("fetched")
        scored, expd, weighed, added = m.sem("scored"), m.sem("expd"), m.sem("weighed"), m.sem("added")
        parts_ok, summed, inverted = m.sem("parts_ok"), m.sem("summed"), m.sem("inverted")
        divided, stored = m.sem("divided"), [m.sem("stored0"), m.sem("stored1")]
        block = m.block()
        raw_cells = r32

        def f(ap):
            return ap.bitcast(F32)

        @block.sync
        def _(sp):
            for s in stored:
                sp.sem_inc(s, 16)
            for dst, src in ((eh, emb_h), (ew, emb_w), (ident, ident_in), (pick, pick_in), (raw_cells, cells_in)):
                sp.dma_start(dst[:], src).then_inc(const, 16)
            with sp.Fori(0, BATCH) as b:
                with sp.Fori(0, HEADS) as h:
                    it = b * HEADS + h
                    sp.wait_ge(filled, it * JOBS + 1)
                    sp.dma_start(xs[:, :], xn[:, bass.ts(b, L)]).then_inc(image_in, 16)
                    sp.dma_start(w[:, :], w_heads[bass.ts(h, P), :]).then_inc(w_in, 16)
                    for j in range(NTB):
                        sp.wait_ge(divided, it * NTB + j + 2)
                        sp.dma_start(att[bass.ts(h, D), bass.ds(b * L + j * TW, TW)], o32[:, j % 2, :]).then_inc(stored[j % 2], 16)
            for s in stored:
                sp.wait_ge(s, 8 * BLOCKS + 16)

        @block.tensor
        def _(pe):
            pe.sem_inc(filled, 1)
            pe.sem_inc(summed, 1)
            pe.wait_ge(const, 80)
            pe.wait_ge(cells_ok, 1)
            pe.wait_ge(ones_ok, 1)
            with pe.Fori(0, BATCH * HEADS) as it:
                pe.wait_ge(image_in, it * 16 + 16)
                pe.wait_ge(w_in, it * 16 + 16)
                n = 0

                def bank_free(k):
                    if k >= 4:
                        pe.wait_ge(copied, it * JOBS + (k - 3))
                    if 4 <= k < 2 * NTB + 4:
                        pe.wait_ge(taken, it * TAKEN + (k - 3))

                for part in range(2):
                    for t in range(NTB):
                        bank_free(n)
                        pe.matmul(ps[:, n % 4, :], w[:, part * P:(part + 1) * P], xs[:, t * TW:(t + 1) * TW],
                                  start=True, stop=True).then_inc(filled, 1)
                        n += 1
                for half in range(2):
                    bank_free(n)
                    for t in range(KT // 2):
                        tok = (half * KT // 2 + t) * P
                        ins = pe.matmul(ps[:, n % 4, t * D:(t + 1) * D], xs[:, tok:tok + P], w[:, 2 * P:2 * P + D],
                                        start=True, stop=True)
                    ins.then_inc(filled, 1)
                    n += 1
                for g in range(NTB):
                    bank_free(n)
                    for k in range(8):
                        x = 8 * g + k
                        ins = pe.matmul(ps[0:SIDE, n % 4, k * SIDE:(k + 1) * SIDE], eh[:, SIDE - 1 - x:2 * SIDE - 1 - x],
                                        q32[:, x * SIDE:(x + 1) * SIDE], start=True, stop=True)
                    ins.then_inc(filled, 1)
                    n += 1
                qcol = q32[:, :].rearrange("d (x y) -> d y x", y=SIDE)
                for g in range(NTB):
                    bank_free(n)
                    for k in range(8):
                        y = 8 * g + k
                        ins = pe.matmul(ps[SIDE:P, n % 4, k * SIDE:(k + 1) * SIDE], ew[:, SIDE - 1 - y:2 * SIDE - 1 - y],
                                        qcol[:, y, :], start=True, stop=True)
                    ins.then_inc(filled, 1)
                    n += 1
                pe.wait_ge(copied, it * JOBS + JOBS)
                pe.wait_ge(taken, it * TAKEN + TAKEN)

                def max_unit(row, u, first=False):
                    bank, keys = ps[:, MAX0 + u % 2, :], slice(u % KC * TW, (u % KC + 1) * TW)
                    if u == 0:
                        pe.wait_ge(fetched, row + 1)
                    if u >= 2 or not first:
                        pe.wait_ge(max_taken, row * UNITS + (u - 1))
                    at = slice(u // KC * P, (u // KC + 1) * P)
                    pe.matmul(bank, qn[:, at], ks[:, keys], start=True, stop=False)
                    pe.matmul(bank, rn[:, at], cells[:, keys], start=False, stop=True).then_inc(max_filled, 1)

                def turn(row):
                    pe.wait_ge(wide_ok, row + 1)
                    for k in range(QT):
                        ins = pe.matmul(ps[0:SIDE, MAX0, k * P:(k + 1) * P], mxw[:, k, :], ident[:, :], start=True, stop=True)
                    ins.then_inc(turned, 1)

                def score(row, queries, i, first=False):
                    if i == 0:
                        pe.wait_ge(shifted, row + 1)
                    if i >= 3:
                        pe.wait_ge(expd, row * KT + (i - 2))
                    elif i < 2 and not first:
                        pe.wait_ge(expd, row * KT + (i - 1))
                    o, keys = ps[:, i % 3, :], slice(i * P, (i + 1) * P)
                    pe.matmul(o, ks[:, keys], qs[:, queries], start=True, stop=False)
                    pe.matmul(o, cells[:, keys], rh[:, queries], start=False, stop=False)
                    pe.matmul(o, cells[:, keys], rl[:, queries], start=False, stop=True).then_inc(scored, 1)

                def finish(row, slot):
                    pe.wait_ge(parts_ok, row + 1)
                    pe.wait_ge(divided, row + 1)
                    pe.matmul(ps[0:D, NUM, :], pick[:, :], osb[:, :], start=True, stop=True)
                    pe.wait_ge(added, row * KT + (KT + SLOTS))
                    pe.matmul(ps[0:D, DEN, :], ones[:, :], acc[:, slot, :], start=True, stop=True).then_inc(summed, 1)

                def attend(row, start, slot, head=False, tail=False):
                    queries, following = bass.ds(start, TW), bass.ds(start + TW, TW)
                    unit = 0
                    for i in range(KT):
                        if i == 2 and not head:
                            finish(row - 1, 1 - slot)
                        if not tail:
                            while unit < UNITS and unit < (i - 5) * 1.7:
                                max_unit(row + 1, unit)
                                unit += 1
                            if i == KT - 5:
                                turn(row + 1)
                        if i + 2 < KT:
                            score(row, queries, i + 2)
                        elif not tail and i == KT - 2:
                            score(row + 1, following, 0)
                        pe.wait_ge(expd, row * KT + (i + 1))
                        if i == 0 and not head:
                            pe.wait_ge(parts_ok, row)
                        s = D * (i % 4)
                        pe.matmul(ps[s:s + D, OUT, :], vv[:, i, :], pt[:, i % SLOTS, :], start=(i < 4), stop=(i >= KT - 4)).then_inc(weighed, 1)
                    if tail:
                        finish(row, slot)
                    else:
                        score(row + 1, following, 1)

                row0 = it * NTB
                for u in range(UNITS):
                    max_unit(row0, u, first=True)
                turn(row0)
                for i in range(2):
                    score(row0, slice(0, TW), i, first=True)
                attend(row0, 0, 0, head=True)
                pe.sem_inc(entered, 1)
                with pe.Fori(0, NTB // 2 - 1) as jj:
                    for k in (1, 2):
                        attend(row0 + jj * 2 + k, jj * (2 * TW) + k * TW, k % 2)
                attend(row0 + (NTB - 1), (NTB - 1) * TW, 1, tail=True)

        @block.scalar
        def _(act):
            act.wait_ge(cells_ok, 1)
            with act.Fori(0, BATCH * HEADS) as it:
                n = 0
                for part in range(2):
                    for t in range(NTB):
                        act.wait_ge(filled, it * JOBS + (n + 2))
                        cols, bank = slice(t * TW, (t + 1) * TW), n % 4
                        if part == 0:
                            act.activation(q32[:, cols], ps[0:D, bank, :], ACT.Copy)
                            act.activation(qs[:, cols], ps[:, bank, :], ACT.Copy).then_inc(copied, 1)
                        else:
                            act.activation(ks[:, cols], ps[:, bank, :], ACT.Copy, scale=SCALE).then_inc(copied, 1)
                        n += 1
                for half in range(2):
                    act.wait_ge(filled, it * JOBS + (n + 2))
                    t0 = half * KT // 2
                    act.activation(vv[:, t0:t0 + KT // 2, :], ps[:, n % 4, :].rearrange("p (t d) -> p t d", d=D), ACT.Copy).then_inc(copied, 1)
                    n += 1
                for g in range(NTB):
                    act.wait_ge(filled, it * JOBS + (n + 2))
                    act.activation(r32[0:SIDE, g * TW:(g + 1) * TW], ps[0:SIDE, n % 4, :], ACT.Copy).then_inc(copied, 1)
                    n += 1
                for g in range(NTB):
                    act.wait_ge(filled, it * JOBS + (n + 2))
                    act.activation(r32[SIDE:P, :].rearrange("p (x y) -> p y x", y=SIDE)[:, 8 * g:8 * g + 8, :],
                                   ps[SIDE:P, n % 4, :].rearrange("p (y x) -> p y x", x=SIDE), ACT.Copy).then_inc(copied, 1)
                    n += 1
                act.sem_inc(entered, 1)
                with act.Fori(0, NTB) as j:
                    tile0 = it * (NTB * KT) + j * KT
                    for i in range(KT):
                        act.wait_ge(scored, tile0 + (i + 1))
                        if i >= SLOTS:
                            act.wait_ge(weighed, tile0 + (i + 1 - SLOTS))
                        act.wait_ge(added, tile0 + (i + 1))
                        act.activation(pt[:, i % SLOTS, :], ps[:, i % 3, :], ACT.Exp).then_inc(expd, 1)

        @block.gpsimd
        def _(pool):
            pool.sem_inc(added, SLOTS)
            pool.sem_inc(summed, 1)
            with pool.Fori(0, BLOCKS // 2) as pair:
                for slot in range(2):
                    row = pair * 2 + slot
                    for i in range(1, KT):
                        pool.wait_ge(expd, row * KT + (i + 1))
                        if i == 1:
                            pool.wait_ge(summed, row + 1)
                            pool.tensor_tensor(acc[:, slot, :], pt[:, 0, :], pt[:, 1, :], ALU.add).then_inc(added, 2)
                        else:
                            pool.wait_ge(added, row * KT + (i + SLOTS))
                            pool.tensor_tensor(acc[:, slot, :], acc[:, slot, :], pt[:, i % SLOTS, :], ALU.add).then_inc(added, 1)

        @block.vector
        def _(dve):
            dve.sem_inc(divided, 1)
            dve.memset(ones[:, :], 1.0).then_inc(ones_ok, 1)
            dve.wait_ge(const, 80)
            dve.tensor_copy(cells[:, :], raw_cells[:, :]).then_inc(cells_ok, 1)
            dve.wait_ge(cells_ok, 1)
            with dve.Fori(0, BATCH * HEADS) as it:
                job0 = it * JOBS
                n = 0
                for t in range(NTB):
                    dve.wait_ge(copied, job0 + (n + 1))
                    cols, bank = slice(t * TW, (t + 1) * TW), n % 4
                    for s in (D, 3 * D):
                        ins = dve.tensor_tensor(qs[s:s + D, cols], ps[s:s + D, bank, :], f(qs[s:s + D, cols]), ALU.subtract)
                    ins.then_inc(taken, 1)
                    n += 1
                for t in range(NTB):
                    dve.wait_ge(copied, job0 + (n + 1))
                    cols, bank = slice(t * TW, (t + 1) * TW), n % 4
                    dve.scalar_tensor_tensor(ks[SIDE:P, cols], ps[SIDE:P, bank, :], SCALE, f(ks[SIDE:P, cols]),
                                             ALU.mult, ALU.subtract).then_inc(taken, 1)
                    n += 1
                n += 2
                for g in range(NTB):
                    dve.wait_ge(copied, job0 + (n + 1))
                    dve.tensor_copy(rh[0:SIDE, g * TW:(g + 1) * TW], r32[0:SIDE, g * TW:(g + 1) * TW]).then_inc(taken, 1)
                    n += 1
                for g in range(NTB):
                    dve.wait_ge(copied, job0 + (n + 1))
                    dst, src = (r[SIDE:P, :].rearrange("p (x y) -> p y x", y=SIDE)[:, 8 * g:8 * g + 8, :] for r in (rh, r32))
                    dve.tensor_copy(dst, src).then_inc(taken, 1)
                    n += 1
                assert n == JOBS

                def fetch(start):
                    dve.tensor_copy(qn[:, :], f(qs[:, start:start + TW]))
                    dve.tensor_copy(rn[:, :], f(rh[:, start:start + TW])).then_inc(fetched, 1)

                def shift(row, start):
                    def link(ins, k):
                        ins.then_inc(own, 1)
                        dve.wait_ge(own, row * 3 + k)

                    for u in range(UNITS):
                        dve.wait_ge(max_filled, row * UNITS + (u + 1))
                        dve.tensor_reduce(mx8[:, u // KC, u % KC:u % KC + 1], ps[:, MAX0 + u % 2, :], AX.X, ALU.max).then_inc(max_taken, 1)
                    dve.wait_ge(max_taken, row * UNITS + UNITS)
                    link(dve.tensor_reduce(mx[:, :], mx8[:, :, :], AX.X, ALU.max), 1)
                    dve.tensor_copy(mxw[:, :, :], mx[:, :].rearrange("p (t a) -> p t a", a=1).to_broadcast((P, QT, SIDE))).then_inc(wide_ok, 1)
                    dve.wait_ge(turned, row + 1)
                    cols = slice(start, start + TW)
                    link(dve.tensor_tensor(r32[0:SIDE, cols], r32[0:SIDE, cols], ps[0:SIDE, MAX0, :], ALU.subtract), 2)
                    link(dve.tensor_copy(rh[:, cols], r32[:, cols]), 3)
                    dve.tensor_tensor(rl[:, cols], r32[:, cols], f(rh[:, cols]), ALU.subtract).then_inc(shifted, 1)
                    if start + TW < L:
                        fetch(start + TW)

                def divide(row, slot, uses):
                    dve.wait_ge(weighed, row * KT + KT)
                    dve.tensor_copy(osb[:, :], ps[:, OUT, :]).then_inc(parts_ok, 1)
                    dve.wait_ge(summed, row + 3)
                    dve.reciprocal(inv[:, :], ps[0:D, DEN, :]).then_inc(inverted, 1)
                    dve.wait_ge(inverted, row + 1)
                    dve.wait_ge(stored[slot], uses * 16 + 16)
                    dve.tensor_tensor(o32[:, slot, :], ps[0:D, NUM, :], inv[:, :], ALU.mult).then_inc(divided, 1)

                dve.wait_ge(taken, it * TAKEN + TAKEN)
                fetch(0)
                shift(it * NTB, 0)
                dve.sem_inc(entered, 1)
                for j in range(NTB):
                    row = it * NTB + j
                    if j + 1 < NTB:
                        shift(row + 1, (j + 1) * TW)
                    divide(row, j % 2, it * (NTB // 2) + j // 2)
INNER_TILES, STATES, RANK, DIRS = 2, 16, 8, 4


W = 1024
CHUNKS = L // W


def in_chunks(steps):
    return steps.rearrange("p (q t) -> p q t", t=W)


def scan_order(image, direction):
    part, (step, _), base = list(image.ap[0]), image.ap[1], image.offset
    if direction == 0:
        return image.rearrange("p (a c) -> p a c", c=SIDE)
    if direction == 1:
        return image.rearrange("p (a c) -> p c a", c=SIDE)
    last = base + (L - 1) * step
    strides = (SIDE, 1) if direction == 2 else (1, SIDE)
    return bass.AP(image.tensor, last, [part] + [[-s * step, SIDE] for s in strides])


def mamba_prepare(nc, sems, stage, xn, gates, u_img, delta, du, bc, w_in, conv_w, conv_b, w_x, w_dt, b_dt, ident_in):
    PADW = SIDE + 2
    ROWS = TW // SIDE
    plan = []
    for b in range(BATCH):
        for ct in range(INNER_TILES):
            plan += [(kind, b, ct, t) for kind in ("inner", "gate", "conv") for t in range(NTB)]
        plan += [("bc", b, 0, t) for t in range(NTB)] + [("rank", b, 0, t) for t in range(NTB)]
        for ct in range(INNER_TILES):
            plan += [("step", b, ct, t) for t in range(NTB)]
    on_dve = ("bc", "step")
    number = {job: n for n, job in enumerate(plan)}
    dve_jobs = [job for job in plan if job[0] in on_dve]
    act_jobs = [job for job in plan if job[0] not in on_dve]
    dve_number = {job: n for n, job in enumerate(dve_jobs)}
    act_number = {job: n for n, job in enumerate(act_jobs)}
    last = NTB - 1
    with Mem(nc, stage, sems) as m:
        xs, wi = m.sb("xn", [P, L]), m.sb("w_in", [P, 4 * P])
        cw, cb, bd = m.sb("conv_w", [P, INNER_TILES, 9]), m.sb("conv_b", [P, INNER_TILES]), m.sb("b_dt", [P, INNER_TILES])
        wx, wd, ident = m.sb("w_x", [P, INNER_TILES, 64 + RANK]), m.sb("w_dt", [RANK, INNER_TILES * P]), m.sb("ident", [P, P])
        diag = m.sb("conv_diagonals", [P, INNER_TILES, 9, P])
        padded = m.sb("padded", [P, PADW, PADW])
        xa = m.sb("u", [P, INNER_TILES, L])
        bcs, rank = m.sb("bc_parts", [64, L], F32R), m.sb("rank", [RANK, L])
        s, e, ln = m.sb("step", [P, L]), m.sb("exp", [P, L]), m.sb("log", [P, L])
        one = m.sb("one", [P, 1])
        dus = m.sb("delta_u", [P, 2, L])
        gs = m.sb("gate", [P, 4, TW])
        ps = m.ps("all", [P, 8, TW])
        names = ("const", "image_in", "border", "filled", "act_taken", "dve_taken", "own", "diagonals", "magnitude",
                 "expd", "logged", "delta_ok", "bc_stored", "u_stored", "conv_done", "bc_ok")
        (const, image_in, border, filled, act_taken, dve_taken, own, diagonals, magnitude, expd, logged, delta_ok,
         bc_stored, u_stored, conv_done, bc_ok) = (m.sem(n) for n in names)
        gate_stored = [m.sem(f"gate_stored{i}") for i in range(4)]
        du_ok = [m.sem(f"du_ok{i}") for i in range(2)]
        du_stored = [m.sem(f"du_stored{i}") for i in range(2)]
        delta_stored = m.sem("delta_stored")
        block = m.block()

        def times_u(eng, g, d):
            eng.wait_ge(delta_ok, g + 1)
            uses = g * DIRS // 2 + d // 2
            if uses:
                eng.wait_ge(du_stored[d % 2], 16 * uses)
            eng.tensor_tensor(dus[:, d % 2, :].rearrange("p (a c) -> p a c", c=SIDE), s[:, :].rearrange("p (a c) -> p a c", c=SIDE),
                              scan_order(xa[:, g % INNER_TILES, :], d), ALU.mult).then_inc(du_ok[d % 2], 1)

        @block.sync
        def _(sp):
            for dst, src in ((wi, w_in), (cw, conv_w), (cb, conv_b), (bd, b_dt), (wx, w_x), (wd, w_dt), (ident, ident_in)):
                sp.dma_start(dst[:], src).then_inc(const, 16)
            for b in range(BATCH):
                if b:
                    sp.wait_ge(filled, number["gate", b - 1, 1, last] + 1)
                sp.dma_start(xs[:, :], xn[:, b * L:(b + 1) * L]).then_inc(image_in, 16)
                for ct in range(INNER_TILES):
                    for t in range(NTB):
                        n = act_number["gate", b, ct, t]
                        sp.wait_ge(act_taken, n + 1)
                        sp.dma_start(gates[b, ct, :, t * TW:(t + 1) * TW], gs[:, t % 4, :]).then_inc(gate_stored[t % 4], 16)
                for ct in range(INNER_TILES):
                    sp.wait_ge(act_taken, act_number["conv", b, ct, last] + 1)
                    sp.dma_start(u_img[b, ct], xa[:, ct, :]).then_inc(u_stored, 16)
                sp.wait_ge(dve_taken, dve_number["bc", b, 0, last] + 1)
                sp.dma_start(bc[b], in_chunks(bcs[:, :].bitcast(F32))).then_inc(bc_stored, 16)
                for ct in range(INNER_TILES):
                    g = b * INNER_TILES + ct
                    sp.wait_ge(delta_ok, g + 1)
                    sp.dma_start(delta[g], in_chunks(s[:, :])).then_inc(delta_stored, 16)
                    for d in range(DIRS):
                        sp.wait_ge(du_ok[d % 2], g * DIRS // 2 + d // 2 + 1)
                        sp.dma_start(du[g, :, :, d], in_chunks(dus[:, d % 2, :])).then_inc(du_stored[d % 2], 16)
            for q in gate_stored:
                sp.wait_ge(q, 16 * NTB * BATCH * INNER_TILES // 4)
            for q in du_stored:
                sp.wait_ge(q, 16 * DIRS * BATCH * INNER_TILES // 2)
            sp.wait_ge(u_stored, 16 * BATCH * INNER_TILES)
            sp.wait_ge(delta_stored, 16 * BATCH * INNER_TILES)
            sp.wait_ge(bc_stored, 16 * BATCH)

        @block.tensor
        def _(pe):
            pe.wait_ge(const, 112)
            pe.wait_ge(diagonals, 18)
            for n, (kind, b, ct, t) in enumerate(plan):
                if n >= 8:
                    before = plan[n - 8]
                    if before[0] in on_dve:
                        pe.wait_ge(dve_taken, dve_number[before] + 1)
                    else:
                        pe.wait_ge(act_taken, act_number[before] + 1)
                cols, bank = slice(t * TW, (t + 1) * TW), ps[:, n % 8, :]
                if kind in ("inner", "gate"):
                    pe.wait_ge(image_in, 16 * (b + 1))
                    w0 = (0 if kind == "inner" else INNER_TILES * P) + ct * P
                    ins = pe.matmul(bank, wi[:, w0:w0 + P], xs[:, cols], start=True, stop=True)
                elif kind == "conv":
                    pe.wait_ge(act_taken, act_number["inner", b, ct, last] + 1)
                    for tap in range(9):
                        src = padded[:, ROWS * t + tap // 3:ROWS * t + tap // 3 + ROWS, tap % 3:tap % 3 + SIDE]
                        ins = pe.matmul(bank.rearrange("p (r c) -> p r c", c=SIDE), diag[:, ct, tap, :], src, start=(tap == 0), stop=(tap == 8))
                elif kind == "bc":
                    pe.wait_ge(act_taken, act_number["conv", b, 1, last] + 1)
                    for k in range(INNER_TILES):
                        ins = pe.matmul(bank[0:64, :], wx[:, k, 0:64], xa[:, k, cols], start=(k == 0), stop=(k == INNER_TILES - 1))
                elif kind == "rank":
                    for k in range(INNER_TILES):
                        ins = pe.matmul(bank[0:RANK, :], wx[:, k, 64:64 + RANK], xa[:, k, cols], start=(k == 0), stop=(k == INNER_TILES - 1))
                else:
                    pe.wait_ge(act_taken, act_number["rank", b, 0, last] + 1)
                    ins = pe.matmul(bank, wd[:, ct * P:(ct + 1) * P], rank[:, cols], start=True, stop=True)
                ins.then_inc(filled, 1)

        @block.scalar
        def _(act):
            act.wait_ge(const, 112)
            act.wait_ge(border, 1)
            for kind, b, ct, t in act_jobs:
                n = number[kind, b, ct, t]
                g = b * INNER_TILES + ct
                cols, bank = slice(t * TW, (t + 1) * TW), ps[:, n % 8, :]
                act.wait_ge(filled, n + 1)
                if kind == "inner":
                    if t == 0 and g:
                        act.wait_ge(filled, number["conv", (g - 1) // 2, (g - 1) % 2, last] + 1)
                    ins = act.activation(padded[:, 1 + ROWS * t:1 + ROWS * (t + 1), 1:1 + SIDE],
                                         bank.rearrange("p (r c) -> p r c", c=SIDE), ACT.Copy)
                elif kind == "gate":
                    uses = g * NTB // 4 + t // 4
                    if uses:
                        act.wait_ge(gate_stored[t % 4], 16 * uses)
                    ins = act.activation(gs[:, t % 4, :], bank, ACT.Silu)
                elif kind == "conv":
                    if t == 0 and b:
                        act.wait_ge(u_stored, 16 * b * INNER_TILES)
                        for q in du_ok:
                            act.wait_ge(q, DIRS * b * INNER_TILES // 2)
                        act.wait_ge(filled, number["rank", b - 1, 0, last] + 1)
                    ins = act.activation(xa[:, ct, cols], bank, ACT.Silu, bias=cb[:, ct:ct + 1])
                else:
                    if t == 0 and b:
                        act.wait_ge(filled, number["step", b - 1, 1, last] + 1)
                    ins = act.activation(rank[:, cols], bank[0:RANK, :], ACT.Copy)
                ins.then_inc(act_taken, 1)
                if kind == "rank" and t == last:
                    for k in range(INNER_TILES):
                        h = b * INNER_TILES + k
                        act.wait_ge(dve_taken, dve_number["step", b, k, last] + 1)
                        if h:
                            act.wait_ge(delta_ok, h)
                        act.activation(e[:, :], s[:, :], ACT.Abs).then_inc(magnitude, 1)
                        act.wait_ge(magnitude, h + 1)
                        act.activation(e[:, :], e[:, :], ACT.Exp, scale=-1.0).then_inc(expd, 1)
                        act.wait_ge(expd, h + 1)
                        act.activation(ln[:, :], e[:, :], ACT.Ln, bias=one[:, :]).then_inc(logged, 1)

        @block.vector
        def _(dve):
            chain = Chain(dve, own)
            dve.memset(one[:, :], 1.0)
            dve.memset(padded[:, :, :], 0.0).then_inc(border, 1)
            dve.wait_ge(const, 112)
            for ct in range(INNER_TILES):
                for tap in range(9):
                    dve.tensor_scalar(diag[:, ct, tap, :], ident[:, :], cw[:, ct, tap:tap + 1], None, ALU.mult).then_inc(diagonals, 1)

            for kind, b, ct, t in dve_jobs:
                n = number[kind, b, ct, t]
                g = b * INNER_TILES + ct
                cols, bank = slice(t * TW, (t + 1) * TW), ps[:, n % 8, :]
                dve.wait_ge(filled, n + 1)
                if kind == "bc":
                    if t == 0 and b:
                        dve.wait_ge(bc_stored, 16 * b)
                    chain.link(dve.tensor_copy(bcs[:, cols], bank[0:64, :]))
                    dve.tensor_tensor(bcs[32:64, cols], bank[32:64, :], bcs[32:64, cols].bitcast(F32), ALU.subtract).then_inc(dve_taken, 1)
                else:
                    if t == 0 and g:
                        dve.wait_ge(delta_stored, 16 * g)
                        for q in du_ok:
                            dve.wait_ge(q, DIRS * g // 2)
                    dve.tensor_scalar(s[:, cols], bank, bd[:, ct:ct + 1], None, ALU.add).then_inc(dve_taken, 1)
                    if t == last:
                        dve.wait_ge(logged, g + 1)
                        chain.link(dve.tensor_tensor(ln[:, :], ln[:, :], e[:, :], ALU.add))
                        chain.link(dve.tensor_scalar(e[:, :], e[:, :], 1.0, 1.0, ALU.add, ALU.subtract))
                        chain.link(dve.tensor_tensor(ln[:, :], ln[:, :], e[:, :], ALU.subtract))
                        dve.scalar_tensor_tensor(s[:, :], s[:, :], 0.0, ln[:, :], ALU.max, ALU.add).then_inc(delta_ok, 1)
                        for d in (0, 2):
                            times_u(dve, g, d)

        @block.gpsimd
        def _(pool):
            for g in range(BATCH * INNER_TILES):
                for d in (1, 3):
                    times_u(pool, g, d)


def mamba_scan(nc, sems, stage, delta, du, bc, ys, a_log, pick_in, ident_in):
    UNITS = DIRS * STATES
    GROUPS = BATCH * INNER_TILES
    BACK = UNITS - 3 * STATES
    with Mem(nc, stage, sems) as m:
        dl = m.sb("delta", [P, W])
        dus = m.sb("delta_u", [P, DIRS, W])
        bcs = m.sb("bc", [64, 2, W], F32R)
        raw_pick, pick, ident = m.sb("raw_pick", [64, 32]), m.sb("pick", [64, 32], F32R), m.sb("ident", [P, P])
        al, exp_al = m.sb("a_log", [P, INNER_TILES, STATES]), m.sb("exp_a_log", [P, INNER_TILES, STATES])
        a = m.sb("a", [P, STATES])
        decay, c = m.sb("decay", [P, STATES, W]), m.sb("c", [P, STATES, W])
        h, ch = m.sb("h", [P, 4, W]), m.sb("c_h", [P, 4, W])
        state = m.sb("state", [P, UNITS])
        yo = m.sb("y", [P, W])
        b_ps, c_ps, y_ps = m.ps("b", [P, 2, W]), m.ps("c", [P, W]), m.ps("y", [P, W])
        const, pick_ok, exp_a, a_ok = m.sem("const"), m.sem("pick_ok"), m.sem("exp_a"), m.sem("a_ok")
        delta_in, du_in = m.sem("delta_in"), [m.sem(f"du_in{d}") for d in range(DIRS)]
        bc_in = [m.sem("bc_in0"), m.sem("bc_in1")]
        b_filled, driven, scanned = m.sem("b_filled"), m.sem("driven"), m.sem("scanned")
        c_filled, c_ok, decay_ok, kept = m.sem("c_filled"), m.sem("c_ok"), m.sem("decay_ok"), m.sem("kept")
        weighed, summed, y_taken, stored = m.sem("weighed"), m.sem("summed"), m.sem("y_taken"), m.sem("stored")
        held = m.sem("held")
        block = m.block()

        def scanned_at(u0, u): return u0 + (u + 1 + BACK)
        def weighed_at(u0, u): return u0 + (u + 1 + BACK)
        def driven_at(u0, u): return u0 + (u + 1 + UNITS)
        def kept_at(u0, u): return u0 + (u + 1 + UNITS)
        def summed_at(u0, u): return u0 + (u + 1 + 4)

        @block.sync
        def _(sp):
            for dst, src in ((raw_pick, pick_in), (ident, ident_in), (al, a_log)):
                sp.dma_start(dst[:], src).then_inc(const, 16)
            with sp.Fori(0, BATCH) as b:
                for ct in range(INNER_TILES):
                    for q in range(CHUNKS):
                        g = b * INNER_TILES + ct
                        it = g * CHUNKS + q
                        u0 = it * UNITS
                        sp.wait_ge(decay_ok, it * STATES + 1)
                        sp.dma_start(dl[:, :], delta[bass.ds(g, 1), q].rearrange("a p t -> (a p) t")).then_inc(delta_in, 16)
                        sp.dma_start(bcs[:, q % 2, :].bitcast(F32), bc[bass.ds(b, 1), q].rearrange("a p t -> (a p) t")).then_inc(bc_in[q % 2], 16)
                        for d in range(DIRS):
                            sp.wait_ge(driven, driven_at(u0, d * STATES + STATES - 1 - UNITS))
                            sp.dma_start(dus[:, d, :], du[bass.ds(g, 1), q, d].rearrange("a p t -> (a p) t")).then_inc(du_in[d], 16)

        @block.tensor
        def _(pe):
            pe.sem_inc(summed, 4)
            pe.wait_ge(const, 48)
            pe.wait_ge(pick_ok, 1)
            with pe.Fori(0, GROUPS * CHUNKS // 2) as pair:
                for q in range(2):
                    it = pair * 2 + q
                    u0 = it * UNITS

                    def spread(dst, row):
                        ones = pick[:, row:row + 1].to_broadcast((64, P))
                        for k in range(2):
                            ins = pe.matmul(dst[:, k * TW:(k + 1) * TW], ones, bcs[:, q, k * TW:(k + 1) * TW], start=True, stop=True)
                        return ins

                    def spread_b(u):
                        pe.wait_ge(scanned, scanned_at(u0, u - 2))
                        spread(b_ps[:, u % 2, :], u % STATES).then_inc(b_filled, 1)

                    def spread_c(n):
                        pe.wait_ge(c_ok, it * STATES + (n + 1))
                        spread(c_ps, STATES + n).then_inc(c_filled, 1)

                    def add_up(u):
                        pe.wait_ge(weighed, weighed_at(u0, u))
                        if u % STATES == 0:
                            pe.wait_ge(y_taken, it * DIRS + (u // STATES + 1))
                        for k in range(2):
                            ins = pe.matmul(y_ps[:, k * TW:(k + 1) * TW], ident[:, :], ch[:, u % 4, k * TW:(k + 1) * TW],
                                            start=(u % STATES == 0), stop=(u % STATES == STATES - 1))
                        ins.then_inc(summed, 1)

                    pe.wait_ge(bc_in[q], pair * 16 + 16)
                    spread_b(0)
                    spread_c(0)
                    spread_b(1)
                    spread_c(1)
                    for u in range(0, UNITS, 2):
                        for v in (u + 2, u + 3):
                            if v < UNITS:
                                spread_b(v)
                        for v in (u - 2, u - 1):
                            if v + 4 < STATES:
                                spread_c(v + 4)
                            if v >= 0:
                                add_up(v)
                    add_up(UNITS - 2)
                    add_up(UNITS - 1)

        @block.scalar
        def _(act):
            for s, credits in ((c_ok, 1), (y_taken, 1), (kept, UNITS), (decay_ok, 1), (stored, 16)):
                act.sem_inc(s, credits)
            act.wait_ge(held, 1)
            act.activation(exp_al[:, :, :], al[:, :, :], ACT.Exp).then_inc(exp_a, 1)
            act.wait_ge(exp_a, 1)
            with act.Fori(0, BATCH) as b:
                for ct in range(INNER_TILES):
                    g = b * INNER_TILES + ct
                    act.wait_ge(decay_ok, g * (CHUNKS * STATES) + 1)
                    act.activation(a[:, :], exp_al[:, ct, :], ACT.Copy, scale=-1.0).then_inc(a_ok, 1)
                    with act.Fori(0, CHUNKS) as q:
                        it = g * CHUNKS + q
                        u0 = it * UNITS

                        def make_decay(n):
                            if n == 0:
                                act.wait_ge(delta_in, it * 16 + 16)
                                act.wait_ge(a_ok, g + 1)
                            act.wait_ge(scanned, scanned_at(u0, 3 * STATES + n - UNITS))
                            act.activation(decay[:, n, :], dl[:, :], ACT.Exp, scale=a[:, n:n + 1]).then_inc(decay_ok, 1)

                        def copy_c(n):
                            act.wait_ge(c_filled, it * STATES + (n + 1))
                            act.wait_ge(weighed, weighed_at(u0, 3 * STATES + n - UNITS))
                            act.activation(c[:, n, :], c_ps[:, :], ACT.Copy).then_inc(c_ok, 1)

                        for n in range(2):
                            make_decay(n)
                            copy_c(n)
                        for n in range(2, 4):
                            make_decay(n)
                        for u in range(UNITS):
                            d, n = u // STATES, u % STATES
                            if u + 4 < STATES:
                                make_decay(u + 4)
                            if u + 2 < STATES:
                                copy_c(u + 2)
                            act.wait_ge(scanned, scanned_at(u0, u))
                            act.activation(state[:, u:u + 1], h[:, u % 4, W - 1:W], ACT.Copy).then_inc(kept, 1)
                            if n == STATES - 1:
                                act.wait_ge(summed, summed_at(u0, u))
                                act.wait_ge(stored, it * 64 + (16 * d + 16))
                                act.activation(yo[:, :], y_ps[:, :], ACT.Copy).then_inc(y_taken, 1)
                                act.wait_ge(y_taken, it * DIRS + (d + 2))
                                act.dma_start(ys[bass.ds(it, 1), d].rearrange("a p t -> (a p) t"), yo[:, :]).then_inc(stored, 16)
            act.wait_ge(stored, 16 * DIRS * CHUNKS * GROUPS + 16)

        @block.vector
        def _(dve):
            dve.sem_inc(scanned, BACK)
            dve.sem_inc(driven, UNITS)
            dve.wait_ge(const, 48)
            dve.tensor_copy(pick[:, :], raw_pick[:, :]).then_inc(pick_ok, 1)
            dve.tensor_scalar(al[:, :, :], al[:, :, :], 80.0, None, ALU.min).then_inc(held, 1)
            with dve.Fori(0, GROUPS) as g:
                for q in range(CHUNKS):
                    it = g * CHUNKS + q
                    u0 = it * UNITS

                    def drive(u):
                        dve.wait_ge(b_filled, u0 + (u + 1))
                        if u % STATES == 0:
                            dve.wait_ge(du_in[u // STATES], it * 16 + 16)
                        both = b_ps[:, u % 2, :]
                        dve.tensor_tensor(both, both, dus[:, u // STATES, :], ALU.mult).then_inc(driven, 1)

                    def scan(u):
                        dve.wait_ge(driven, driven_at(u0, u))
                        if u < STATES:
                            dve.wait_ge(decay_ok, it * STATES + (u + 2))
                        dve.wait_ge(weighed, weighed_at(u0, u - 4))
                        dve.wait_ge(kept, kept_at(u0, u - 4))
                        dve.tensor_tensor_scan(h[:, u % 4, :], decay[:, u % STATES, :], b_ps[:, u % 2, :],
                                               state[:, u:u + 1] if q else 0.0, ALU.mult, ALU.add).then_inc(scanned, 1)

                    for u in range(0, UNITS, 2):
                        drive(u)
                        drive(u + 1)
                        scan(u)
                        scan(u + 1)

        @block.gpsimd
        def _(pool):
            pool.sem_inc(weighed, BACK)
            with pool.Fori(0, GROUPS * CHUNKS) as it:
                u0 = it * UNITS
                for u in range(UNITS):
                    pool.wait_ge(scanned, scanned_at(u0, u))
                    if u < STATES:
                        pool.wait_ge(c_ok, it * STATES + (u + 2))
                    pool.wait_ge(summed, summed_at(u0, u - 4))
                    pool.tensor_tensor(ch[:, u % 4, :], h[:, u % 4, :], c[:, u % STATES, :], ALU.mult).then_inc(weighed, 1)


def mamba_finish(nc, sems, stage, x, x_out, ys, u_img, gates, d_param, ln_w, ln_b, w_out, inner_mean, eps):
    with Mem(nc, stage, sems) as m:
        yd, acc = m.sb("direction", [P, 2, L]), m.sb("acc", [P, INNER_TILES, L])
        xs = m.sb("x", [P, L])
        gs = m.sb("gate", [P, 2, INNER_TILES, TW])
        sq = m.sb("square", [P, 2, INNER_TILES, TW])
        dp, d4 = m.sb("d", [P, INNER_TILES]), m.sb("four_d", [P, INNER_TILES])
        lw, lb, wo = m.sb("ln_w", [P, INNER_TILES]), m.sb("ln_b", [P, INNER_TILES]), m.sb("w_out", [P, INNER_TILES, P])
        mean, epst = m.sb("inner_mean", [P, P]), m.sb("eps", [P, 1])
        std, rstd = m.sb("deviation", [P, 2, TW]), m.sb("reciprocal", [P, 2, TW])
        mean_ps, var_ps, out_ps = m.ps("mean", [P, 2, TW]), m.ps("variance", [P, 2, TW]), m.ps("out", [P, 2, TW])
        const, x_in, own, eps_ok = m.sem("const"), m.sem("x_in"), m.sem("own"), m.sem("eps_ok")
        part_in, part_used = [m.sem("part_in0"), m.sem("part_in1")], m.sem("part_used")
        gate_in = [m.sem("gate_in0"), m.sem("gate_in1")]
        combined, meaned, centred, squared, varied, rooted, gated, outed, added, stored = (m.sem(n) for n in (
            "combined", "meaned", "centred", "squared", "varied", "rooted", "gated", "outed", "added", "stored"))
        block = m.block()
        PARTS = DIRS + 1

        @block.sync
        def _(sp):
            for dst, src in ((dp, d_param), (lw, ln_w), (lb, ln_b), (wo, w_out), (mean, inner_mean)):
                sp.dma_start(dst[:], src).then_inc(const, 16)
            for b in range(BATCH):
                for ct in range(INNER_TILES):
                    g = b * INNER_TILES + ct
                    for d in range(PARTS):
                        k = g * PARTS + d
                        if k >= 2:
                            sp.wait_ge(part_used, k - 1)
                        src = in_chunks(u_img[b, ct]) if d == DIRS else ys[g * CHUNKS:(g + 1) * CHUNKS, d].rearrange("q p t -> p q t")
                        sp.dma_start(in_chunks(yd[:, k % 2, :]), src).then_inc(part_in[k % 2], 16)
                if b:
                    sp.wait_ge(stored, 16 * b)
                sp.dma_start(xs[:, :], x[:, b * L:(b + 1) * L]).then_inc(x_in, 16)
                for t in range(NTB):
                    n = b * NTB + t
                    if n >= 2:
                        sp.wait_ge(gated, (n - 1) * INNER_TILES)
                    sp.dma_start(gs[:, n % 2, :, :], gates[b, :, :, t * TW:(t + 1) * TW].rearrange("c p t -> p c t")).then_inc(gate_in[n % 2], 16)
                sp.wait_ge(added, NTB * (b + 1))
                sp.dma_start(x_out[:, b * L:(b + 1) * L], xs[:, :]).then_inc(stored, 16)
            sp.wait_ge(stored, 16 * BATCH)

        @block.tensor
        def _(pe):
            pe.wait_ge(const, 80)
            for b in range(BATCH):
                pe.wait_ge(combined, INNER_TILES * (b + 1))
                for t in range(NTB):
                    n = b * NTB + t
                    cols = slice(t * TW, (t + 1) * TW)
                    if n >= 2:
                        pe.wait_ge(centred, (n - 1) * INNER_TILES)
                    for ct in range(INNER_TILES):
                        ins = pe.matmul(mean_ps[:, n % 2, :], mean[:, :], acc[:, ct, cols], start=(ct == 0), stop=(ct == INNER_TILES - 1))
                    ins.then_inc(meaned, 1)
                    pe.wait_ge(squared, (n + 1) * INNER_TILES)
                    if n >= 2:
                        pe.wait_ge(rooted, n - 1)
                    for ct in range(INNER_TILES):
                        ins = pe.matmul(var_ps[:, n % 2, :], mean[:, :], sq[:, n % 2, ct, :], start=(ct == 0), stop=(ct == INNER_TILES - 1))
                    ins.then_inc(varied, 1)
                    pe.wait_ge(gated, (n + 1) * INNER_TILES)
                    if n >= 2:
                        pe.wait_ge(added, n - 1)
                    for ct in range(INNER_TILES):
                        ins = pe.matmul(out_ps[:, n % 2, :], wo[:, ct, :], acc[:, ct, cols], start=(ct == 0), stop=(ct == INNER_TILES - 1))
                    ins.then_inc(outed, 1)

        @block.scalar
        def _(act):
            act.wait_ge(eps_ok, 1)
            for n in range(NT):
                t = n % NTB
                if n >= 2:
                    act.wait_ge(varied, n - 1)
                for ct in range(INNER_TILES):
                    act.wait_ge(centred, n * INNER_TILES + ct + 1)
                    act.activation(sq[:, n % 2, ct, :], acc[:, ct, t * TW:(t + 1) * TW], ACT.Square).then_inc(squared, 1)
                act.wait_ge(varied, n + 1)
                act.activation(std[:, n % 2, :], var_ps[:, n % 2, :], ACT.Sqrt, bias=epst[:, :]).then_inc(rooted, 1)

        @block.vector
        def _(dve):
            chain = Chain(dve, own)
            dve.memset(epst[:, :], eps).then_inc(eps_ok, 1)
            dve.wait_ge(const, 80)
            chain.link(dve.tensor_scalar(d4[:, :], dp[:, :], float(DIRS), None, ALU.mult))
            for b in range(BATCH):
                for ct in range(INNER_TILES):
                    g = b * INNER_TILES + ct
                    image = acc[:, ct, :].rearrange("p (a c) -> p a c", c=SIDE)
                    for d in range(PARTS):
                        k = g * PARTS + d
                        if d == 0 and b:
                            dve.wait_ge(outed, NTB * b)
                        dve.wait_ge(part_in[k % 2], 16 * (k // 2 + 1))
                        part = yd[:, k % 2, :]
                        if d == 0:
                            ins = dve.tensor_copy(acc[:, ct, :], part)
                        elif d < DIRS:
                            ins = dve.tensor_tensor(image, image, scan_order(part, d), ALU.add)
                        else:
                            ins = dve.scalar_tensor_tensor(acc[:, ct, :], part, d4[:, ct:ct + 1], acc[:, ct, :], ALU.mult, ALU.add)
                        ins.then_inc(part_used, 1)
                        dve.wait_ge(part_used, k + 1)
                    dve.sem_inc(combined, 1)
                for t in range(NTB):
                    n = b * NTB + t
                    cols = slice(t * TW, (t + 1) * TW)
                    dve.wait_ge(meaned, n + 1)
                    for ct in range(INNER_TILES):
                        dve.tensor_tensor(acc[:, ct, cols], acc[:, ct, cols], mean_ps[:, n % 2, :], ALU.subtract).then_inc(centred, 1)
                    dve.wait_ge(rooted, n + 1)
                    chain.link(dve.reciprocal(rstd[:, n % 2, :], std[:, n % 2, :]))
                    dve.wait_ge(squared, (n + 1) * INNER_TILES)
                    for ct in range(INNER_TILES):
                        v = acc[:, ct, cols]
                        chain.link(dve.scalar_tensor_tensor(v, v, lw[:, ct:ct + 1], rstd[:, n % 2, :], ALU.mult, ALU.mult))
                        if ct == 0:
                            dve.wait_ge(gate_in[n % 2], 16 * (n // 2 + 1))
                        dve.scalar_tensor_tensor(v, v, lb[:, ct:ct + 1], gs[:, n % 2, ct, :], ALU.add, ALU.mult).then_inc(gated, 1)
                    dve.wait_ge(outed, n + 1)
                    if t == 0:
                        dve.wait_ge(x_in, 16 * (b + 1))
                    dve.tensor_tensor(xs[:, cols], out_ps[:, n % 2, :], xs[:, cols], ALU.add).then_inc(added, 1)
def full_attention(nc, sems, stage, xn, x, x_out, wq, wk, wv, ident_in, first_in):
    SCALE = float(P) ** -0.5
    QT, KC = TW // P, L // TW
    UNITS = QT * KC
    BLOCKS = BATCH * NTB
    JOBS = 3 * NTB
    SLOTS = 8
    with Mem(nc, stage, sems) as m:
        xs = m.sb("xn", [P, L])
        w = m.sb("w", [P, 3, P])
        ident, ones = m.sb("ident", [P, P]), m.sb("ones", [P, P])
        raw_first, first = m.sb("raw_first", [P, P]), m.sb("first", [P, P], F32R)
        qh, ql = m.sb("q_high", [P, L], F32R), m.sb("q_low", [P, L], F32R)
        kh, kl = m.sb("k_high", [P, L], F32R), m.sb("k_low", [P, L], F32R)
        qn = m.sb("q_of_maxima", [P, TW], F32R)
        v = m.sb("v", [P, KT, P])
        mx8, mx = m.sb("max_chunks", [P, QT, KC]), m.sb("max", [P, QT])
        mxw = m.sb("max_wide", [P, QT, P])
        shift = m.sb("shift", [P, 2, TW], F32R)
        pt = m.sb("probs", [P, SLOTS, TW])
        acc = m.sb("probs_sum", [P, 2, TW])
        inv, res, o = m.sb("inverse", [P, TW]), m.sb("x", [P, 2, TW]), m.sb("out", [P, 2, TW])
        ps = m.ps("all", [P, 8, TW])
        MAX0, OUT0, SUM = 3, 5, 7
        const, first_ok, ones_ok, entered = m.sem("const"), m.sem("first_ok"), m.sem("ones_ok"), m.sem("entered")
        image_in, filled, copied, taken, own = m.sem("image_in"), m.sem("filled"), m.sem("copied"), m.sem("taken"), m.sem("own")
        fetched = m.sem("fetched")
        max_filled, max_taken, wide_ok = m.sem("max_filled"), m.sem("max_taken"), m.sem("wide_ok")
        turned, shifted = m.sem("turned"), m.sem("shifted")
        scored, expd, weighed, added = m.sem("scored"), m.sem("expd"), m.sem("weighed"), m.sem("added")
        summed, inverted, scaled, done = m.sem("summed"), m.sem("inverted"), m.sem("scaled"), m.sem("done")
        stored = [m.sem("stored0"), m.sem("stored1")]
        res_in = [m.sem("res_in0"), m.sem("res_in1")]
        block = m.block()

        def f(ap):
            return ap.bitcast(F32)

        @block.sync
        def _(sp):
            for s in stored:
                sp.sem_inc(s, 16)
            for n, src in enumerate((wq, wk, wv)):
                sp.dma_start(w[:, n, :], src).then_inc(const, 16)
            sp.dma_start(ident[:, :], ident_in).then_inc(const, 16)
            sp.dma_start(raw_first[:, :], first_in).then_inc(const, 16)
            with sp.Fori(0, BATCH) as b:
                sp.wait_ge(filled, b * JOBS + 1)
                sp.dma_start(xs[:, :], xn[:, bass.ts(b, L)]).then_inc(image_in, 16)
                for j in range(NTB):
                    tokens = bass.ds(b * L + j * TW, TW)
                    sp.wait_ge(done, b * NTB + j + 1 if j < 2 else b * NTB + j)
                    sp.dma_start(res[:, j % 2, :], x[:, tokens]).then_inc(res_in[j % 2], 16)
                    sp.wait_ge(done, b * NTB + j + 2)
                    sp.dma_start(x_out[:, tokens], o[:, j % 2, :]).then_inc(stored[j % 2], 16)
            for s in stored:
                sp.wait_ge(s, 8 * BLOCKS + 16)

        @block.tensor
        def _(pe):
            pe.sem_inc(filled, 1)
            pe.sem_inc(summed, 1)
            pe.wait_ge(const, 80)
            pe.wait_ge(first_ok, 1)
            pe.wait_ge(ones_ok, 1)
            with pe.Fori(0, BATCH) as it:
                pe.wait_ge(image_in, it * 16 + 16)
                n = 0
                for part in range(3):
                    for t in range(NTB):
                        if n >= 4:
                            pe.wait_ge(copied, it * JOBS + (n - 3))
                            if n < 2 * NTB + 4:
                                pe.wait_ge(taken, it * (2 * NTB) + (n - 3))
                        if part < 2:
                            ins = pe.matmul(ps[:, n % 4, :], w[:, part, :], xs[:, t * TW:(t + 1) * TW], start=True, stop=True)
                        else:
                            for k in range(4):
                                tok = (4 * t + k) * P
                                ins = pe.matmul(ps[:, n % 4, k * P:(k + 1) * P], xs[:, tok:tok + P], w[:, 2, :], start=True, stop=True)
                        ins.then_inc(filled, 1)
                        n += 1
                pe.wait_ge(copied, it * JOBS + JOBS)

                def max_unit(row, u, head=False):
                    if u == 0:
                        pe.wait_ge(fetched, row + 1)
                    if u >= 2 or not head:
                        pe.wait_ge(max_taken, row * UNITS + (u - 1))
                    at = slice(u // KC * P, (u // KC + 1) * P)
                    keys = slice(u % KC * TW, (u % KC + 1) * TW)
                    pe.matmul(ps[:, MAX0 + u % 2, :], qn[:, at], kh[:, keys], start=True, stop=True).then_inc(max_filled, 1)

                def turn(row):
                    pe.wait_ge(wide_ok, row + 1)
                    for k in range(QT):
                        ins = pe.matmul(ps[:, MAX0, k * P:(k + 1) * P], mxw[:, k, :], ident[:, :], start=True, stop=True)
                    ins.then_inc(turned, 1)

                def score(row, queries, slot, i, head=False):
                    if i == 0:
                        pe.wait_ge(shifted, row + 1)
                    if i >= 3:
                        pe.wait_ge(expd, row * KT + (i - 2))
                    elif i < 2 and not head:
                        pe.wait_ge(expd, row * KT + (i - 1))
                    bank, keys = ps[:, i % 3, :], slice(i * P, (i + 1) * P)
                    pe.matmul(bank, first[:, :], shift[:, slot, :], start=True, stop=False)
                    pe.matmul(bank, kh[:, keys], qh[:, queries], start=False, stop=False)
                    pe.matmul(bank, kh[:, keys], ql[:, queries], start=False, stop=False)
                    pe.matmul(bank, kl[:, keys], qh[:, queries], start=False, stop=True).then_inc(scored, 1)

                def finish(row, slot):
                    pe.wait_ge(added, row * KT + (KT + SLOTS))
                    pe.wait_ge(inverted, row + 1)
                    pe.matmul(ps[:, SUM, :], ones[:, :], acc[:, slot, :], start=True, stop=True).then_inc(summed, 1)

                def attend(row, start, slot, head=False, tail=False):
                    queries, following = bass.ds(start, TW), bass.ds(start + TW, TW)
                    unit = 0
                    for i in range(KT):
                        if i == 2 and not head:
                            finish(row - 1, 1 - slot)
                        if not tail:
                            while unit < UNITS and unit < (i - 4) * 1.6:
                                max_unit(row + 1, unit)
                                unit += 1
                            if i == KT - 5:
                                turn(row + 1)
                        if i + 2 < KT:
                            score(row, queries, slot, i + 2)
                        elif not tail and i == KT - 2:
                            score(row + 1, following, 1 - slot, 0)
                        pe.wait_ge(expd, row * KT + (i + 1))
                        if i == 0:
                            pe.wait_ge(scaled, row + 1)
                        pe.matmul(ps[:, OUT0 + slot, :], v[:, i, :], pt[:, i % SLOTS, :], start=(i == 0), stop=(i == KT - 1)).then_inc(weighed, 1)
                    if tail:
                        finish(row, slot)
                    else:
                        score(row + 1, following, 1 - slot, 1)

                row0 = it * NTB
                for u in range(UNITS):
                    max_unit(row0, u, head=True)
                turn(row0)
                for i in range(2):
                    score(row0, slice(0, TW), 0, i, head=True)
                attend(row0, 0, 0, head=True)
                pe.sem_inc(entered, 1)
                with pe.Fori(0, NTB // 2 - 1) as jj:
                    for k in (1, 2):
                        attend(row0 + jj * 2 + k, jj * (2 * TW) + k * TW, k % 2)
                attend(row0 + (NTB - 1), (NTB - 1) * TW, 1, tail=True)

        @block.scalar
        def _(act):
            with act.Fori(0, BATCH) as it:
                for n in range(JOBS):
                    part, t = n // NTB, n % NTB
                    act.wait_ge(filled, it * JOBS + (n + 2))
                    cols, bank = slice(t * TW, (t + 1) * TW), ps[:, n % 4, :]
                    if part == 0:
                        ins = act.activation(qh[:, cols], bank, ACT.Copy)
                    elif part == 1:
                        ins = act.activation(kh[:, cols], bank, ACT.Copy, scale=SCALE)
                    else:
                        ins = act.activation(v[:, 4 * t:4 * t + 4, :], bank.rearrange("p (t d) -> p t d", d=P), ACT.Copy)
                    ins.then_inc(copied, 1)
                act.sem_inc(entered, 1)
                with act.Fori(0, NTB) as j:
                    tile0 = it * (NTB * KT) + j * KT
                    for i in range(KT):
                        act.wait_ge(scored, tile0 + (i + 1))
                        if i >= SLOTS:
                            act.wait_ge(weighed, tile0 + (i + 1 - SLOTS))
                        act.wait_ge(added, tile0 + (i + 1))
                        act.activation(pt[:, i % SLOTS, :], ps[:, i % 3, :], ACT.Exp).then_inc(expd, 1)

        @block.gpsimd
        def _(pool):
            pool.sem_inc(added, SLOTS)
            pool.sem_inc(summed, 1)
            with pool.Fori(0, BLOCKS // 2) as pair:
                for slot in range(2):
                    row = pair * 2 + slot
                    for i in range(1, KT):
                        pool.wait_ge(expd, row * KT + (i + 1))
                        if i == 1:
                            pool.wait_ge(summed, row + 1)
                            pool.tensor_tensor(acc[:, slot, :], pt[:, 0, :], pt[:, 1, :], ALU.add).then_inc(added, 2)
                        else:
                            pool.wait_ge(added, row * KT + (i + SLOTS))
                            pool.tensor_tensor(acc[:, slot, :], acc[:, slot, :], pt[:, i % SLOTS, :], ALU.add).then_inc(added, 1)

        @block.vector
        def _(dve):
            dve.sem_inc(scaled, 2)
            for s in (inverted, done):
                dve.sem_inc(s, 1)
            dve.memset(ones[:, :], 1.0).then_inc(ones_ok, 1)
            dve.wait_ge(const, 80)
            dve.tensor_copy(first[:, :], raw_first[:, :]).then_inc(first_ok, 1)
            with dve.Fori(0, BATCH) as it:
                for n in range(2 * NTB):
                    t = n % NTB
                    high, low, scale = (qh, ql, 1.0) if n < NTB else (kh, kl, SCALE)
                    dve.wait_ge(copied, it * JOBS + (n + 1))
                    cols, bank = slice(t * TW, (t + 1) * TW), n % 4
                    dve.scalar_tensor_tensor(low[:, cols], ps[:, bank, :], scale, f(high[:, cols]), ALU.mult, ALU.subtract).then_inc(taken, 1)

                def fetch(start):
                    dve.tensor_copy(qn[:, :], f(qh[:, start:start + TW])).then_inc(fetched, 1)

                def find_shift(row, j):
                    for u in range(UNITS):
                        dve.wait_ge(max_filled, row * UNITS + (u + 1))
                        dve.tensor_reduce(mx8[:, u // KC, u % KC:u % KC + 1], ps[:, MAX0 + u % 2, :], AX.X, ALU.max).then_inc(max_taken, 1)
                    dve.wait_ge(max_taken, row * UNITS + UNITS)
                    dve.tensor_reduce(mx[:, :], mx8[:, :, :], AX.X, ALU.max).then_inc(own, 1)
                    dve.wait_ge(own, row + 1)
                    dve.tensor_copy(mxw[:, :, :], mx[:, :].rearrange("p (t a) -> p t a", a=1).to_broadcast((P, QT, P))).then_inc(wide_ok, 1)
                    dve.wait_ge(turned, row + 1)
                    dve.tensor_scalar(shift[:, j % 2, :], ps[:, MAX0, :], -1.0, None, ALU.mult).then_inc(shifted, 1)
                    if j + 1 < NTB:
                        fetch((j + 1) * TW)

                def divide(row, j):
                    slot = j % 2
                    dve.wait_ge(summed, row + 3)
                    dve.reciprocal(inv[:, :], ps[:, SUM, :]).then_inc(inverted, 1)
                    dve.wait_ge(inverted, row + 2)
                    dve.wait_ge(weighed, row * KT + KT)
                    dve.wait_ge(stored[slot], 8 * NTB * it + 16 * (j // 2 + 1))
                    dve.tensor_tensor(o[:, slot, :], ps[:, OUT0 + slot, :], inv[:, :], ALU.mult).then_inc(scaled, 1)
                    dve.wait_ge(scaled, row + 3)
                    dve.wait_ge(res_in[slot], 8 * NTB * it + 16 * (j // 2 + 1))
                    dve.tensor_tensor(o[:, slot, :], o[:, slot, :], res[:, slot, :], ALU.add).then_inc(done, 1)

                dve.wait_ge(copied, it * JOBS + JOBS)
                fetch(0)
                find_shift(it * NTB, 0)
                dve.sem_inc(entered, 1)
                for j in range(NTB):
                    row = it * NTB + j
                    if j + 1 < NTB:
                        find_shift(row + 1, j + 1)
                    divide(row, j)
RANGES = 4


def spectral_prepare(nc, sems, stage, xn, x, y0, u_tok, scales, logits_in, gumbel_in, sigma_in, m_u, ident_in, exchange_in, rank_in):
    TAPS, K = 3, 16
    with Mem(nc, stage, sems) as m:
        pad = TAPS - 1
        xs = m.sb("xn", [P, BATCH, L + pad])
        y = m.sb("y", [P, TOK])
        ident, mu, mr = m.sb("ident", [P, P]), m.sb("m_u", [P, 4, TAPS * P]), m.sb("m_range", [P, RANGES, TAPS * P])
        ut, exchange = m.sb("u_tok", [P, TOK]), m.sb("exchange", [P, P])
        flipped, reversed_ok = m.sem("flipped"), m.sem("reversed_ok")
        z, e4, soft, hard, key, rank = (m.sb(n, [P, 4]) for n in ("logits", "exp", "soft", "hard", "key", "rank"))
        g4, sg, sc = m.sb("gumbel", [P, 4]), m.sb("sigma", [P, K]), m.sb("scales", [P, K + 1, 4])
        root, root2 = m.sb("root", [P, K]), m.sb("root_of_root", [P, K])
        tr_ps, ar_ps = m.ps("turned", [P, 4, TW]), m.ps("auto", [P, 2, TW])
        loaded, padded, own, own_act = m.sem("loaded"), m.sem("padded"), m.sem("own"), m.sem("own_act")
        shifted, expd, rooted = m.sem("shifted"), m.sem("expd"), m.sem("rooted")
        turned, copied, ranged, auto, added, stored, scales_ok = (
            m.sem(n) for n in ("turned", "copied", "ranged", "auto", "added", "stored", "scales_ok"))
        block = m.block()
        LOADS = 16 * 10

        @block.sync
        def _(sp):
            for dst, src in ((ident, ident_in), (exchange, exchange_in), (mu, m_u), (z, logits_in), (g4, gumbel_in), (sg, sigma_in), (rank, rank_in), (y, x)):
                sp.dma_start(dst[:], src).then_inc(loaded, 16)
            for b in range(BATCH):
                sp.dma_start(xs[:, b, pad:], xn[:, b * L:(b + 1) * L]).then_inc(loaded, 16)
            sp.wait_ge(reversed_ok, NT)
            sp.dma_start(u_tok, ut[:, :]).then_inc(stored, 16)
            sp.wait_ge(scales_ok, 1)
            sp.dma_start(scales, sc[:, :, :]).then_inc(stored, 16)
            sp.wait_ge(added, NT)
            sp.dma_start(y0, y[:, :]).then_inc(stored, 16)
            sp.wait_ge(stored, 48)

        @block.tensor
        def _(pe):
            pe.wait_ge(loaded, LOADS)
            for t in range(NT):
                if t >= 4:
                    pe.wait_ge(copied, t - 3)
                for k in range(4):
                    n = 4 * t + k
                    b, par, j = n // 32, n // 16 % 2, n % 16
                    first = pad + 2 * P * j + par
                    ins = pe.matmul(tr_ps[:, t % 4, k * P:(k + 1) * P], xs[:, b, first:first + 2 * P - 1:2], ident[:, :], start=True, stop=True)
                ins.then_inc(turned, 1)
            for t in range(NT):
                pe.wait_ge(copied, t + 1)
                if t >= 2:
                    pe.wait_ge(reversed_ok, t - 1)
                pe.matmul(ar_ps[:, t % 2, :], exchange[:, :], ut[:, t * TW:(t + 1) * TW], start=True, stop=True).then_inc(flipped, 1)
            pe.wait_ge(reversed_ok, NT)
            pe.wait_ge(ranged, 1)
            pe.wait_ge(padded, 1)
            for t in range(NT):
                b, tile = t // NTB, t % NTB
                r = (0, 1, 2, 2, 3, 3, 3, 3)[tile]
                if t >= 2:
                    pe.wait_ge(added, t - 1)
                for tap in range(TAPS):
                    first = pad + tile * TW - tap
                    ins = pe.matmul(ar_ps[:, t % 2, :], mr[:, r, tap * P:(tap + 1) * P], xs[:, b, first:first + TW],
                                    start=(tap == 0), stop=(tap == TAPS - 1))
                ins.then_inc(auto, 1)

        @block.scalar
        def _(act):
            act.wait_ge(loaded, LOADS)
            act.activation(root[:, :], sg[:, :], ACT.Sqrt).then_inc(own_act, 1)
            act.wait_ge(own_act, 1)
            act.activation(root2[:, :], root[:, :], ACT.Sqrt).then_inc(rooted, 1)
            act.wait_ge(shifted, 1)
            act.activation(e4[:, :], z[:, :], ACT.Exp).then_inc(expd, 1)

        @block.vector
        def _(dve):
            chain = Chain(dve, own)
            dve.memset(xs[:, :, 0:pad], 0.0).then_inc(padded, 1)
            dve.wait_ge(loaded, LOADS)
            chain.link(dve.tensor_tensor(z[:, :], z[:, :], g4[:, :], ALU.add))
            chain.link(dve.tensor_reduce(key[:, 0:1], z[:, :], AX.X, ALU.max))
            dve.tensor_scalar(z[:, :], z[:, :], key[:, 0:1], None, ALU.subtract).then_inc(shifted, 1)
            dve.wait_ge(expd, 1)
            chain.link(dve.tensor_reduce(key[:, 0:1], e4[:, :], AX.X, ALU.add))
            chain.link(dve.reciprocal(key[:, 1:2], key[:, 0:1]))
            chain.link(dve.tensor_scalar(soft[:, :], e4[:, :], key[:, 1:2], None, ALU.mult))
            chain.link(dve.tensor_reduce(g4[:, 0:1], soft[:, :], AX.X, ALU.max))
            chain.link(dve.tensor_scalar(hard[:, :], soft[:, :], g4[:, 0:1], None, ALU.is_equal))
            chain.link(dve.tensor_tensor(key[:, :], hard[:, :], rank[:, :], ALU.mult))
            chain.link(dve.tensor_reduce(g4[:, 1:2], key[:, :], AX.X, ALU.max))
            chain.link(dve.tensor_scalar(hard[:, :], key[:, :], g4[:, 1:2], None, ALU.is_equal))
            chain.link(dve.tensor_tensor(hard[:, :], hard[:, :], soft[:, :], ALU.subtract))
            chain.link(dve.tensor_tensor(sc[:, K, :], hard[:, :], soft[:, :], ALU.add))
            dve.wait_ge(rooted, 1)
            for i in range(4):
                chain.step(dve.tensor_scalar(sc[:, 0:K, i], root2[:, :], sc[:, K, i:i + 1], None, ALU.mult))
            chain.done()
            dve.sem_inc(scales_ok, 1)
            chain.link(dve.tensor_scalar(mr[:, 3, :], mu[:, 0, :], sc[:, K, 0:1], None, ALU.mult))
            for i in range(1, 4):
                ins = dve.scalar_tensor_tensor(mr[:, 3 - i, :], mu[:, i, :], sc[:, K, i:i + 1], mr[:, 4 - i, :], ALU.mult, ALU.add)
                if i < 3:
                    chain.link(ins)
            ins.then_inc(ranged, 1)
            for t in range(NT):
                dve.wait_ge(turned, t + 1)
                dve.tensor_copy(ut[:, t * TW:(t + 1) * TW], tr_ps[:, t % 4, :]).then_inc(copied, 1)
            for t in range(NT):
                dve.wait_ge(flipped, t + 1)
                dve.tensor_copy(ut[:, t * TW:(t + 1) * TW], ar_ps[:, t % 2, :]).then_inc(reversed_ok, 1)
            for t in range(NT):
                dve.wait_ge(auto, t + 1)
                part = y[:, t * TW:(t + 1) * TW]
                dve.tensor_tensor(part, ar_ps[:, t % 2, :], part, ALU.add).then_inc(added, 1)


def spectral(nc, sems, stage, u_tok, y0, y_out, scales_in, phi, m_phi):
    K, HALF = 16, L // 2
    CHUNKS, BLOCKS = HALF // TW, HALF // P
    ODD = HALF
    WIDTH = 2 * HALF + 1
    YJOBS = BATCH * CHUNKS * 2
    LINKS = 5 + 8
    with Mem(nc, stage, sems) as m:
        uh, ul = m.sb("u_high", [P, TOK], F32R), m.sb("u_low", [P, TOK], F32R)
        raw = m.sb("toeplitz", [P, WIDTH])
        th, tl = m.sb("toeplitz_high", [P, 2, WIDTH], F32R), m.sb("toeplitz_low", [P, 2, WIDTH], F32R)
        y = m.sb("y", [P, TOK])
        mraw, meff = m.sb("m_phi", [P, 2, 4 * P]), m.sb("m_range", [P, 2, RANGES, 2, P])
        pq = m.sb("sum_and_difference", [P, 4, 2, P])
        sc, sk = m.sb("scales", [P, (K + 1) * 4]), m.sb("scales_k", [P, 4])
        a = m.sb("filtered", [P, 4, TW])
        ps = m.ps("all", [P, 6, TW])
        loaded, u_in, u_split, own = m.sem("loaded"), m.sem("u_in"), m.sem("u_split"), m.sem("own")
        t_in, m_in, piece_done, matrices = m.sem("t_in"), m.sem("m_in"), m.sem("piece_done"), m.sem("matrices")
        convolved, taken, mixed, added, stored = (m.sem(n) for n in ("convolved", "taken", "mixed", "added", "stored"))
        entered = m.sem("entered")
        block = m.block()

        def f(ap):
            return ap.bitcast(F32)

        def pieces():
            return [slice(i * TW, (i + 1) * TW if i < 7 else WIDTH) for i in range(8)]

        @block.sync
        def _(sp):
            sp.dma_start(sc[:, :], scales_in).then_inc(loaded, 16)
            sp.dma_start(y[:, :], y0).then_inc(loaded, 16)
            for half in range(2):
                if half:
                    sp.wait_ge(u_split, 1)
                sp.dma_start(raw[:, 0:2 * HALF], u_tok[:, half * 2 * HALF:(half + 1) * 2 * HALF]).then_inc(u_in, 16)
            sp.wait_ge(u_split, 2)
            with sp.Fori(0, K) as k:
                sp.wait_ge(piece_done, k * 8 + 1)
                row = phi[bass.ds(k, 1), :]
                for first, count, dst in ((0, HALF, raw[:, 0:HALF]), (HALF + P, HALF + 1, raw[:, HALF:WIDTH])):
                    sp.dma_start(dst, bass.AP(row.tensor, row.offset + first, [[1, P], [1, count]])).then_inc(t_in, 16)
                sp.wait_ge(matrices, k + 1)
                sp.dma_start(mraw[:, :, :], m_phi[bass.ts(k, P), :]).then_inc(m_in, 16)
            sp.wait_ge(added, K * YJOBS + 1)
            sp.dma_start(y_out, y[:, :]).then_inc(stored, 16)
            sp.wait_ge(stored, 16)

        @block.tensor
        def _(pe):
            pe.wait_ge(u_split, 2)
            with pe.Fori(0, K // 2) as kk:
                for s in range(2):
                    k8, k1 = kk * 16 + s * 8, kk * 2 + s
                    job0, y0job = (kk * 2 + s) * 2 * YJOBS + 1, (kk * 2 + s) * YJOBS + 1
                    pe.wait_ge(piece_done, k8 + 9)

                    def conv(n):
                        b, c, par, kind = n // 16, n // 4 % 4, n // 2 % 2, n % 2
                        src = par if kind == 0 else 1 - par
                        t0 = 0 if kind == 0 else ODD + par
                        pe.wait_ge(taken, job0 + (n - 3) if n >= 4 else job0)
                        for j in range(4 * c + 4):
                            lag = TW * c - P * j
                            skip = max(0, -lag)
                            at_u = slice(((b * 2 + src) * BLOCKS + j) * P, ((b * 2 + src) * BLOCKS + j + 1) * P)
                            cols = slice(t0 + lag + skip, t0 + lag + TW)
                            o = ps[:, n % 4, skip:TW]
                            for q, (uu, tt) in enumerate(((uh, th), (uh, tl), (ul, th))):
                                ins = pe.matmul(o, uu[:, at_u], tt[:, s, cols], start=(j == 0 and q == 0), stop=(j == 4 * c + 3 and q == 2))
                        ins.then_inc(convolved, 1)

                    def mix(i):
                        b, c, par = i // 8, i // 2 % 4, i % 2
                        pe.wait_ge(taken, job0 + (2 * i + 2))
                        if i == 0:
                            pe.wait_ge(matrices, k1 + 2)
                        pe.wait_ge(added, y0job + (i - 1) if i >= 2 else y0job)
                        spans = [(0, 0, 256), (1, 256, 512)] if c == 0 else [(2 if c == 1 else 3, 0, TW)]
                        for r, lo, hi in spans:
                            for kind in range(2):
                                ins = pe.matmul(ps[:, 4 + i % 2, lo:hi], meff[:, s, r, kind, :], a[:, (2 * i + kind) % 4, lo:hi],
                                                start=(kind == 0), stop=(kind == 1))
                        ins.then_inc(mixed, 1)

                    for i in range(YJOBS + 1):
                        if i < YJOBS:
                            conv(2 * i)
                            conv(2 * i + 1)
                        if i >= 1:
                            mix(i - 1)

        @block.scalar
        def _(act):
            act.sem_inc(taken, 1)
            with act.Fori(0, K) as k:
                for n in range(2 * YJOBS):
                    act.wait_ge(convolved, k * 2 * YJOBS + (n + 1))
                    if n >= 4:
                        act.wait_ge(mixed, k * YJOBS + (n // 2 - 1))
                    act.activation(a[:, n % 4, :], ps[:, n % 4, :], ACT.Copy).then_inc(taken, 1)

        @block.vector
        def _(dve):
            for s in (piece_done, matrices, added):
                dve.sem_inc(s, 1)
            for half in range(2):
                dve.wait_ge(u_in, 16 * (half + 1))
                cols = slice(half * 2 * HALF, (half + 1) * 2 * HALF)
                dve.tensor_copy(uh[:, cols], raw[:, 0:2 * HALF]).then_inc(own, 1)
                dve.wait_ge(own, half + 1)
                dve.tensor_tensor(ul[:, cols], raw[:, 0:2 * HALF], f(uh[:, cols]), ALU.subtract).then_inc(u_split, 1)
            dve.wait_ge(loaded, 32)

            def split(k, s, i):
                cols = pieces()[i]
                if i == 0:
                    dve.wait_ge(t_in, k * 32 + 32)
                dve.tensor_copy(th[:, s, cols], raw[:, cols]).then_inc(own, 1)
                dve.wait_ge(own, k * LINKS + (3 + i))
                dve.tensor_tensor(tl[:, s, cols], raw[:, cols], f(th[:, s, cols]), ALU.subtract).then_inc(piece_done, 1)

            def combine(k, s):
                base = k * LINKS + 2 + 8
                dve.wait_ge(m_in, k * 16 + 16)
                plus = mraw[:, 0, :].rearrange("p (i e) -> p i e", e=P)
                minus = mraw[:, 1, :].rearrange("p (i e) -> p i e", e=P)
                dve.tensor_copy(sk[:, :], sc[:, bass.ts(k, 4)]).then_inc(own, 1)
                dve.tensor_tensor(pq[:, :, 0, :], plus, minus, ALU.add)
                dve.tensor_tensor(pq[:, :, 1, :], plus, minus, ALU.subtract).then_inc(own, 1)
                dve.wait_ge(own, base + 2)
                dve.tensor_scalar(meff[:, s, 3, :, :], pq[:, 0, :, :], sk[:, 0:1], None, ALU.mult).then_inc(own, 1)
                for i in range(1, 4):
                    dve.wait_ge(own, base + 2 + i)
                    ins = dve.scalar_tensor_tensor(meff[:, s, 3 - i, :, :], pq[:, i, :, :], sk[:, i:i + 1], meff[:, s, 4 - i, :, :], ALU.mult, ALU.add)
                    ins.then_inc(own if i < 3 else matrices, 1)

            def add(k, i):
                b, c, par = i // 8, i // 2 % 4, i % 2
                dve.wait_ge(mixed, k * YJOBS + (i + 1))
                part = y[:, :].rearrange("p (b a two) -> p b two a", b=BATCH, two=2)[:, b, par, c * TW:(c + 1) * TW]
                dve.tensor_tensor(part, ps[:, 4 + i % 2, :], part, ALU.add).then_inc(added, 1)

            for i in range(8):
                split(0, 0, i)
            combine(0, 0)

            def filter_sums(k, s, last):
                for i in range(YJOBS):
                    add(k, i)
                    if not last and i % 2 == 0:
                        split(k + 1, 1 - s, i // 2)
                if not last:
                    combine(k + 1, 1 - s)

            with dve.Fori(0, K // 2 - 1) as kk:
                for s in range(2):
                    filter_sums(kk * 2 + s, s, False)
            filter_sums(K - 2, 0, False)
            filter_sums(K - 1, 1, True)
def linear_attention(nc, sems, stage, xn, x, x_out, wk_t, wq, wv_t, ident_in):
    H, KQ = 8, 64
    with Mem(nc, stage, sems) as m:
        xs, res = m.sb("xn", [P, TOK]), m.sb("x", [P, TOK])
        ident, wks, wvs = m.sb("ident", [P, P]), m.sb("wk", [P, H * KQ]), m.sb("wv", [P, H * P])
        wqs = m.sb("wq", [KQ, H, P])
        xt = m.sb("xn_by_token", [P, 4, P])
        gram = m.sb("gram", [P, P])
        kg = m.sb("keys_gram", [P, H * KQ])
        ktv = m.sb("ktv", [KQ, H, P])
        mix = m.sb("mix", [P, BATCH, P])
        tr_ps, gram_ps = m.ps("transposed", [P, 4, TW]), m.ps("gram", [P, TW])
        kg_ps, ktv_ps = m.ps("keys_gram", [P, TW]), m.ps("ktv", [KQ, TW])
        mix_ps = m.ps("mix", [P, TW])
        loaded, own_pe, turned, copied, grammed = (m.sem(n) for n in ("loaded", "own_pe", "turned", "copied", "grammed"))
        gram_ok, kg_done, kg_ok, ktv_done, ktv_ok, mixed, mix_ok = (
            m.sem(n) for n in ("gram_ok", "kg_done", "kg_ok", "ktv_done", "ktv_ok", "mixed", "mix_ok"))
        outed, added, stored = m.sem("outed"), m.sem("added"), m.sem("stored")
        block = m.block()

        @block.sync
        def _(sp):
            for dst, src in ((ident, ident_in), (wks, wk_t), (wvs, wv_t), (wqs, wq), (xs, xn), (res, x)):
                sp.dma_start(dst[:], src).then_inc(loaded, 16)
            for b in range(BATCH):
                sp.wait_ge(added, NTB * (b + 1))
                sp.dma_start(x_out[:, b * L:(b + 1) * L], res[:, b * L:(b + 1) * L]).then_inc(stored, 16)
            sp.wait_ge(stored, 16 * BATCH)

        @block.tensor
        def _(pe):
            pe.wait_ge(loaded, 96)
            for b in range(BATCH):
                for t in range(KT + 1):
                    n = b * KT + t
                    if t < KT:
                        if n >= 4:
                            pe.wait_ge(copied, n - 3)
                        pe.transpose(tr_ps[:, n % 4, 0:P], xs[:, b * L + t * P:b * L + (t + 1) * P], ident[:, :]).then_inc(turned, 1)
                    if t >= 1:
                        u = n - 1
                        pe.wait_ge(copied, u + 1)
                        if t == 1 and b:
                            pe.wait_ge(gram_ok, b)
                        pe.matmul(gram_ps[:, 0:P], xt[:, u % 4, :], xt[:, u % 4, :],
                                  start=(t == 1), stop=(t == KT)).then_inc(grammed, 1)
                pe.wait_ge(gram_ok, b + 1)
                pe.matmul(kg_ps[:, :], gram[:, :], wks[:, :], start=True, stop=True).then_inc(kg_done, 1)
                pe.wait_ge(kg_ok, b + 1)
                for h in range(H):
                    if h % 4 == 0 and (h or b):
                        pe.wait_ge(ktv_ok, 2 * b + h // 4)
                    pe.matmul(ktv_ps[:, (h % 4) * P:(h % 4 + 1) * P], kg[:, h * KQ:(h + 1) * KQ], wvs[:, h * P:(h + 1) * P],
                              start=True, stop=True).then_inc(ktv_done, 1)
                pe.wait_ge(ktv_ok, 2 * b + 2)
                for h in range(H):
                    pe.matmul(mix_ps[:, 0:P], wqs[:, h, :], ktv[:, h, :], start=(h == 0), stop=(h == H - 1)).then_inc(mixed, 1)
                pe.wait_ge(mix_ok, b + 1)
                for t in range(NTB):
                    n = b * NTB + t
                    pe.wait_ge(copied, KT * (b + 1))
                    if n >= 4:
                        pe.wait_ge(added, n - 3)
                    pe.matmul(tr_ps[:, n % 4, :], mix[:, b, :], xs[:, n * TW:(n + 1) * TW], start=True, stop=True).then_inc(outed, 1)
                if b + 1 < BATCH:
                    pe.wait_ge(added, NTB * (b + 1))

        @block.vector
        def _(dve):
            dve.wait_ge(loaded, 96)
            for b in range(BATCH):
                for t in range(KT):
                    n = b * KT + t
                    dve.wait_ge(turned, n + 1)
                    if n >= 4:
                        dve.wait_ge(grammed, n - 3)
                    dve.tensor_copy(xt[:, n % 4, :], tr_ps[:, n % 4, 0:P]).then_inc(copied, 1)
                dve.wait_ge(grammed, KT * (b + 1))
                dve.tensor_copy(gram[:, :], gram_ps[:, 0:P]).then_inc(gram_ok, 1)
                dve.wait_ge(kg_done, b + 1)
                dve.tensor_copy(kg[:, :], kg_ps[:, :]).then_inc(kg_ok, 1)
                for g in range(2):
                    dve.wait_ge(ktv_done, H * b + 4 * g + 4)
                    dve.tensor_copy(ktv[:, 4 * g:4 * g + 4, :], ktv_ps[:, :].rearrange("p (h e) -> p h e", e=P)).then_inc(ktv_ok, 1)
                dve.wait_ge(mixed, H * (b + 1))
                dve.tensor_copy(mix[:, b, :], mix_ps[:, 0:P]).then_inc(mix_ok, 1)
                for t in range(NTB):
                    n = b * NTB + t
                    dve.wait_ge(outed, n + 1)
                    part = res[:, n * TW:(n + 1) * TW]
                    dve.tensor_tensor(part, tr_ps[:, n % 4, :], part, ALU.add).then_inc(added, 1)


def experts(nc, sems, stage, xn, x, out, router_w, router_b, expert_w, expert_b, ident_in, rank_in):
    E, BLK = 8, TOK // P
    with Mem(nc, stage, sems) as m:
        xs, res = m.sb("xn", [P, TOK]), m.sb("x", [P, TOK])
        ident, rw, ew = m.sb("ident", [P, P]), m.sb("router_w", [P, E]), m.sb("expert_w", [P, E * P])
        eb, rb, rank = m.sb("expert_b", [1, E * P]), m.sb("router_b", [P, E]), m.sb("rank", [P, E])
        ones = m.sb("ones", [1, P])
        pr = m.sb("probs", [P, BLK, E])
        rest, hit, key, gate = (m.sb(n, [P, BLK, E]) for n in ("rest", "hit", "key", "gate"))
        top1, top2, best, tot, inv = (m.sb(n, [P, BLK, 1]) for n in ("top1", "top2", "best", "total", "inverse"))
        acc = m.sb("acc", [P, 4, P])
        lg_ps = m.ps("logits", [P, TW])
        ex_ps = m.ps("expert_out", [P, 2, 2 * TW])
        xt_ps = m.ps("x_by_token", [P, 2, TW])
        loaded, own, own_act = m.sem("loaded"), m.sem("own"), m.sem("own_act")
        logits, gated, shifted, expd, mixed, turned, accd, stored = (
            m.sem(n) for n in ("logits", "gated", "shifted", "expd", "mixed", "turned", "accd", "stored"))
        chain_acc, one_set = m.sem("chain_acc"), m.sem("one_set")
        slot_stored = [m.sem(f"slot_stored{i}") for i in range(4)]
        block = m.block()

        @block.sync
        def _(sp):
            loads = ((ident, ident_in), (rw, router_w), (ew, expert_w), (eb, expert_b), (rb, router_b),
                     (rank, rank_in), (xs, xn), (res, x))
            for dst, src in loads:
                sp.dma_start(dst[:], src).then_inc(loaded, 16)
            for t in range(BLK):
                sp.wait_ge(accd, t + 1)
                sp.dma_start(out[t * P:(t + 1) * P, :], acc[:, t % 4, :]).then_inc(slot_stored[t % 4], 16)
            for i in range(4):
                sp.wait_ge(slot_stored[i], 16 * BLK // 4)

        @block.tensor
        def _(pe):
            pe.wait_ge(loaded, 128)
            pe.wait_ge(one_set, 1)
            for t in range(BLK):
                ins = pe.matmul(lg_ps[:, t * E:(t + 1) * E], xs[:, t * P:(t + 1) * P], rw[:, :], start=True, stop=True)
            ins.then_inc(logits, 1)
            for t in range(BLK):
                if t >= 2:
                    pe.wait_ge(accd, t - 1)
                for half in range(2):
                    o = ex_ps[:, t % 2, half * TW:(half + 1) * TW]
                    pe.matmul(o, xs[:, t * P:(t + 1) * P], ew[:, half * TW:(half + 1) * TW], start=True, stop=False)
                    pe.matmul(o, ones[:, :], eb[:, half * TW:(half + 1) * TW], start=False, stop=True)
                pe.transpose(xt_ps[:, t % 2, 0:P], res[:, t * P:(t + 1) * P], ident[:, :]).then_inc(mixed, 1)

        @block.scalar
        def _(act):
            act.wait_ge(shifted, 1)
            act.activation(pr[:, :, :], rest[:, :, :], ACT.Exp).then_inc(expd, 1)

        @block.vector
        def _(dve):
            own_chain = Chain(dve, own)
            dve.memset(ones[:, :], 1.0).then_inc(one_set, 1)
            dve.wait_ge(loaded, 128)
            dve.wait_ge(logits, 1)

            def wide(a):
                return a[:, :, :].to_broadcast((P, BLK, E))

            lg = lg_ps[:, :].rearrange("p (t e) -> p t e", e=E)
            rbw = rb[:, :].rearrange("p (a e) -> p a e", a=1).to_broadcast((P, BLK, E))
            rkw = rank[:, :].rearrange("p (a e) -> p a e", a=1).to_broadcast((P, BLK, E))
            own_chain.link(dve.tensor_tensor(pr[:, :, :], lg, rbw, ALU.add))
            own_chain.link(dve.tensor_reduce(best[:, :, :], pr[:, :, :], AX.X, ALU.max))
            dve.tensor_tensor(rest[:, :, :], pr[:, :, :], wide(best), ALU.subtract).then_inc(shifted, 1)
            dve.wait_ge(expd, 1)
            own_chain.link(dve.tensor_copy(rest[:, :, :], pr[:, :, :]))
            for n, top in enumerate((top1, top2)):
                own_chain.link(dve.tensor_reduce(top[:, :, :], rest[:, :, :], AX.X, ALU.max))
                own_chain.link(dve.tensor_tensor(hit[:, :, :], rest[:, :, :], wide(top), ALU.is_equal))
                own_chain.link(dve.tensor_tensor(key[:, :, :], hit[:, :, :], rkw, ALU.mult))
                own_chain.link(dve.tensor_reduce(best[:, :, :], key[:, :, :], AX.X, ALU.max))
                own_chain.link(dve.tensor_tensor(hit[:, :, :], key[:, :, :], wide(best), ALU.is_equal))
                own_chain.link(dve.tensor_tensor(key[:, :, :], hit[:, :, :], wide(top), ALU.mult))
                if n == 0:
                    own_chain.link(dve.tensor_copy(gate[:, :, :], key[:, :, :]))
                    own_chain.link(dve.scalar_tensor_tensor(rest[:, :, :], hit[:, :, :], -2.0, rest[:, :, :], ALU.mult, ALU.add))
            own_chain.link(dve.tensor_tensor(gate[:, :, :], gate[:, :, :], key[:, :, :], ALU.add))
            own_chain.link(dve.tensor_tensor(tot[:, :, :], top1[:, :, :], top2[:, :, :], ALU.add))
            own_chain.link(dve.reciprocal(inv[:, :, :], tot[:, :, :]))
            own_chain.link(dve.tensor_tensor(gate[:, :, :], gate[:, :, :], wide(inv), ALU.mult))
            acc_chain = Chain(dve, chain_acc)
            for t in range(BLK):
                dve.wait_ge(mixed, t + 1)
                if t >= 4:
                    dve.wait_ge(slot_stored[t % 4], 16 * (t // 4))
                a = acc[:, t % 4, :]
                acc_chain.link(dve.tensor_copy(a, xt_ps[:, t % 2, 0:P]))
                for e in range(E):
                    ins = dve.scalar_tensor_tensor(a, ex_ps[:, t % 2, e * P:(e + 1) * P], gate[:, t, e:e + 1], a, ALU.mult, ALU.add)
                    if e < E - 1:
                        acc_chain.link(ins)
                ins.then_inc(accd, 1)
def block_layers(nc, a, out):
    def dram(name, *shape):
        return nc.dram_tensor(name, shape, F32, kind="Internal").ap()

    def act_map(name):
        return dram(name, P, TOK)

    with ExitStack() as sems:
        xn0, att = act_map("xn0"), act_map("att")
        group_norm(nc, sems, "gn0", a["x"], xn0, a["group_mean"], 1e-5)
        bias_attention(nc, sems, "l0", xn0, att, a["w_heads"], a["emb_h"], a["emb_w"], a["cells"], a["ident"], a["pick_quarters"])
        x1, xn1, x2 = act_map("x1"), act_map("xn1"), act_map("x2")
        group_norm(nc, sems, "gn1", a["x"], xn1, a["group_mean"], 1e-5, addend=att, x_sum=x1)
        gates, u_img = dram("gates", BATCH, INNER_TILES, P, L), dram("u_img", BATCH, INNER_TILES, P, L)
        delta = dram("delta", BATCH * INNER_TILES, CHUNKS, P, W)
        du = dram("du", BATCH * INNER_TILES, CHUNKS, DIRS, P, W)
        bc = dram("bc", BATCH, CHUNKS, 64, W)
        ys = dram("ys", BATCH * INNER_TILES * CHUNKS, DIRS, P, W)
        mamba_prepare(nc, sems, "m1", xn1, gates, u_img, delta.rearrange("g q p t -> g p q t"),
                      du.rearrange("g q d p t -> g p q d t"), bc.rearrange("b q p t -> b p q t"), a["w_in"], a["conv_w"],
                      a["conv_b"], a["w_x"], a["w_dt"], a["b_dt"], a["ident"])
        mamba_scan(nc, sems, "m2", delta, du, bc, ys, a["a_log"], a["pick_parts"], a["ident"])
        mamba_finish(nc, sems, "m3", x1, x2, ys, u_img, gates, a["d_param"], a["ln_w"], a["ln_b"], a["w_out"],
                     a["inner_mean"], 1e-5)
        xn2, x3, xn3 = act_map("xn2"), act_map("x3"), act_map("xn3")
        layer_norm(nc, sems, "ln2", x2, xn2, a["channel_mean"], a["ident"], 1e-5)
        full_attention(nc, sems, "l2", xn2, x2, x3, a["w_query"], a["w_key"], a["w_value"], a["ident"], a["first"])
        layer_norm(nc, sems, "ln3", x3, xn3, a["channel_mean"], a["ident"], 1e-5)
        y0, u_tok, x4, scales = act_map("y0"), act_map("u_tok"), act_map("x4"), dram("scales", P, 68)
        spectral_prepare(nc, sems, "s1", xn3, x3, y0, u_tok, scales, a["log_weights"], a["gumbel"], a["sigma"], a["m_u"],
                         a["ident"], a["exchange"], a["rank4"])
        spectral(nc, sems, "s2", u_tok, y0, x4, scales, a["phi"], a["m_phi"])
        xn4, x5, xn5 = act_map("xn4"), act_map("x5"), act_map("xn5")
        layer_norm(nc, sems, "ln4", x4, xn4, a["channel_mean"], a["ident"], 1e-5)
        linear_attention(nc, sems, "l3", xn4, x4, x5, a["wk_t"], a["wq_heads"], a["wv_t"], a["ident"])
        layer_norm(nc, sems, "ln5", x5, xn5, a["channel_mean"], a["ident"], 1e-5)
        experts(nc, sems, "moe", xn5, x5, out, a["router_w"], a["router_b"], a["expert_w"], a["expert_b"], a["ident"], a["rank8"])


def layout(i):
    import numpy as np

    i = {name: np.asarray(v) for name, v in i.items()}
    eye = np.eye(P, dtype=np.float32)
    side, e32, z32 = np.eye(SIDE, dtype=np.float32), np.eye(32, dtype=np.float32), np.zeros((32, 32), np.float32)

    def rows(v):
        return np.broadcast_to(v.reshape(1, -1), (P, v.size))

    def tiles(v):
        return v.reshape(INNER_TILES, P, -1).transpose(1, 0, 2)

    w = i["L0_conv_w_qkv"]
    heads = [np.concatenate([np.tile(w[:, h * 32:h * 32 + 32], (1, 4)), np.tile(w[:, P + h * 32:P + h * 32 + 32], (1, 4)),
                             w[:, 2 * P + h * 32:2 * P + h * 32 + 32]], 1) for h in range(4)]
    w_x, filters = i["L1_conv_w_xproj"], i["L2_ffn_phi"].T
    first = np.zeros((P, P), np.float32)
    first[0] = 1
    return {
        "x": i["x"].reshape(TOK, P).T,
        "group_mean": np.kron(np.eye(P // 4, dtype=np.float32), np.full((4, 4), 0.25, np.float32)),
        "channel_mean": np.full((P, P), 1 / P, np.float32),
        "inner_mean": np.full((P, P), 1 / (INNER_TILES * P), np.float32),
        "ident": eye, "exchange": eye[::-1], "first": first,
        "cells": np.concatenate([np.repeat(side, SIDE, 1), np.tile(side, (1, SIDE))], 0),
        "pick_quarters": np.tile(e32, (4, 1)),
        "pick_parts": np.concatenate([e32, e32], 0),
        "rank4": rows(np.arange(4, 0, -1).astype(np.float32)), "rank8": rows(np.arange(8, 0, -1).astype(np.float32)),
        "w_heads": np.concatenate(heads, 0), "emb_h": i["L0_conv_pos_emb_h"].T, "emb_w": i["L0_conv_pos_emb_w"].T,
        "w_in": i["L1_conv_w_in"], "conv_w": tiles(i["L1_conv_conv_w"].reshape(9, 2 * P).T), "conv_b": i["L1_conv_conv_b"].reshape(2, P).T,
        "w_x": tiles(np.concatenate([w_x[:, 8:40], w_x[:, 8:40], w_x[:, :8]], 1)), "w_dt": i["L1_conv_w_dt"],
        "b_dt": i["L1_conv_b_dt"].reshape(2, P).T, "a_log": tiles(i["L1_conv_A_log"]), "d_param": i["L1_conv_D_param"].reshape(2, P).T,
        "ln_w": i["L1_conv_ln_w"].reshape(2, P).T, "ln_b": i["L1_conv_ln_b"].reshape(2, P).T, "w_out": tiles(i["L1_conv_w_out"]),
        "w_query": i["L2_attn_w_query"], "w_key": i["L2_attn_w_key"], "w_value": i["L2_attn_w_value"],
        "log_weights": rows(i["L2_ffn_log_weights"]), "gumbel": rows(i["L2_ffn_gumbel"]), "sigma": rows(i["L2_ffn_sigma"]),
        "m_u": i["L2_ffn_M_u"].transpose(2, 0, 1, 3).reshape(P, 4, 3 * P),
        "phi": np.concatenate([np.zeros((16, 127), np.float32), filters[:, 0::2], np.zeros((16, 129), np.float32), filters[:, 1::2]], 1),
        "m_phi": np.stack([i["L2_ffn_M_phi_plus"], i["L2_ffn_M_phi_minus"]]).transpose(2, 3, 0, 1, 4).reshape(16 * P, 8 * P),
        "wk_t": i["L3_attn_Wk"].reshape(8 * 64, P).T, "wq_heads": i["L3_attn_Wq"].transpose(1, 0, 2), "wv_t": i["L3_attn_Wv"].reshape(8 * P, P).T,
        "router_w": i["L3_ffn_router_w"], "router_b": rows(i["L3_ffn_router_b"]),
        "expert_w": i["L3_ffn_expert_w"].transpose(1, 0, 2).reshape(P, 8 * P), "expert_b": i["L3_ffn_expert_b"].reshape(1, 8 * P),
    }


def kernel(**inputs):
    import numpy as _np
    import concourse.bacc as _bacc
    from concourse import mybir as _mybir
    from concourse.bass_utils import run_bass_kernel_spmd as _run

    nc = _bacc.Bacc("TRN2", target_bir_lowering=False, num_devices=1)
    arrays = {f"in_{name}": _np.ascontiguousarray(v) for name, v in layout(inputs).items()}
    args = {name[3:]: nc.dram_tensor(name, v.shape, _mybir.dt.from_np(v.dtype), kind="ExternalInput").ap() for name, v in arrays.items()}
    out = nc.dram_tensor("out", (TOK, P), _mybir.dt.float32, kind="ExternalOutput").ap()
    block_layers(nc, args, out)
    r = _run(nc, [arrays], core_ids=[0])
    return r.results[0]["out"].reshape(BATCH, SIDE, SIDE, P)
```
